# Optimizing a Trainium2 kernel written in Bass

```python
import numpy as np
import jax
import jax.numpy as jnp

def _softmax(x, axis=-1):
    return jax.nn.softmax(x, axis=axis)

def _gelu(x):
    return jax.nn.gelu(x, approximate=True)

def _silu(x):
    return jax.nn.silu(x)

def _sigmoid(x):
    return jax.nn.sigmoid(x)

def _layernorm(x, axis=-1, eps=1e-05):
    m = jnp.mean(x, axis=axis, keepdims=True)
    v = jnp.var(x, axis=axis, keepdims=True)
    return (x - m) / jnp.sqrt(v + eps)

def _scatter_add(tgt, idx, src, axis=0):
    return tgt.at[idx].add(src)

def _segment_sum(src, seg, n):
    return jax.ops.segment_sum(src, seg, n)
kernel_name = 'mk_decoder_preln_d1_seqx_r4_5b5f86'

def setup_inputs(seed: int=0):
    np.random.seed(seed)
    _w = jnp.asarray

    def _rec_inputs():
        import jax
        import jax.numpy as jnp
        _rk = jax.random.key(seed)
        x = -0.0003929 + 0.9999 * jax.random.normal(jax.random.fold_in(_rk, 1), (16, 256, 512), jnp.float32)
        _lenS = 256 - jax.random.randint(jax.random.fold_in(_rk, 7), (16,), 0, max(1, 256 // 4) + 1, jnp.int32)
        _lenS2 = 256 - jax.random.randint(jax.random.fold_in(_rk, 8), (16,), 0, max(1, 256 // 4) + 1, jnp.int32)
        _ctx_2048P = jax.random.normal(jax.random.fold_in(_rk, 11), (16, 16, 512), jnp.float32)
        _ctx_2048c = jax.random.dirichlet(jax.random.fold_in(_rk, 511), 0.3 * jnp.ones((16,), jnp.float32), (16, 256))
        _ctx_2048t = jnp.einsum('bsk,bkd->bsd', _ctx_2048c, _ctx_2048P)
        _ctx_2048t = _ctx_2048t * jax.lax.rsqrt(jnp.mean(jnp.square(_ctx_2048t)) + 1e-12) * 0.953939
        ctx_2048 = -1.39393e-06 + 0.999914 * (_ctx_2048t + 0.3 * jax.random.normal(jax.random.fold_in(_rk, 611), (16, 256, 512), jnp.float32))
        itok_BxS_0_1023 = jax.random.randint(jax.random.fold_in(_rk, 12), (16, 256), 0, 256, jnp.int32)
        return (x, ctx_2048, itok_BxS_0_1023)
    x, ctx_2048, itok_BxS_0_1023 = _rec_inputs()

    def _L0_attn_setup():
        import jax, jax.numpy as jnp
        import numpy as np
        import math
        B, T, C = (2, 512, 512)
        NH, L = (16, 128)
        key = jax.random.key(seed)
        ks = jax.random.split(key, 7)
        s = 0.02
        return {'x': jax.random.normal(ks[0], (B, T, C), dtype=jnp.float32), 'W_lat': jax.random.normal(ks[1], (C, L), dtype=jnp.float32) * s, 'b_lat': jnp.zeros((L,), dtype=jnp.float32), 'W_d': jax.random.normal(ks[2], (C, NH * L), dtype=jnp.float32) * s, 'b_d': jnp.zeros((NH * L,), dtype=jnp.float32), 'W_proj': jax.random.normal(ks[3], (NH * L, C), dtype=jnp.float32) * s, 'b_proj': jnp.zeros((C,), dtype=jnp.float32)}
    _L0_attn_all = _L0_attn_setup()
    _L0_attn_in = {k: v for k, v in _L0_attn_all.items() if k in ('W_lat', 'b_lat', 'W_d', 'b_d', 'W_proj', 'b_proj')}
    del _L0_attn_all

    def _L0_xattn_setup():
        import jax, jax.numpy as jnp
        import numpy as np
        B, Lq, Lk = (2, 1024, 256)
        Q_DIM, KV_DIM = (512, 512)
        H, HD = (16, 128)
        KVC, QC, R = (128, 192, 64)
        LOOKBACK = 8
        NEG = -1e+30

        def _rope(x, L):
            half = x.shape[-1] // 2
            inv_freq = 1.0 / 10000.0 ** (jnp.arange(half, dtype=jnp.float32) / half)
            ang = jnp.arange(L, dtype=jnp.float32)[:, None] * inv_freq
            cos, sin = (jnp.cos(ang), jnp.sin(ang))
            x1, x2 = (x[..., :half], x[..., half:])
            return jnp.concatenate([x1 * cos - x2 * sin, x1 * sin + x2 * cos], axis=-1)
        key = jax.random.key(seed)
        ks = jax.random.split(key, 11)

        def w(k, shape, fan_in):
            return jax.random.normal(k, shape, jnp.float32) / np.sqrt(fan_in).astype(np.float32)
        return {'q': jax.random.normal(ks[0], (B, Lq, Q_DIM), jnp.float32), 'kv': jax.random.normal(ks[1], (B, Lk, KV_DIM), jnp.float32), 'seg_id': jnp.sort(jax.random.randint(ks[2], (B, Lq), 0, Lk), axis=-1), 'W_kvc': w(ks[3], (KV_DIM, KVC), KV_DIM), 'W_dq': w(ks[4], (Q_DIM, QC), Q_DIM), 'W_uq': w(ks[5], (QC, H * HD), QC), 'W_qr': w(ks[6], (QC, H * R), QC), 'W_uk': w(ks[7], (KVC, H * HD), KVC), 'W_kr': w(ks[8], (KVC, R), KVC), 'W_uv': w(ks[9], (KVC, H * HD), KVC), 'W_o': w(ks[10], (H * HD, Q_DIM), H * HD)}
    _L0_xattn_all = _L0_xattn_setup()
    _L0_xattn_in = {k: v for k, v in _L0_xattn_all.items() if k in ('W_kvc', 'W_dq', 'W_uq', 'W_qr', 'W_uk', 'W_kr', 'W_uv', 'W_o')}
    del _L0_xattn_all

    def _L0_ffn_setup():
        import jax, jax.numpy as jnp
        import numpy as np
        TOP_K = 2
        CAPACITY_FACTOR = 1.0

        def _ffn(x, w1, w2):
            h = x @ w1
            x1, x2 = jnp.split(h, 2, axis=-1)
            return x1 * jax.nn.silu(x2) @ w2
        key = jax.random.key(seed)
        ks = jax.random.split(key, 6)
        B, S, D, F, E_r, E_s = (4, 512, 512, 256, 7, 1)
        sc_in = 1.0 / np.sqrt(D)
        sc_mid = 1.0 / np.sqrt(F)
        return {'x': jax.random.normal(ks[0], (B, S, D), dtype=jnp.float32), 'gate_w': jax.random.normal(ks[1], (D, E_r), dtype=jnp.float32) * sc_in, 'expert_bias': jnp.zeros((E_r,), dtype=jnp.float32), 'shared_w1': jax.random.normal(ks[2], (E_s, D, 2 * F), dtype=jnp.float32) * sc_in, 'shared_w2': jax.random.normal(ks[3], (E_s, F, D), dtype=jnp.float32) * sc_mid, 'routed_w1': jax.random.normal(ks[4], (E_r, D, 2 * F), dtype=jnp.float32) * sc_in, 'routed_w2': jax.random.normal(ks[5], (E_r, F, D), dtype=jnp.float32) * sc_mid}
    _L0_ffn_all = _L0_ffn_setup()
    _L0_ffn_in = {k: v for k, v in _L0_ffn_all.items() if k in ('gate_w', 'expert_bias', 'shared_w1', 'shared_w2', 'routed_w1', 'routed_w2')}
    del _L0_ffn_all
    return {'x': x, 'ctx_2048': ctx_2048, 'itok_BxS_0_1023': itok_BxS_0_1023, 'L0_attn_W_lat': _L0_attn_in['W_lat'], 'L0_attn_b_lat': _L0_attn_in['b_lat'], 'L0_attn_W_d': _L0_attn_in['W_d'], 'L0_attn_b_d': _L0_attn_in['b_d'], 'L0_attn_W_proj': _L0_attn_in['W_proj'], 'L0_attn_b_proj': _L0_attn_in['b_proj'], 'L0_xattn_W_kvc': _L0_xattn_in['W_kvc'], 'L0_xattn_W_dq': _L0_xattn_in['W_dq'], 'L0_xattn_W_uq': _L0_xattn_in['W_uq'], 'L0_xattn_W_qr': _L0_xattn_in['W_qr'], 'L0_xattn_W_uk': _L0_xattn_in['W_uk'], 'L0_xattn_W_kr': _L0_xattn_in['W_kr'], 'L0_xattn_W_uv': _L0_xattn_in['W_uv'], 'L0_xattn_W_o': _L0_xattn_in['W_o'], 'L0_ffn_gate_w': _L0_ffn_in['gate_w'], 'L0_ffn_expert_bias': _L0_ffn_in['expert_bias'], 'L0_ffn_shared_w1': _L0_ffn_in['shared_w1'], 'L0_ffn_shared_w2': _L0_ffn_in['shared_w2'], 'L0_ffn_routed_w1': _L0_ffn_in['routed_w1'], 'L0_ffn_routed_w2': _L0_ffn_in['routed_w2']}

def reference(x, ctx_2048, itok_BxS_0_1023, L0_attn_W_lat, L0_attn_b_lat, L0_attn_W_d, L0_attn_b_d, L0_attn_W_proj, L0_attn_b_proj, L0_xattn_W_kvc, L0_xattn_W_dq, L0_xattn_W_uq, L0_xattn_W_qr, L0_xattn_W_uk, L0_xattn_W_kr, L0_xattn_W_uv, L0_xattn_W_o, L0_ffn_gate_w, L0_ffn_expert_bias, L0_ffn_shared_w1, L0_ffn_shared_w2, L0_ffn_routed_w1, L0_ffn_routed_w2):
    import jax
    import jax.numpy as jnp

    def _L0_attn_ref(x, W_lat, b_lat, W_d, b_d, W_proj, b_proj):
        import jax, jax.numpy as jnp
        import numpy as np
        import math
        B, T, C = (2, 512, 512)
        NH, L = (16, 128)
        Bx, Tx, Cx = x.shape
        k = x @ W_lat + b_lat
        q = (x @ W_d + b_d).reshape(Bx, Tx, NH, L)
        q = jnp.transpose(q, (0, 2, 1, 3))
        scale = 1.0 / math.sqrt(L)
        att = jnp.einsum('bhtl,bsl->bhts', q, k) * scale
        causal = jnp.tril(jnp.ones((Tx, Tx), dtype=bool))
        att = jnp.where(causal[None, None], att, -jnp.inf)
        att = jax.nn.softmax(att, axis=-1)
        y = jnp.einsum('bhts,bsl->bhtl', att, k)
        y = jnp.transpose(y, (0, 2, 1, 3)).reshape(Bx, Tx, NH * L)
        return y @ W_proj + b_proj

    def _L0_xattn_ref(q, kv, seg_id, W_kvc, W_dq, W_uq, W_qr, W_uk, W_kr, W_uv, W_o):
        import jax, jax.numpy as jnp
        import numpy as np
        B, Lq, Lk = (2, 1024, 256)
        Q_DIM, KV_DIM = (512, 512)
        H, HD = (16, 128)
        KVC, QC, R = (128, 192, 64)
        LOOKBACK = 8
        NEG = -1e+30

        def _rope(x, L):
            half = x.shape[-1] // 2
            inv_freq = 1.0 / 10000.0 ** (jnp.arange(half, dtype=jnp.float32) / half)
            ang = jnp.arange(L, dtype=jnp.float32)[:, None] * inv_freq
            cos, sin = (jnp.cos(ang), jnp.sin(ang))
            x1, x2 = (x[..., :half], x[..., half:])
            return jnp.concatenate([x1 * cos - x2 * sin, x1 * sin + x2 * cos], axis=-1)
        b, lq, _ = q.shape
        lk = kv.shape[1]
        kv_c = kv @ W_kvc
        q_c = q @ W_dq
        q_nope = (q_c @ W_uq).reshape(b, lq, H, HD).transpose(0, 2, 1, 3)
        q_rope = (q_c @ W_qr).reshape(b, lq, H, R).transpose(0, 2, 1, 3)
        k_nope = (kv_c @ W_uk).reshape(b, lk, H, HD)
        v = (kv_c @ W_uv).reshape(b, lk, H, HD)
        k_rope = kv_c @ W_kr
        q_rope = _rope(q_rope, lq)
        k_rope = _rope(k_rope, lk)
        scale = 1.0 / np.sqrt(HD + R).astype(np.float32)
        scores = (jnp.einsum('bhqd,bkhd->bhqk', q_nope, k_nope) + jnp.einsum('bhqr,bkr->bhqk', q_rope, k_rope)) * scale
        k_ids = jnp.arange(lk)[None, None, :]
        qs = seg_id[:, :, None]
        good = (k_ids <= qs) & (k_ids >= qs - LOOKBACK)
        scores = jnp.where(good[:, None, :, :], scores, NEG)
        attn = jax.nn.softmax(scores, axis=-1)
        out = jnp.einsum('bhqk,bkhd->bqhd', attn, v).reshape(b, lq, H * HD)
        return out @ W_o

    def _L0_ffn_ref(x, gate_w, expert_bias, shared_w1, shared_w2, routed_w1, routed_w2):
        import jax, jax.numpy as jnp
        import numpy as np
        TOP_K = 2
        CAPACITY_FACTOR = 1.0

        def _ffn(x, w1, w2):
            h = x @ w1
            x1, x2 = jnp.split(h, 2, axis=-1)
            return x1 * jax.nn.silu(x2) @ w2
        B, S, D = x.shape
        E_r = gate_w.shape[1]
        T = B * S
        capacity = max(1, int(CAPACITY_FACTOR * T / E_r))
        flat_x = x.reshape(T, D)
        shared_sum = jax.vmap(_ffn, in_axes=(None, 0, 0))(flat_x, shared_w1, shared_w2).sum(0)
        gate_logits = flat_x @ gate_w + expert_bias
        aff = jax.nn.sigmoid(gate_logits)
        _, topk_idx = jax.lax.top_k(aff, TOP_K)
        mask = (topk_idx[:, :, None] == jnp.arange(E_r)[None, None, :]).any(axis=1)
        score = jnp.where(mask, aff, -1.0).T
        _, sel_idx = jax.lax.top_k(score, capacity)
        kept = jnp.take_along_axis(mask.T, sel_idx, axis=1)
        w = jnp.where(kept, jnp.take_along_axis(aff.T, sel_idx, axis=1), 0.0)
        inp = flat_x[sel_idx]
        out = jax.vmap(_ffn)(inp, routed_w1, routed_w2)
        routed_sum = jnp.zeros_like(flat_x).at[sel_idx].add(out * w[:, :, None])
        return (shared_sum + routed_sum).reshape(B, S, D)
    x = x + _L0_attn_ref(_layernorm(x, axis=-1), L0_attn_W_lat, L0_attn_b_lat, L0_attn_W_d, L0_attn_b_d, L0_attn_W_proj, L0_attn_b_proj)
    x = x + _L0_xattn_ref(_layernorm(x, axis=-1), ctx_2048, itok_BxS_0_1023, L0_xattn_W_kvc, L0_xattn_W_dq, L0_xattn_W_uq, L0_xattn_W_qr, L0_xattn_W_uk, L0_xattn_W_kr, L0_xattn_W_uv, L0_xattn_W_o)
    x = x + _L0_ffn_ref(_layernorm(x, axis=-1), L0_ffn_gate_w, L0_ffn_expert_bias, L0_ffn_shared_w1, L0_ffn_shared_w2, L0_ffn_routed_w1, L0_ffn_routed_w2)
    return x

_drawn_inputs = setup_inputs


def setup_inputs(seed=0):
    import zlib

    import numpy as np

    out = dict(_drawn_inputs(seed))
    spreads = {'L0_attn_b_lat': (0.0, 0.1),
     'L0_attn_b_d': (0.0, 0.383),
     'L0_attn_b_proj': (0.0, 0.1),
     'L0_ffn_expert_bias': (0.0, 0.1)}
    factors = {}
    for name, (base, spread) in spreads.items():
        noise = np.random.default_rng([zlib.crc32(name.encode()), seed]).standard_normal(out[name].shape)
        drawn = base * np.exp(spread * noise) if base else spread * noise
        out[name] = jnp.asarray(drawn.astype(out[name].dtype))
    for name, factor in factors.items():
        out[name] = (out[name] * factor).astype(out[name].dtype)
    return out
```

```python
import math
from contextlib import ExitStack

import concourse.bass as bass
from concourse import mybir

F32 = mybir.dt.float32
F32R = mybir.dt.float32r
BF16 = mybir.dt.bfloat16
I32 = mybir.dt.int32
U32 = mybir.dt.uint32
ALU = mybir.AluOpType
ACT = mybir.ActivationFunctionType
AX = mybir.AxisListType

P = 128
B, S, D = 16, 256, 512
H = 16
L = 128
ST = S // P
DC = D // P
QC, QCC = 192, 2
R = 64
EPS = 1e-5
MASKED = -float(2 ** 100)
LOOKBACK = 8
NT = B * ST
E, EP = 7, 8
F = 256
FC = F // P
TOP_K = 2
CAP = B * S // E
CT = -(-CAP // P)
SLOTS = CT * P
ROWS = E * SLOTS
LN_LINKS = 14
SEED = 2


class Values:

    def __init__(self, eng, i=None):
        self.eng, self.i, self.known = eng, i, {}

    def __call__(self, per, k):
        if self.i is None or per == 0:
            return k
        if (per, k) not in self.known:
            self.known[per, k] = self.eng.snap(self.i * per + k)
        return self.known[per, k]


class Unit:

    def __init__(self, values):
        self.values = values

    def done(self, h):
        return self.values(H, h + 1 + SEED)


class Batch:

    def __init__(self, values, shift):
        self.values, self.shift = values, shift

    def done(self, per=1, k=0):
        return self.values(per, per * self.shift + k)


def clear(nc, sems):
    for s in sems:
        nc.gpsimd.sem_clear(s)
    nc.all_engine_barrier()


def hold(eng, sem, value, step):
    eng.wait_ge(sem, value)
    eng.sem_inc(step, 1)


def product(pe, out, lhs, rhs, first, last):
    pe.matmul(out, lhs[0], rhs[0], start=first, stop=False)
    pe.matmul(out, lhs[0], rhs[1], start=False, stop=False)
    return pe.matmul(out, lhs[1], rhs[0], start=False, stop=last)


def layer_norm(v, xt, stats, small, chain, at, step, out=None):
    k = [0]

    def link(ins):
        k[0] += 1
        ins.then_inc(chain, 1)
        v.wait_ge(chain, at(k[0]))

    for t in range(ST):
        last = v.bn_stats(stats[:, t, 0:6], xt[:, t, :])
    last.then_inc(chain, 1)
    k[0] += 1
    hold(v, chain, at(1), step)
    for t in range(ST):
        last = v.bn_aggr(stats[:, t, 6:8], stats[:, t, 0:6])
    link(last)
    ve, half, y, w = small[:, 0, :], small[:, 1, :], small[:, 2, :], small[:, 3, :]
    link(v.tensor_scalar(ve, stats[:, :, 7], EPS, None, ALU.add))
    v.tensor_scalar(half, ve, -0.5, None, ALU.mult)
    link(v.tensor_scalar(y.bitcast(I32), ve.bitcast(I32), 1, None, ALU.logical_shift_right))
    link(v.tensor_scalar(y.bitcast(I32), y.bitcast(I32), -1.0, float(0x5F3759DF), ALU.mult, ALU.add))
    for _ in range(3):
        link(v.tensor_tensor(w, y, half, ALU.mult))
        link(v.tensor_tensor(w, w, y, ALU.mult))
        if _ < 2:
            link(v.scalar_tensor_tensor(y, w, 1.5, y, ALU.add, ALU.mult))
    link(v.scalar_tensor_tensor(y, w, 1.5, y, ALU.add, ALU.mult))
    assert k[0] == LN_LINKS
    for t in range(ST):
        last = v.tensor_scalar((xt if out is None else out)[:, t, :], xt[:, t, :], stats[:, t, 6:7], y[:, t:t + 1], ALU.subtract, ALU.mult)
    return last


def self_attention(nc, x, w_lat, b_lat, w_d, b_d, w_proj, b_proj, causal, ident_in, x1):
    scale = 1.0 / math.sqrt(L)
    PK = 3 * P
    with ExitStack() as ctx:
        sems = []

        def sb(name, shape, dt=F32):
            return ctx.enter_context(nc.sbuf_tensor("a_" + name, shape, dt))

        def pb(name, shape):
            return ctx.enter_context(nc.psum_tensor("a_" + name, shape, F32))

        def sem(name):
            sems.append(ctx.enter_context(nc.semaphore("a_" + name)))
            return sems[-1]

        def parts(name, shape):
            return sb(name + "_hi", shape, F32R), sb(name + "_lo", shape, F32R)

        wd = parts("wd", [P, DC, H * L])
        wp = parts("wp", [P, H, D])
        wl = parts("wl", [P, DC, L])
        raw = [sb(f"raw{n}", [P, 2048]) for n in range(2)]
        raw_l = raw[0][:, 0:DC * L].rearrange("p (c n) -> p c n", c=DC)
        bd = sb("bd", [P, H])
        bl = sb("bl", [P, 1])
        bp = sb("bp", [P, D])
        mask = sb("mask", [P, PK])
        ident = sb("ident", [P, P])
        xin = sb("xin", [P, ST, D])
        stats = sb("stats", [P, ST, 8])
        small = sb("small", [P, 4, ST])
        xt = parts("xt", [P, DC, S])
        kt = parts("kt", [P, S])
        kn = parts("kn", [P, ST, L])
        q = [parts(f"q{n}", [P, S]) for n in range(2)]
        pr = [sb(f"pr{n}", [P, PK]) for n in range(2)]
        top = [sb(f"top{n}", [P, ST]) for n in range(2)]
        rsum = [sb(f"rsum{n}", [P, ST]) for n in range(2)]
        rinv = [sb(f"rinv{n}", [P, ST]) for n in range(2)]
        pt = parts("pt", [P, PK])
        y = parts("y", [P, S])
        res = sb("res", [P, ST, D])

        q_ps, s_ps, t_ps, y_ps = (pb(n, [P, 512]) for n in ("q_ps", "s_ps", "t_ps", "y_ps"))
        o_ps = [pb(f"o_ps{n}", [P, D]) for n in range(ST)]
        x_ps = [pb(f"x_ps{n}", [P, 512]) for n in range(2)]

        raw_in = [sem(f"raw_in{n}") for n in range(2)]
        raw_split, w_hi = sem("raw_split"), sem("w_hi")
        const_in = sem("const_in")
        x_in, res_in, stored = sem("x_in"), sem("res_in"), sem("stored")
        ln_chain, xn_ready = sem("ln_chain"), sem("xn_ready")
        xt_mm, xt_hi, xt_lo = sem("xt_mm"), sem("xt_hi"), sem("xt_lo")
        k_mm, k_hi, k_lo = sem("k_mm"), sem("k_hi"), sem("k_lo")
        kn_mm, kn_ready = sem("kn_mm"), sem("kn_ready")
        res_biased, out_ready = sem("res_biased"), sem("out_ready")
        sp_step, v_step, g_step = sem("sp_step"), sem("v_step"), sem("g_step")
        q_mm, q_hi, q_lo = sem("q_mm"), sem("q_hi"), sem("q_lo")
        s_mm, s_masked, p_exp, p_inv, p_norm = sem("s_mm"), sem("s_masked"), sem("p_exp"), sem("p_inv"), sem("p_norm")
        t_mm, pt_hi, pt_lo = sem("t_mm"), sem("pt_hi"), sem("pt_lo")
        y_mm, y_hi, y_lo, o_mm = sem("y_mm"), sem("y_hi"), sem("y_lo"), sem("o_mm")

        def piece(src, dst, width):
            return src, dst[0], dst[1], width

        pieces = [piece(w_lat.rearrange("(c p) n -> p c n", p=P),
                        [w[:, :, :].rearrange("p c n -> p (c n)") for w in wl], DC * L)]
        for c in range(DC):
            pieces.append(piece(w_d[c * P:(c + 1) * P, :], [w[:, c, :] for w in wd], H * L))
        for g in range(0, H, 4):
            pieces.append(piece(w_proj[g * P:(g + 4) * P, :].rearrange("(h p) n -> p h n", p=P),
                                [w[:, g:g + 4, :].rearrange("p h n -> p (h n)") for w in wp], 4 * D))

        ctx.callback(clear, nc, sems)
        block = ctx.enter_context(nc.Block())

        @block.sync
        def _(sp):
            sp.dma_start(xin[:], x[0].rearrange("(t p) c -> p t c", p=P)).then_inc(x_in, 16)
            sp.dma_start(ident[:], ident_in).then_inc(const_in, 16)
            sp.dma_start(mask[:], causal).then_inc(const_in, 16)
            sp.dma_start(bd[:], b_d).then_inc(const_in, 16)
            sp.dma_start(bl[:], b_lat.rearrange("(p o) -> p o", o=1)).then_inc(const_in, 16)
            sp.dma_start(bp[:], b_proj.rearrange("(o n) -> o n", o=1).to_broadcast([P, D])).then_inc(const_in, 16)
            for n, (src, _, _, width) in enumerate(pieces):
                if n >= 2:
                    sp.wait_ge(raw_split, n - 1)
                dst = raw[n % 2][:, 0:width]
                if n == 0:
                    dst = raw_l
                elif n > DC:
                    dst = dst.rearrange("p (h n) -> p h n", n=D)
                sp.dma_start(dst, src).then_inc(raw_in[n % 2], 16)
            with sp.Fori(0, B) as i:
                val = Values(sp, i)
                now = Batch(val, 0)
                nxt = sp.snap((i + 1) % B)
                xt_read, out_done, out_stored = now.done(1, 1), now.done(1, 1 + SEED), now.done(16, 16)
                hold(sp, xt_mm, xt_read, sp_step)
                sp.dma_start(xin[:], x[bass.ds(nxt, 1)].rearrange("o (t p) c -> p (o t) c", p=P)).then_inc(x_in, 16)
                sp.dma_start(res[:], x[bass.ds(i, 1)].rearrange("o (t p) c -> p (o t) c", p=P)).then_inc(res_in, 16)
                hold(sp, out_ready, out_done, sp_step)
                sp.dma_start(x1[bass.ds(i, 1)].rearrange("o (t p) c -> p (o t) c", p=P), res[:]).then_inc(stored, 16)
                hold(sp, stored, out_stored, sp_step)

        @block.scalar
        def _(act):
            for n, (_, hi, _, width) in enumerate(pieces):
                act.wait_ge(raw_in[n % 2], 16 * (n // 2 + 1))
                act.activation(hi, raw[n % 2][:, 0:width], ACT.Copy).then_inc(w_hi, 1)
            act.wait_ge(const_in, 80)
            for s in (q_hi, p_exp, pt_hi, y_hi):
                act.sem_inc(s, SEED)

            def keys(batch):
                for n in range(2):
                    act.wait_ge(xt_mm, batch.done(1, 1))
                    act.activation(xt[0][:, 2 * n:2 * n + 2, :].rearrange("p c t -> p (c t)"), x_ps[n][:],
                                   ACT.Copy).then_inc(xt_hi, 1)

            def latent(batch):
                act.wait_ge(k_mm, batch.done(1, 1))
                act.activation(kt[0][:], q_ps[:, 0:S], ACT.Identity, bias=bl[:]).then_inc(k_hi, 1)

            def latent_rows(batch):
                act.wait_ge(kn_mm, batch.done(1, 1))
                for n in range(2):
                    last = act.activation(kn[n][:].rearrange("p t l -> p (t l)"), x_ps[0][:, n * S:(n + 1) * S], ACT.Copy)
                last.then_inc(kn_ready, 1)

            def query(unit, h, head):
                act.wait_ge(q_mm, unit.done(h))
                act.activation(q[h % 2][0][:], q_ps[:, 0:S], ACT.Identity, bias=bd[:, head:head + 1]).then_inc(q_hi, 1)

            def exps(unit, h):
                act.wait_ge(s_masked, unit.done(h))
                n = h % 2
                act.activation(pr[n][:, 0:P], pr[n][:, 0:P], ACT.Exp, bias=top[n][:, 0:1], scale=-1.0,
                               accum_out=rsum[n][:, 0:1])
                act.activation(pr[n][:, P:PK], pr[n][:, P:PK], ACT.Exp, bias=top[n][:, 1:2], scale=-1.0,
                               accum_out=rsum[n][:, 1:2]).then_inc(p_exp, 1)

            def probs_t(unit, h):
                act.wait_ge(t_mm, unit.done(h))
                act.activation(pt[0][:], t_ps[:, 0:PK], ACT.Copy).then_inc(pt_hi, 1)

            def mixed(unit, h):
                act.wait_ge(y_mm, unit.done(h))
                act.activation(y[0][:], y_ps[:, 0:S], ACT.Copy).then_inc(y_hi, 1)

            first, unit = Batch(Values(act), 0), Unit(Values(act))
            keys(first)
            latent(first)
            query(unit, 0, 0)
            query(unit, 1, 1)
            exps(unit, 0)
            latent_rows(first)
            with act.Fori(0, B) as i:
                val = Values(act, i)
                unit, nxt = Unit(val), Batch(val, 1)
                for h in range(H):
                    if h + 2 < H:
                        query(unit, h + 2, h + 2)
                    if h == H - 2:
                        keys(nxt)
                    probs_t(unit, h)
                    if h + 1 < H:
                        exps(unit, h + 1)
                        mixed(unit, h)
                    if h == H - 2:
                        latent(nxt)
                query(unit, H, 0)
                mixed(unit, H - 1)
                query(unit, H + 1, 1)
                exps(unit, H)
                latent_rows(nxt)

        @block.vector
        def _(v):
            for n, (_, hi, lo, width) in enumerate(pieces):
                v.wait_ge(w_hi, n + 1)
                v.tensor_tensor(lo, raw[n % 2][:, 0:width], hi.bitcast(F32), ALU.subtract).then_inc(raw_split, 1)
            v.wait_ge(const_in, 80)
            for s in (q_lo, s_masked, p_inv, pt_lo, y_lo, out_ready, ln_chain):
                v.sem_inc(s, SEED)

            def norm(batch):
                v.wait_ge(x_in, batch.done(16, 16))
                layer_norm(v, xin, stats, small, ln_chain,
                           lambda k: batch.done(LN_LINKS, k + SEED), v_step).then_inc(xn_ready, 1)

            def keys(batch):
                for n in range(2):
                    v.wait_ge(xt_hi, batch.done(2, n + 1))
                    half = slice(2 * n, 2 * n + 2)
                    v.tensor_tensor(xt[1][:, half, :].rearrange("p c t -> p (c t)"), x_ps[n][:],
                                    xt[0][:, half, :].rearrange("p c t -> p (c t)").bitcast(F32),
                                    ALU.subtract).then_inc(xt_lo, 1)

            def latent(batch):
                v.wait_ge(k_hi, batch.done(1, 1))
                v.scalar_tensor_tensor(kt[1][:], q_ps[:, 0:S], bl[:], kt[0][:].bitcast(F32), ALU.add,
                                       ALU.subtract).then_inc(k_lo, 1)

            def query(unit, h, head):
                v.wait_ge(q_hi, unit.done(h))
                v.scalar_tensor_tensor(q[h % 2][1][:], q_ps[:, 0:S], bd[:, head:head + 1],
                                       q[h % 2][0][:].bitcast(F32), ALU.add, ALU.subtract).then_inc(q_lo, 1)

            def masked(unit, h):
                n = h % 2
                hold(v, s_mm, unit.done(h), v_step)
                v.tensor_tensor_reduce(out=pr[n][:, 0:P], in0=s_ps[:, 0:P], in1=mask[:, 0:P], scale=-scale, scalar=3e38,
                                       op0=ALU.add, op1=ALU.min, accum_out=top[n][:, 0:1])
                v.tensor_tensor_reduce(out=pr[n][:, P:PK], in0=s_ps[:, P:PK], in1=mask[:, P:PK], scale=-scale,
                                       scalar=3e38, op0=ALU.add, op1=ALU.min,
                                       accum_out=top[n][:, 1:2]).then_inc(s_masked, 1)

            def inverse(unit, h):
                v.wait_ge(p_exp, unit.done(h))
                v.reciprocal(rinv[h % 2][:], rsum[h % 2][:]).then_inc(p_inv, 1)

            def probs_t(unit, h):
                v.wait_ge(pt_hi, unit.done(h))
                v.tensor_tensor(pt[1][:], t_ps[:, 0:PK], pt[0][:].bitcast(F32), ALU.subtract).then_inc(pt_lo, 1)

            def mixed(unit, h):
                v.wait_ge(y_hi, unit.done(h))
                v.tensor_tensor(y[1][:], y_ps[:, 0:S], y[0][:].bitcast(F32), ALU.subtract).then_inc(y_lo, 1)

            first, unit = Batch(Values(v), 0), Unit(Values(v))
            norm(first)
            keys(first)
            latent(first)
            query(unit, 0, 0)
            query(unit, 1, 1)
            masked(unit, 0)
            inverse(unit, 0)
            with v.Fori(0, B) as i:
                val = Values(v, i)
                unit, now, nxt = Unit(val), Batch(val, 0), Batch(val, 1)
                for h in range(H):
                    if h + 2 < H:
                        query(unit, h + 2, h + 2)
                    if h + 1 < H:
                        masked(unit, h + 1)
                    if h == H // 2:
                        norm(nxt)
                    if h == H - 2:
                        keys(nxt)
                    probs_t(unit, h)
                    if h + 1 < H:
                        inverse(unit, h + 1)
                        mixed(unit, h)
                    if h == H - 2:
                        latent(nxt)
                query(unit, H, 0)
                mixed(unit, H - 1)
                query(unit, H + 1, 1)
                masked(unit, H)
                inverse(unit, H)
                v.wait_ge(res_biased, now.done(1, 1))
                v.wait_ge(o_mm, unit.done(H - 1))
                for t in range(ST):
                    last = v.tensor_tensor(res[:, t, :], o_ps[t][:], res[:, t, :], ALU.add)
                last.then_inc(out_ready, 1)

        @block.gpsimd
        def _(g):
            g.wait_ge(const_in, 80)
            g.sem_inc(p_norm, SEED)

            def normalize(unit, h):
                n = h % 2
                hold(g, p_inv, unit.done(h), g_step)
                g.tensor_scalar(pr[n][:, 0:P], pr[n][:, 0:P], rinv[n][:, 0:1], None, ALU.mult)
                g.tensor_scalar(pr[n][:, P:PK], pr[n][:, P:PK], rinv[n][:, 1:2], None, ALU.mult).then_inc(p_norm, 1)

            normalize(Unit(Values(g)), 0)
            with g.Fori(0, B) as i:
                val = Values(g, i)
                unit, now = Unit(val), Batch(val, 0)
                for h in range(H):
                    if h == 2:
                        g.wait_ge(res_in, now.done(16, 16))
                        for t in range(ST):
                            last = g.tensor_tensor(res[:, t, :], res[:, t, :], bp[:], ALU.add)
                        last.then_inc(res_biased, 1)
                    normalize(unit, h + 1)

        @block.tensor
        def _(pe):
            pe.wait_ge(raw_split, len(pieces))
            pe.wait_ge(const_in, 80)
            for s in (q_mm, s_mm, t_mm, y_mm, o_mm):
                pe.sem_inc(s, SEED)

            def transposed_norm(batch):
                pe.wait_ge(xn_ready, batch.done(1, 1))
                for c in range(DC):
                    for t in range(ST):
                        at = (c % 2) * S + t * P
                        last = pe.transpose(x_ps[c // 2][:, at:at + P], xin[:, t, c * P:(c + 1) * P], ident[:])
                last.then_inc(xt_mm, 1)

            def latent(batch, unit, h):
                pe.wait_ge(xt_lo, batch.done(2, 2))
                pe.wait_ge(q_lo, unit.done(h - 1))
                for c in range(DC):
                    last = product(pe, q_ps[:, 0:S], [w[:, c, :] for w in wl], [w[:, c, :] for w in xt],
                                   c == 0, c == DC - 1)
                last.then_inc(k_mm, 1)

            def latent_rows(batch):
                for n in range(2):
                    for t in range(ST):
                        at = n * S + t * P
                        last = pe.transpose(x_ps[0][:, at:at + P], kt[n][:, t * P:(t + 1) * P].bitcast(F32), ident[:])
                last.then_inc(kn_mm, 1)

            def query(unit, h, head):
                pe.wait_ge(q_lo, unit.done(h - 1))
                for c in range(DC):
                    last = product(pe, q_ps[:, 0:S], [w[:, c, head * L:(head + 1) * L] for w in wd],
                                   [w[:, c, :] for w in xt], c == 0, c == DC - 1)
                last.then_inc(q_mm, 1)

            def scores(unit, h):
                n = h % 2
                pe.wait_ge(s_masked, unit.done(h - 1))
                pe.wait_ge(q_lo, unit.done(h))
                product(pe, s_ps[:, 0:P], [w[:, 0:P] for w in q[n]], [w[:, 0:P] for w in kt], True, True)
                product(pe, s_ps[:, P:PK], [w[:, P:S] for w in q[n]], [w[:, :] for w in kt], True,
                        True).then_inc(s_mm, 1)

            def probs_t(unit, h):
                n = h % 2
                pe.wait_ge(pt_lo, unit.done(h - 1))
                pe.wait_ge(p_norm, unit.done(h))
                for c in range(3):
                    last = pe.transpose(t_ps[:, c * P:(c + 1) * P], pr[n][:, c * P:(c + 1) * P], ident[:])
                last.then_inc(t_mm, 1)

            def mixed(unit, h):
                pe.wait_ge(y_lo, unit.done(h - 1))
                pe.wait_ge(pt_lo, unit.done(h))
                product(pe, y_ps[:, 0:S], [w[:, 0, :] for w in kn], [w[:, 0:S] for w in pt], True, False)
                product(pe, y_ps[:, P:S], [w[:, 1, :] for w in kn], [w[:, S:PK] for w in pt], False,
                        True).then_inc(y_mm, 1)

            def projected(unit, h):
                pe.wait_ge(y_lo, unit.done(h))
                for t in range(ST):
                    last = product(pe, o_ps[t][:], [w[:, t * P:(t + 1) * P] for w in y], [w[:, h, :] for w in wp],
                                   h == 0, h == H - 1)
                last.then_inc(o_mm, 1)

            first, unit = Batch(Values(pe), 0), Unit(Values(pe))
            transposed_norm(first)
            latent(first, unit, 0)
            pe.wait_ge(k_lo, 1)
            query(unit, 0, 0)
            query(unit, 1, 1)
            scores(unit, 0)
            latent_rows(first)
            with pe.Fori(0, B) as i:
                val = Values(pe, i)
                unit, now, nxt = Unit(val), Batch(val, 0), Batch(val, 1)
                for h in range(H):
                    if h + 2 < H:
                        query(unit, h + 2, h + 2)
                    if h + 1 < H:
                        scores(unit, h + 1)
                    if h == H - 2:
                        transposed_norm(nxt)
                    probs_t(unit, h)
                    if h == 1:
                        pe.wait_ge(out_ready, now.done(1, SEED))
                    if h >= 1:
                        projected(unit, h - 1)
                    if h == 0:
                        pe.wait_ge(kn_ready, now.done(1, 1))
                    if h + 1 < H:
                        mixed(unit, h)
                    if h == H - 2:
                        latent(nxt, unit, H)
                pe.wait_ge(k_lo, nxt.done(1, 1))
                query(unit, H, 0)
                mixed(unit, H - 1)
                query(unit, H + 1, 1)
                scores(unit, H)
                projected(unit, H - 1)
                latent_rows(nxt)


def cross_attention(nc, x1, ctx_t, seg_cols, w_kvc, w_dq, uq_t, w_qr, uk_t, kr_uv, uv_t, w_o, trig, rot_cs, key_ids,
                    ident_in, x2):
    scale = 1.0 / math.sqrt(L + R)
    with ExitStack() as outer:
        def osb(name, shape, dt=F32):
            return outer.enter_context(nc.sbuf_tensor("b_" + name, shape, dt))

        def oparts(name, shape):
            return osb(name + "_hi", shape, F32R), osb(name + "_lo", shape, F32R)

        wa = oparts("wa", [P, QCC, H * L])
        wr = oparts("wr", [P, QCC, H * 2 * R])
        wvo = oparts("wvo", [P, H, D])
        wdq = oparts("wdq", [P, DC, QCC * P])
        wkv = oparts("wkv", [P, DC, L])
        wkr = oparts("wkr", [P, 2, 2 * R])

        with ExitStack() as ctx:
            sems = []

            def sb(name, shape, dt=F32):
                return ctx.enter_context(nc.sbuf_tensor("bw_" + name, shape, dt))

            def sem(name):
                sems.append(ctx.enter_context(nc.semaphore("bw_" + name)))
                return sems[-1]

            r_uq, r_uk, r_uv = sb("uq", [P, H, QC]), sb("uk", [P, H, L]), sb("uv", [P, H, L])
            r_o = [sb(f"o{n}", [P, 4, D]) for n in range(2)]
            r_dq, r_kv, r_kr = sb("dq", [P, DC, QC]), sb("kv", [P, DC, L]), sb("kr", [P, 2, 2 * R])
            r_qr = sb("qr", [P, QCC, H * R])
            fold_ps = [ctx.enter_context(nc.psum_tensor(f"bw_ps{n}", [P, 512], F32)) for n in range(4)]
            plain_in, up_in = sem("plain_in"), sem("up_in")
            o_in = [sem(f"o_in{n}") for n in range(2)]
            plain_hi, fold_mm, fold_hi, fold_lo = (
                sem("plain_hi"), sem("fold_mm"), sem("fold_hi"), sem("fold_lo"))
            QT = QC - P

            ctx.callback(clear, nc, sems)
            block = ctx.enter_context(nc.Block())

            plain = [(r_kv[:], wkv[0][:], wkv[1][:]), (r_kr[:], wkr[0][:], wkr[1][:]),
                     (r_dq[:], wdq[0][:, :, 0:QC], wdq[1][:, :, 0:QC])]
            for c, rows in enumerate((P, QT)):
                for copy in range(2):
                    plain.append((r_qr[0:rows, c, :].rearrange("p (h r) -> p h r", r=R),
                                  *[w[0:rows, c, :].rearrange("p (h two r) -> p h two r", two=2, r=R)[:, :, copy, :]
                                    for w in wr]))
            folded = []
            for g in range(H // 4):
                for c, rows in enumerate((P, QT)):
                    folded.append((fold_ps[len(folded) % 4][0:rows, :],
                                   *[w[0:rows, c, g * 4 * L:(g + 1) * 4 * L] for w in wa]))
            for h in range(H):
                folded.append((fold_ps[len(folded) % 4][:], *[w[:, h, :] for w in wvo]))

            @block.sync
            def _(sp):
                sp.dma_start(r_uq[:], uq_t.rearrange("(h p) n -> p h n", p=P)).then_inc(up_in, 16)
                sp.dma_start(r_uk[:], uk_t.rearrange("(h p) n -> p h n", p=P)).then_inc(up_in, 16)
                sp.dma_start(r_kv[:], w_kvc.rearrange("(c p) n -> p c n", p=P)).then_inc(plain_in, 16)
                sp.dma_start(r_kr[:], kr_uv).then_inc(plain_in, 16)
                sp.dma_start(r_dq[:], w_dq.rearrange("(c p) n -> p c n", p=P)).then_inc(plain_in, 16)
                sp.dma_start(r_qr[:, 0, :], w_qr[0:P, :]).then_inc(plain_in, 16)
                sp.dma_start(r_qr[0:QT, 1, :], w_qr[P:QC, :]).then_inc(plain_in, 16)
                sp.dma_start(r_uv[:], uv_t.rearrange("(h p) n -> p h n", p=P)).then_inc(up_in, 16)
                for g in range(H // 4):
                    if g >= 2:
                        sp.wait_ge(fold_mm, 8 + 4 * (g - 1))
                    sp.dma_start(r_o[g % 2][:], w_o[g * 4 * L:(g + 1) * 4 * L, :].rearrange(
                        "(h p) n -> p h n", p=P)).then_inc(o_in[g % 2], 16)

            @block.gpsimd
            def _(g):
                for w in (*wa, *wr):
                    g.memset(w[QT:P, 1, :].bitcast(F32), 0.0)

            @block.scalar
            def _(act):
                act.wait_ge(plain_in, 80)
                for raw, hi, _ in plain:
                    act.activation(hi, raw, ACT.Copy).then_inc(plain_hi, 1)
                for n, (bank, hi, _) in enumerate(folded):
                    act.wait_ge(fold_mm, n + 1)
                    act.activation(hi, bank, ACT.Copy).then_inc(fold_hi, 1)

            @block.vector
            def _(v):
                for w in wdq:
                    v.memset(w[:, :, QC:].bitcast(F32), 0.0)
                v.wait_ge(plain_in, 80)
                for n, (raw, hi, lo) in enumerate(plain):
                    v.wait_ge(plain_hi, n + 1)
                    v.tensor_tensor(lo, raw, hi.bitcast(F32), ALU.subtract)
                for n, (bank, hi, lo) in enumerate(folded):
                    v.wait_ge(fold_hi, n + 1)
                    v.tensor_tensor(lo, bank, hi.bitcast(F32), ALU.subtract).then_inc(fold_lo, 1)

            @block.tensor
            def _(pe):
                pe.wait_ge(up_in, 48)
                n = 0
                for g in range(H // 4):
                    for c, rows in enumerate((P, QT)):
                        if n >= 4:
                            pe.wait_ge(fold_lo, n - 3)
                        for k in range(4):
                            last = pe.matmul(fold_ps[n % 4][0:rows, k * L:(k + 1) * L],
                                             r_uq[:, 4 * g + k, c * P:c * P + rows], r_uk[:, 4 * g + k, :],
                                             start=True, stop=True)
                        last.then_inc(fold_mm, 1)
                        n += 1
                for h in range(H):
                    pe.wait_ge(fold_lo, n - 3)
                    if h % 4 == 0:
                        pe.wait_ge(o_in[(h // 4) % 2], 16 * (h // 8 + 1))
                    pe.matmul(fold_ps[n % 4][:], r_uv[:, h, :], r_o[(h // 4) % 2][:, h % 4, :], start=True,
                              stop=True).then_inc(fold_mm, 1)
                    n += 1

        with ExitStack() as ctx:
            sems = []

            def sb(name, shape, dt=F32):
                return ctx.enter_context(nc.sbuf_tensor("b_" + name, shape, dt))

            def pb(name, shape):
                return ctx.enter_context(nc.psum_tensor("b_" + name, shape, F32))

            def sem(name):
                sems.append(ctx.enter_context(nc.semaphore("b_" + name)))
                return sems[-1]

            def parts(name, shape):
                return sb(name + "_hi", shape, F32R), sb(name + "_lo", shape, F32R)

            ident, qtrig = sb("ident", [P, P]), sb("qtrig", [P, S])
            kcos, ksin, ids = sb("kcos", [P, S]), sb("ksin", [P, S]), sb("ids", [P, S])
            segi = sb("segi", [P, B * ST], I32)
            segf, segmid = sb("segf", [P, B * ST]), sb("segmid", [P, B * ST])
            seg_b = sb("seg_b", [P, ST])
            mask, mask_next = sb("mask", [P, ST, S], BF16), sb("mask_next", [P, ST, S], BF16)
            xin, res, ctr = sb("xin", [P, ST, D]), sb("res", [P, ST, D]), sb("ctr", [P, DC, S])
            stats, small = sb("stats", [P, ST, 8]), sb("small", [P, 4, ST])
            xt, ct, qc = parts("xt", [P, DC, S]), parts("ct", [P, DC, S]), parts("qc", [P, QCC, S])
            kt, kr, kn = parts("kt", [P, S]), parts("kr", [P, S]), parts("kn", [P, ST, L])
            q = [parts(f"q{n}", [P, S]) for n in range(2)]
            qr = [parts(f"qr{n}", [P, S]) for n in range(2)]
            tq = [sb(f"tq{n}", [P, S]) for n in range(2)]
            pr = [sb(f"pr{n}", [P, ST, S]) for n in range(2)]
            kr1, kr2 = pr[0][:, 0, :], pr[0][:, 1, :]
            top = [sb(f"top{n}", [P, ST]) for n in range(2)]
            rsum = [sb(f"rsum{n}", [P, ST]) for n in range(2)]
            rinv = [sb(f"rinv{n}", [P, ST]) for n in range(2)]
            pt, z = parts("pt", [P, ST, S]), parts("z", [P, S])

            qa_ps, qr_ps, s_ps, t_ps, z_ps, x_ps = (pb(n, [P, 512]) for n in ("qa_ps", "qr_ps", "s_ps", "t_ps", "z_ps",
                                                                              "x_ps"))
            o_ps = [pb(f"o_ps{n}", [P, D]) for n in range(ST)]

            const_in, seg_float, seg_ready = sem("const_in"), sem("seg_float"), sem("seg_ready")
            x_in, res_in, ctx_in, stored = sem("x_in"), sem("res_in"), sem("ctx_in"), sem("stored")
            ct_hi, ct_lo = sem("ct_hi"), sem("ct_lo")
            seg_copied, distance, squared, mask_made, mask_moved = (
                sem("seg_copied"), sem("distance"), sem("squared"), sem("mask_made"), sem("mask_moved"))
            ln_chain, xn_ready = sem("ln_chain"), sem("xn_ready")
            xt_mm, xt_hi, xt_lo = sem("xt_mm"), sem("xt_hi"), sem("xt_lo")
            qc_mm, qc_hi, qc_lo = sem("qc_mm"), sem("qc_hi"), sem("qc_lo")
            k_mm, k_hi, k_lo = sem("k_mm"), sem("k_hi"), sem("k_lo")
            kr_mm, kr_prod, kr_sum, kr_hi, kr_lo = (sem("kr_mm"), sem("kr_prod"), sem("kr_sum"), sem("kr_hi"),
                                                    sem("kr_lo"))
            kn_mm, kn_ready = sem("kn_mm"), sem("kn_ready")
            out_ready = sem("out_ready")
            sp_step, v_step, g_step = sem("sp_step"), sem("v_step"), sem("g_step")
            qa_mm, qa_hi, qa_lo = sem("qa_mm"), sem("qa_hi"), sem("qa_lo")
            qr_mm, qr_rot, qr_hi, qr_lo = sem("qr_mm"), sem("qr_rot"), sem("qr_hi"), sem("qr_lo")
            s_mm, s_masked, p_exp, p_inv, p_norm = (sem("s_mm"), sem("s_masked"), sem("p_exp"), sem("p_inv"),
                                                    sem("p_norm"))
            t_mm, pt_hi, pt_lo = sem("t_mm"), sem("pt_hi"), sem("pt_lo")
            z_mm, z_hi, z_lo, o_mm = sem("z_mm"), sem("z_hi"), sem("z_lo"), sem("o_mm")

            ctx.callback(clear, nc, sems)
            block = ctx.enter_context(nc.Block())

            def rows_of(array, b):
                return array[b].rearrange("o (t p) c -> p (o t) c", p=P)

            def context_of(b):
                return ctx_t[b].rearrange("o (c p) t -> p (o c) t", p=P)

            @block.sync
            def _(sp):
                sp.dma_start(xin[:], rows_of(x1, slice(0, 1))).then_inc(x_in, 16)
                sp.dma_start(ctr[:], context_of(slice(0, 1))).then_inc(ctx_in, 16)
                sp.dma_start(segi[:], seg_cols).then_inc(const_in, 16)
                for dst, src in ((ident, ident_in), (qtrig, trig), (kcos, rot_cs[0]), (ksin, rot_cs[1]), (ids, key_ids)):
                    sp.dma_start(dst[:], src).then_inc(const_in, 16)
                with sp.Fori(0, B) as i:
                    val = Values(sp, i)
                    now = Batch(val, 0)
                    nxt = sp.snap((i + 1) % B)
                    one, out_done, out_stored = now.done(1, 1), now.done(1, 1 + SEED), now.done(16, 16)
                    hold(sp, xt_mm, now.done(2, 2), sp_step)
                    sp.dma_start(xin[:], rows_of(x1, bass.ds(nxt, 1))).then_inc(x_in, 16)
                    hold(sp, ct_lo, one, sp_step)
                    sp.dma_start(ctr[:], context_of(bass.ds(nxt, 1))).then_inc(ctx_in, 16)
                    sp.dma_start(res[:], rows_of(x1, bass.ds(i, 1))).then_inc(res_in, 16)
                    hold(sp, out_ready, out_done, sp_step)
                    sp.dma_start(rows_of(x2, bass.ds(i, 1)), res[:]).then_inc(stored, 16)
                    hold(sp, stored, out_stored, sp_step)

            @block.scalar
            def _(act):
                act.wait_ge(const_in, 96)
                for s in (qa_hi, qr_hi, p_exp, pt_hi, z_hi):
                    act.sem_inc(s, SEED)

                def context(batch):
                    act.wait_ge(ctx_in, batch.done(16, 16))
                    act.activation(ct[0][:], ctr[:], ACT.Copy).then_inc(ct_hi, 1)

                def norm_t(batch):
                    for n in range(2):
                        act.wait_ge(xt_mm, batch.done(2, n + 1))
                        act.activation(xt[0][:, 2 * n:2 * n + 2, :].rearrange("p c t -> p (c t)"), x_ps[:],
                                       ACT.Copy).then_inc(xt_hi, 1)

                def latent(batch):
                    act.wait_ge(k_mm, batch.done(1, 1))
                    act.activation(kt[0][:], qa_ps[:, 0:S], ACT.Copy).then_inc(k_hi, 1)

                def query_latent(batch):
                    act.wait_ge(qc_mm, batch.done(1, 1))
                    act.activation(qc[0][:].rearrange("p c t -> p (c t)"), qr_ps[:], ACT.Copy).then_inc(qc_hi, 1)

                def rotated_keys(batch):
                    act.wait_ge(kr_sum, batch.done(1, 1))
                    act.activation(kr[0][:], kr1, ACT.Copy).then_inc(kr_hi, 1)

                def latent_rows(batch):
                    act.wait_ge(kn_mm, batch.done(1, 1))
                    for n in range(2):
                        last = act.activation(kn[n][:].rearrange("p t l -> p (t l)"), x_ps[:, n * S:(n + 1) * S],
                                              ACT.Copy)
                    last.then_inc(kn_ready, 1)

                def query(unit, h):
                    act.wait_ge(qa_mm, unit.done(h))
                    act.activation(q[h % 2][0][:], qa_ps[:, 0:S], ACT.Copy).then_inc(qa_hi, 1)
                    act.wait_ge(qr_rot, unit.done(h))
                    act.activation(qr[h % 2][0][:], tq[h % 2][:], ACT.Copy).then_inc(qr_hi, 1)

                def exps(unit, h):
                    act.wait_ge(s_masked, unit.done(h))
                    n = h % 2
                    for t in range(ST):
                        last = act.activation(pr[n][:, t, :], pr[n][:, t, :], ACT.Exp, bias=top[n][:, t:t + 1],
                                              scale=-1.0, accum_out=rsum[n][:, t:t + 1])
                    last.then_inc(p_exp, 1)

                def probs_t(unit, h):
                    act.wait_ge(t_mm, unit.done(h))
                    act.activation(pt[0][:].rearrange("p k t -> p (k t)"), t_ps[:], ACT.Copy).then_inc(pt_hi, 1)

                def mixed(unit, h):
                    act.wait_ge(z_mm, unit.done(h))
                    act.activation(z[0][:], z_ps[:, 0:S], ACT.Copy).then_inc(z_hi, 1)

                first, unit = Batch(Values(act), 0), Unit(Values(act))
                context(first)
                norm_t(first)
                latent(first)
                query_latent(first)
                rotated_keys(first)
                query(unit, 0)
                query(unit, 1)
                exps(unit, 0)
                latent_rows(first)
                with act.Fori(0, B) as i:
                    val = Values(act, i)
                    unit, nxt = Unit(val), Batch(val, 1)
                    for h in range(H):
                        if h + 2 < H:
                            query(unit, h + 2)
                        if h == H // 2:
                            context(nxt)
                        if h == H - 2:
                            norm_t(nxt)
                        probs_t(unit, h)
                        if h + 1 < H:
                            exps(unit, h + 1)
                            mixed(unit, h)
                        if h == H - 2:
                            latent(nxt)
                            query_latent(nxt)
                    rotated_keys(nxt)
                    mixed(unit, H - 1)
                    query(unit, H)
                    query(unit, H + 1)
                    exps(unit, H)
                    latent_rows(nxt)

            @block.vector
            def _(v):
                v.wait_ge(const_in, 96)
                for s in (qa_lo, qr_rot, s_masked, p_inv, p_norm, pt_lo, z_lo, out_ready, ln_chain):
                    v.sem_inc(s, SEED)
                v.tensor_copy(segf[:], segi[:]).then_inc(seg_float, 1)
                v.wait_ge(seg_float, 1)
                v.tensor_scalar(segmid[:], segf[:], -float(LOOKBACK // 2), None, ALU.add).then_inc(seg_ready, 1)

                def norm(batch):
                    v.wait_ge(x_in, batch.done(16, 16))
                    layer_norm(v, xin, stats, small, ln_chain,
                               lambda k: batch.done(LN_LINKS, k + SEED), v_step).then_inc(xn_ready, 1)

                def norm_t(batch):
                    for n in range(2):
                        v.wait_ge(xt_hi, batch.done(2, n + 1))
                        half = slice(2 * n, 2 * n + 2)
                        v.tensor_tensor(xt[1][:, half, :].rearrange("p c t -> p (c t)"), x_ps[:],
                                        xt[0][:, half, :].rearrange("p c t -> p (c t)").bitcast(F32),
                                        ALU.subtract).then_inc(xt_lo, 1)

                def latent(batch):
                    v.wait_ge(k_hi, batch.done(1, 1))
                    v.tensor_tensor(kt[1][:], qa_ps[:, 0:S], kt[0][:].bitcast(F32), ALU.subtract).then_inc(k_lo, 1)

                def query_latent(batch):
                    v.wait_ge(qc_hi, batch.done(1, 1))
                    v.tensor_tensor(qc[1][:].rearrange("p c t -> p (c t)"), qr_ps[:],
                                    qc[0][:].rearrange("p c t -> p (c t)").bitcast(F32),
                                    ALU.subtract).then_inc(qc_lo, 1)

                def rotated_keys(batch):
                    v.wait_ge(kr_mm, batch.done(1, 1))
                    v.tensor_tensor(kr1, x_ps[:, 0:S], kcos[:], ALU.mult)
                    v.tensor_tensor(kr2, x_ps[:, S:], ksin[:], ALU.mult).then_inc(kr_prod, 1)
                    v.wait_ge(kr_prod, batch.done(1, 1))
                    v.tensor_tensor(kr1, kr1, kr2, ALU.add).then_inc(kr_sum, 1)
                    v.wait_ge(kr_hi, batch.done(1, 1))
                    v.tensor_tensor(kr[1][:], kr1, kr[0][:].bitcast(F32), ALU.subtract).then_inc(kr_lo, 1)

                def new_mask(batch):
                    v.wait_ge(mask_made, batch.done(1, 1))
                    v.tensor_copy(mask[:], mask_next[:]).then_inc(mask_moved, 1)

                def query(unit, h):
                    v.wait_ge(qr_mm, unit.done(h))
                    v.tensor_tensor(tq[h % 2][:], qr_ps[:, 0:S], qtrig[:], ALU.mult).then_inc(qr_rot, 1)
                    v.wait_ge(qa_hi, unit.done(h))
                    v.tensor_tensor(q[h % 2][1][:], qa_ps[:, 0:S], q[h % 2][0][:].bitcast(F32),
                                    ALU.subtract).then_inc(qa_lo, 1)

                def masked(unit, h, batch):
                    n = h % 2
                    if h == H or batch.shift == 0 and h == 0:
                        v.wait_ge(mask_moved, batch.done(1, 1))
                    hold(v, s_mm, unit.done(h), v_step)
                    for t in range(ST):
                        last = v.tensor_tensor_reduce(out=pr[n][:, t, :], in0=s_ps[:, t * S:(t + 1) * S],
                                                      in1=mask[:, t, :], scale=-scale, scalar=3e38, op0=ALU.add,
                                                      op1=ALU.min, accum_out=top[n][:, t:t + 1])
                    last.then_inc(s_masked, 1)

                def normalize(unit, h):
                    n = h % 2
                    v.wait_ge(p_exp, unit.done(h))
                    v.reciprocal(rinv[n][:], rsum[n][:]).then_inc(p_inv, 1)
                    v.wait_ge(p_inv, unit.done(h))
                    for t in range(ST):
                        last = v.tensor_scalar(pr[n][:, t, :], pr[n][:, t, :], rinv[n][:, t:t + 1], None, ALU.mult)
                    last.then_inc(p_norm, 1)

                def probs_t(unit, h):
                    v.wait_ge(pt_hi, unit.done(h))
                    v.tensor_tensor(pt[1][:].rearrange("p k t -> p (k t)"), t_ps[:],
                                    pt[0][:].rearrange("p k t -> p (k t)").bitcast(F32),
                                    ALU.subtract).then_inc(pt_lo, 1)

                def mixed(unit, h):
                    v.wait_ge(z_hi, unit.done(h))
                    v.tensor_tensor(z[1][:], z_ps[:, 0:S], z[0][:].bitcast(F32), ALU.subtract).then_inc(z_lo, 1)

                first, unit = Batch(Values(v), 0), Unit(Values(v))
                norm(first)
                norm_t(first)
                latent(first)
                query_latent(first)
                rotated_keys(first)
                query(unit, 0)
                query(unit, 1)
                new_mask(first)
                masked(unit, 0, first)
                normalize(unit, 0)
                with v.Fori(0, B) as i:
                    val = Values(v, i)
                    unit, now, nxt = Unit(val), Batch(val, 0), Batch(val, 1)
                    for h in range(H):
                        if h + 2 < H:
                            query(unit, h + 2)
                        if h + 1 < H:
                            masked(unit, h + 1, nxt)
                        if h == H // 2:
                            norm(nxt)
                        if h == H - 2:
                            norm_t(nxt)
                        probs_t(unit, h)
                        if h + 1 < H:
                            normalize(unit, h + 1)
                            mixed(unit, h)
                        if h == H - 2:
                            latent(nxt)
                            query_latent(nxt)
                    rotated_keys(nxt)
                    mixed(unit, H - 1)
                    query(unit, H)
                    new_mask(nxt)
                    query(unit, H + 1)
                    masked(unit, H, nxt)
                    normalize(unit, H)
                    v.wait_ge(res_in, now.done(16, 16))
                    v.wait_ge(o_mm, unit.done(H - 1))
                    for t in range(ST):
                        last = v.tensor_tensor(res[:, t, :], o_ps[t][:], res[:, t, :], ALU.add)
                    last.then_inc(out_ready, 1)

            @block.gpsimd
            def _(g):
                g.wait_ge(const_in, 96)
                g.sem_inc(qr_lo, SEED)
                g.wait_ge(seg_ready, 1)

                def context(batch):
                    g.wait_ge(ct_hi, batch.done(1, 1))
                    g.tensor_tensor(ct[1][:], ctr[:], ct[0][:].bitcast(F32), ALU.subtract).then_inc(ct_lo, 1)

                def make_mask(batch, col, moved):
                    g.tensor_copy(seg_b[:], segmid[:, col]).then_inc(seg_copied, 1)
                    if moved is not None:
                        hold(g, mask_moved, moved, g_step)
                    hold(g, seg_copied, batch.done(1, 1), g_step)
                    for t in range(ST):
                        last = g.tensor_scalar(mask_next[:, t, :], ids[:], seg_b[:, t:t + 1], None, ALU.subtract)
                    last.then_inc(distance, 1)
                    g.wait_ge(distance, batch.done(1, 1))
                    g.tensor_tensor(mask_next[:], mask_next[:], mask_next[:], ALU.mult).then_inc(squared, 1)
                    hold(g, squared, batch.done(1, 1), g_step)
                    last = g.tensor_scalar(mask_next[:], mask_next[:], float(LOOKBACK // 2) ** 2, MASKED, ALU.is_gt,
                                           ALU.mult)
                    last.then_inc(mask_made, 1)

                def query(unit, h):
                    g.wait_ge(qr_hi, unit.done(h))
                    g.tensor_tensor(qr[h % 2][1][:], tq[h % 2][:], qr[h % 2][0][:].bitcast(F32),
                                    ALU.subtract).then_inc(qr_lo, 1)

                first, unit = Batch(Values(g), 0), Unit(Values(g))
                context(first)
                make_mask(first, slice(0, ST), None)
                query(unit, 0)
                query(unit, 1)
                with g.Fori(0, B) as i:
                    val = Values(g, i)
                    unit, now, nxt = Unit(val), Batch(val, 0), Batch(val, 1)
                    col = g.snap(((i + 1) % B) * ST)
                    for h in range(H):
                        query(unit, h + 2)
                        if h == 3:
                            make_mask(nxt, bass.ds(col, ST), now.done(1, 1))
                        if h == H // 2:
                            context(nxt)

            @block.tensor
            def _(pe):
                pe.wait_ge(const_in, 96)
                for s in (qa_mm, qr_mm, s_mm, t_mm, z_mm, o_mm):
                    pe.sem_inc(s, SEED)

                def norm_t(batch, n):
                    pe.wait_ge(xn_ready, batch.done(1, 1))
                    if n:
                        pe.wait_ge(xt_lo, batch.done(2, 1))
                    for c in range(2):
                        for t in range(ST):
                            at = c * S + t * P
                            last = pe.transpose(x_ps[:, at:at + P], xin[:, t, (2 * n + c) * P:(2 * n + c + 1) * P],
                                                ident[:])
                    last.then_inc(xt_mm, 1)

                def latent(batch, unit, h):
                    pe.wait_ge(ct_lo, batch.done(1, 1))
                    pe.wait_ge(qa_lo, unit.done(h - 1))
                    for c in range(DC):
                        last = product(pe, qa_ps[:, 0:S], [w[:, c, :] for w in wkv], [w[:, c, :] for w in ct],
                                       c == 0, c == DC - 1)
                    last.then_inc(k_mm, 1)

                def query_latent(batch, unit, h):
                    pe.wait_ge(xt_lo, batch.done(2, 2))
                    pe.wait_ge(qr_rot, unit.done(h - 1))
                    for n in range(QCC):
                        for c in range(DC):
                            last = product(pe, qr_ps[:, n * S:(n + 1) * S], [w[:, c, n * P:(n + 1) * P] for w in wdq],
                                           [w[:, c, :] for w in xt], c == 0, c == DC - 1)
                    last.then_inc(qc_mm, 1)

                def rotated_keys(batch):
                    pe.wait_ge(k_lo, batch.done(1, 1))
                    for n in range(2):
                        last = product(pe, x_ps[:, n * S:(n + 1) * S], [w[:, n, :] for w in wkr], [w[:] for w in kt],
                                       True, True)
                    last.then_inc(kr_mm, 1)

                def latent_rows(batch):
                    pe.wait_ge(kr_sum, batch.done(1, 1))
                    for n in range(2):
                        for t in range(ST):
                            at = n * S + t * P
                            last = pe.transpose(x_ps[:, at:at + P], kt[n][:, t * P:(t + 1) * P].bitcast(F32), ident[:])
                    last.then_inc(kn_mm, 1)

                def query(unit, h, head):
                    for bank, free, w, done in ((qr_ps, qr_rot, wr, qr_mm), (qa_ps, qa_lo, wa, qa_mm)):
                        pe.wait_ge(free, unit.done(h - 1))
                        for c in range(QCC):
                            last = product(pe, bank[:, 0:S], [a[:, c, head * L:(head + 1) * L] for a in w],
                                           [a[:, c, :] for a in qc], c == 0, c == QCC - 1)
                        last.then_inc(done, 1)

                def scores(unit, h):
                    n = h % 2
                    pe.wait_ge(s_masked, unit.done(h - 1))
                    pe.wait_ge(qa_lo, unit.done(h))
                    pe.wait_ge(qr_lo, unit.done(h))
                    for t in range(ST):
                        rows = slice(t * P, (t + 1) * P)
                        product(pe, s_ps[:, t * S:(t + 1) * S], [w[:, rows] for w in q[n]], [w[:] for w in kt], True,
                                False)
                        last = product(pe, s_ps[:, t * S:(t + 1) * S], [w[:, rows] for w in qr[n]], [w[:] for w in kr],
                                       False, True)
                    last.then_inc(s_mm, 1)

                def probs_t(unit, h):
                    n = h % 2
                    pe.wait_ge(pt_lo, unit.done(h - 1))
                    pe.wait_ge(p_norm, unit.done(h))
                    for k in range(ST):
                        for t in range(ST):
                            at = k * S + t * P
                            last = pe.transpose(t_ps[:, at:at + P], pr[n][:, t, k * P:(k + 1) * P], ident[:])
                    last.then_inc(t_mm, 1)

                def mixed(unit, h):
                    pe.wait_ge(z_lo, unit.done(h - 1))
                    pe.wait_ge(pt_lo, unit.done(h))
                    for k in range(ST):
                        last = product(pe, z_ps[:, 0:S], [w[:, k, :] for w in kn], [w[:, k, :] for w in pt], k == 0,
                                       k == ST - 1)
                    last.then_inc(z_mm, 1)

                def projected(unit, h):
                    pe.wait_ge(z_lo, unit.done(h))
                    for t in range(ST):
                        last = product(pe, o_ps[t][:], [w[:, t * P:(t + 1) * P] for w in z], [w[:, h, :] for w in wvo],
                                       h == 0, h == H - 1)
                    last.then_inc(o_mm, 1)

                first, unit = Batch(Values(pe), 0), Unit(Values(pe))
                norm_t(first, 0)
                norm_t(first, 1)
                latent(first, unit, 0)
                query_latent(first, unit, 0)
                rotated_keys(first)
                pe.wait_ge(qc_lo, 1)
                query(unit, 0, 0)
                query(unit, 1, 1)
                pe.wait_ge(kr_lo, 1)
                scores(unit, 0)
                latent_rows(first)
                with pe.Fori(0, B) as i:
                    val = Values(pe, i)
                    unit, now, nxt = Unit(val), Batch(val, 0), Batch(val, 1)
                    for h in range(H):
                        if h + 2 < H:
                            query(unit, h + 2, h + 2)
                        if h + 1 < H:
                            scores(unit, h + 1)
                        if h == H - 2:
                            norm_t(nxt, 0)
                        probs_t(unit, h)
                        if h == 1:
                            pe.wait_ge(out_ready, now.done(1, SEED))
                        if h >= 1:
                            projected(unit, h - 1)
                        if h == H - 2:
                            norm_t(nxt, 1)
                        if h == 0:
                            pe.wait_ge(kn_ready, now.done(1, 1))
                        if h + 1 < H:
                            mixed(unit, h)
                        if h == H - 2:
                            latent(nxt, unit, H)
                            query_latent(nxt, unit, H)
                    rotated_keys(nxt)
                    mixed(unit, H - 1)
                    pe.wait_ge(qc_lo, nxt.done(1, 1))
                    query(unit, H, 0)
                    query(unit, H + 1, 1)
                    pe.wait_ge(kr_lo, nxt.done(1, 1))
                    scores(unit, H)
                    projected(unit, H - 1)
                    latent_rows(nxt)


def shared_expert(nc, x2, gate_w, bias, w1, w2, ident_in, xn3, logits, acc_dram, xg, yg):
    with ExitStack() as ctx:
        sems = []

        def sb(name, shape, dt=F32):
            return ctx.enter_context(nc.sbuf_tensor("s_" + name, shape, dt))

        def pb(name, shape):
            return ctx.enter_context(nc.psum_tensor("s_ps_" + name, shape, F32))

        def sem(name):
            sems.append(ctx.enter_context(nc.semaphore("s_" + name)))
            return sems[-1]

        def parts(name, shape):
            return sb(name + "_hi", shape, F32R), sb(name + "_lo", shape, F32R)

        r1, r2, rg = sb("r1", [P, DC, 2 * F]), sb("r2", [P, FC, D]), sb("rg", [P, DC, EP])
        w1p, w2p, wg = parts("w1", [P, DC, 2 * F]), parts("w2", [P, FC, D]), parts("wg", [P, DC, EP])
        ident, zeros, eb = sb("ident", [P, P]), sb("zeros", [P, CT * D]), sb("eb", [P, ST, EP])
        xin, xn, res = sb("xin", [P, ST, D]), sb("xn", [P, ST, D]), sb("res", [P, ST, D])
        stats, small = sb("stats", [P, ST, 8]), sb("small", [P, 4, ST])
        xt = parts("xt", [P, DC, S])
        sil = [sb(f"sil{n}", [P, S]) for n in range(FC)]
        gate = [sb(f"gate{n}", [P, S]) for n in range(FC)]
        gt = [parts(f"gt{n}", [P, S]) for n in range(FC)]
        up_ps = [pb(f"up{n}", [P, 512]) for n in range(FC)]
        gate_ps = [pb(f"gt{n}", [P, 512]) for n in range(FC)]
        x_ps = [pb(f"x{n}", [P, 512]) for n in range(2)]
        y_ps = [pb(f"y{n}", [P, D]) for n in range(ST)]

        w_in, w_hi, w_lo, const_in, zeroed, cleared = (sem("w_in"), sem("w_hi"), sem("w_lo"), sem("const_in"),
                                                       sem("zeroed"), sem("cleared"))
        x_in, res_in, stored = sem("x_in"), sem("res_in"), sem("stored")
        ln_chain, xn_ready, xn_kept = sem("ln_chain"), sem("xn_ready"), sem("xn_kept")
        xt_mm, xt_hi, xt_lo = sem("xt_mm"), sem("xt_hi"), sem("xt_lo")
        logit_mm, logit_out = sem("logit_mm"), sem("logit_out")
        gate_mm, up_mm = sem("gate_mm"), sem("up_mm")
        silu, gated, gt_hi, gt_lo = sem("silu"), sem("gated"), sem("gt_hi"), sem("gt_lo")
        y_mm, acc_ready = sem("y_mm"), sem("acc_ready")
        sp_step, v_step, g_step = sem("sp_step"), sem("v_step"), sem("g_step")

        weights = [(r1, w1p), (r2, w2p), (rg, wg)]
        ctx.callback(clear, nc, sems)
        block = ctx.enter_context(nc.Block())

        def rows_of(array, b):
            return array[b].rearrange("o (t p) c -> p (o t) c", p=P)

        @block.sync
        def _(sp):
            sp.dma_start(xin[:], rows_of(x2, slice(0, 1))).then_inc(x_in, 16)
            sp.dma_start(ident[:], ident_in).then_inc(const_in, 16)
            for t in range(ST):
                sp.dma_start(eb[:, t, :], bias.to_broadcast([P, EP])).then_inc(const_in, 16)
            sp.dma_start(r1[:], w1.rearrange("(c p) n -> p c n", p=P)).then_inc(w_in, 16)
            sp.dma_start(r2[:], w2.rearrange("(c p) n -> p c n", p=P)).then_inc(w_in, 16)
            sp.dma_start(rg[:], gate_w.rearrange("(c p) n -> p c n", p=P)).then_inc(w_in, 16)
            sp.wait_ge(xn_ready, 1)
            sp.dma_start(xin[:], rows_of(x2, slice(1, 2))).then_inc(x_in, 16)
            sp.wait_ge(zeroed, 1)
            for e in range(E):
                sp.dma_start(xg[e * SLOTS:(e + 1) * SLOTS, :].rearrange("(p t) d -> p (t d)", t=CT),
                             zeros[:]).then_inc(cleared, 16)
            sp.dma_start(yg[ROWS:ROWS + P, :], zeros[:, 0:D]).then_inc(cleared, 16)
            with sp.Fori(0, B) as i:
                val = Values(sp, i)
                now = Batch(val, 0)
                after = sp.snap((i + 2) % B)
                normed, out_done, out_stored = now.done(1, 2), now.done(1, 1 + SEED), now.done(16, 16)
                sp.dma_start(res[:], rows_of(x2, bass.ds(i, 1))).then_inc(res_in, 16)
                hold(sp, xn_ready, normed, sp_step)
                sp.dma_start(xin[:], rows_of(x2, bass.ds(after, 1))).then_inc(x_in, 16)
                hold(sp, acc_ready, out_done, sp_step)
                sp.dma_start(rows_of(acc_dram, bass.ds(i, 1)), res[:]).then_inc(stored, 16)
                hold(sp, stored, out_stored, sp_step)
            sp.wait_ge(cleared, 16 * (E + 1))

        @block.scalar
        def _(act):
            act.wait_ge(w_in, 48)
            for raw, w in weights:
                act.activation(w[0][:], raw[:], ACT.Copy).then_inc(w_hi, 1)

            def norm_t(batch):
                for n in range(2):
                    act.wait_ge(xt_mm, batch.done(1, 1))
                    act.activation(xt[0][:, 2 * n:2 * n + 2, :].rearrange("p c t -> p (c t)"), x_ps[n][:],
                                   ACT.Copy).then_inc(xt_hi, 1)

            norm_t(Batch(Values(act), 0))
            with act.Fori(0, B) as i:
                val = Values(act, i)
                now, nxt = Batch(val, 0), Batch(val, 1)
                for n in range(FC):
                    act.wait_ge(gate_mm, now.done(FC, n + 1))
                    act.activation(sil[n][:], gate_ps[n][:, 0:S], ACT.Silu).then_inc(silu, 1)
                    act.wait_ge(gated, now.done(FC, n + 1))
                    act.activation(gt[n][0][:], gate[n][:], ACT.Copy).then_inc(gt_hi, 1)
                norm_t(nxt)

        @block.vector
        def _(v):
            v.memset(zeros[:], 0.0).then_inc(zeroed, 1)
            for n, (raw, w) in enumerate(weights):
                v.wait_ge(w_hi, n + 1)
                v.tensor_tensor(w[1][:], raw[:], w[0][:].bitcast(F32), ALU.subtract).then_inc(w_lo, 1)
            v.wait_ge(const_in, 16 * (1 + ST))
            for s in (ln_chain, acc_ready):
                v.sem_inc(s, SEED)

            def norm(batch, kept):
                v.wait_ge(x_in, batch.done(16, 16))
                if kept:
                    v.wait_ge(xn_kept, batch.done(1, 0))
                    v.wait_ge(xt_mm, batch.done(1, 0))
                layer_norm(v, xin, stats, small, ln_chain, lambda k: batch.done(LN_LINKS, k + SEED), v_step,
                           out=xn).then_inc(xn_ready, 1)

            def norm_t(batch):
                for n in range(2):
                    v.wait_ge(xt_hi, batch.done(2, n + 1))
                    half = slice(2 * n, 2 * n + 2)
                    v.tensor_tensor(xt[1][:, half, :].rearrange("p c t -> p (c t)"), x_ps[n][:],
                                    xt[0][:, half, :].rearrange("p c t -> p (c t)").bitcast(F32),
                                    ALU.subtract).then_inc(xt_lo, 1)

            norm(Batch(Values(v), 0), False)
            norm_t(Batch(Values(v), 0))
            norm(Batch(Values(v), 1), True)
            with v.Fori(0, B) as i:
                val = Values(v, i)
                now, nxt, after = Batch(val, 0), Batch(val, 1), Batch(val, 2)
                col = v.snap(i * ST)
                v.wait_ge(logit_mm, now.done(1, 1))
                v.tensor_tensor(logits[:, bass.ds(col, ST), :], x_ps[0][:, 0:ST * EP].rearrange("p (t e) -> p t e", e=EP),
                                eb[:], ALU.add).then_inc(logit_out, 1)
                for n in range(FC):
                    v.wait_ge(silu, now.done(FC, n + 1))
                    v.wait_ge(up_mm, now.done(FC, n + 1))
                    v.tensor_tensor(gate[n][:], up_ps[n][:, 0:S], sil[n][:], ALU.mult).then_inc(gated, 1)
                    v.wait_ge(gt_hi, now.done(FC, n + 1))
                    v.tensor_tensor(gt[n][1][:], gate[n][:], gt[n][0][:].bitcast(F32), ALU.subtract).then_inc(gt_lo, 1)
                norm_t(nxt)
                norm(after, True)
                v.wait_ge(res_in, now.done(16, 16))
                v.wait_ge(y_mm, now.done(1, 1))
                for t in range(ST):
                    last = v.tensor_tensor(res[:, t, :], y_ps[t][:], res[:, t, :], ALU.add)
                last.then_inc(acc_ready, 1)

        @block.gpsimd
        def _(g):
            hold(g, xn_ready, 1, g_step)
            g.tensor_copy(xn3[:, 0:ST, :], xn[:]).then_inc(xn_kept, 1)
            hold(g, xn_ready, 2, g_step)
            g.tensor_copy(xn3[:, ST:2 * ST, :], xn[:]).then_inc(xn_kept, 1)
            with g.Fori(0, B) as i:
                val = Values(g, i)
                ready, col = val(1, 3), g.snap(((i + 2) % B) * ST)
                hold(g, xn_ready, ready, g_step)
                g.tensor_copy(xn3[:, bass.ds(col, ST), :], xn[:]).then_inc(xn_kept, 1)

        @block.tensor
        def _(pe):
            pe.wait_ge(w_lo, len(weights))
            pe.wait_ge(const_in, 16 * (1 + ST))

            def norm_t(batch):
                pe.wait_ge(xn_ready, batch.done(1, 1))
                for c in range(DC):
                    for t in range(ST):
                        at = (c % 2) * S + t * P
                        last = pe.transpose(x_ps[c // 2][:, at:at + P], xn[:, t, c * P:(c + 1) * P], ident[:])
                last.then_inc(xt_mm, 1)

            norm_t(Batch(Values(pe), 0))
            with pe.Fori(0, B) as i:
                val = Values(pe, i)
                now, nxt = Batch(val, 0), Batch(val, 1)
                pe.wait_ge(xt_lo, now.done(2, 2))
                for t in range(ST):
                    for c in range(DC):
                        last = product(pe, x_ps[0][:, t * EP:(t + 1) * EP], [w[:, c, t * P:(t + 1) * P] for w in xt],
                                       [w[:, c, :] for w in wg], c == 0, c == DC - 1)
                last.then_inc(logit_mm, 1)
                for n in range(FC):
                    for bank, f, done in ((gate_ps[n], FC + n, gate_mm), (up_ps[n], n, up_mm)):
                        for c in range(DC):
                            last = product(pe, bank[:, 0:S], [w[:, c, f * P:(f + 1) * P] for w in w1p],
                                           [w[:, c, :] for w in xt], c == 0, c == DC - 1)
                        last.then_inc(done, 1)
                pe.wait_ge(logit_out, now.done(1, 1))
                norm_t(nxt)
                pe.wait_ge(acc_ready, now.done(1, SEED))
                pe.wait_ge(gt_lo, now.done(FC, FC))
                for t in range(ST):
                    for n in range(FC):
                        last = product(pe, y_ps[t][:], [w[:, t * P:(t + 1) * P] for w in gt[n]],
                                       [w[:, n, :] for w in w2p], n == 0, n == FC - 1)
                last.then_inc(y_mm, 1)


def route(nc, logits, low_tri, slot_base, xn3, weight, gather_at, xg):
    with ExitStack() as ctx:
        sems = []

        def sb(name, shape, dt=F32):
            return ctx.enter_context(nc.sbuf_tensor("r_" + name, shape, dt))

        def sem(name):
            sems.append(ctx.enter_context(nc.semaphore("r_" + name)))
            return sems[-1]

        W = [P, NT, EP]
        aff, rank, beats, chosen, score = sb("aff", W), sb("rank", W), [sb(f"beats{n}", W) for n in range(2)], sb(
            "chosen", W), sb("score", W)
        over, tied, kept, place, tot = sb("over", W), sb("tied", W), sb("kept", W), sb("place", W), sb("tot", W)
        scan = [sb(f"scan{n}", W) for n in range(2)]
        cum, pick, tmp = sb("cum", W), sb("pick", W), sb("tmp", W)
        base = sb("base", [P, EP])
        cnt, need = sb("cnt", [P, EP]), sb("need", [P, EP])
        bit, thr, cand, add = (sb(n, [P, EP], I32) for n in ("bit", "thr", "cand", "add"))
        ones, tri = sb("ones", [P, P]), sb("tri", [P, P])
        dest, has = sb("dest", [P, 2, NT]), sb("has", [P, 2, NT])
        at_s, at_g = sb("at_s", [P, 2, NT]), sb("at_g", [P, 2, NT])
        scatter_at = sb("scatter_at", [P, 2, NT], U32)
        count_ps = ctx.enter_context(nc.psum_tensor("r_count_ps", [P, 512], F32))
        pre_ps = ctx.enter_context(nc.psum_tensor("r_pre_ps", [P, 512], F32))
        tot_ps = ctx.enter_context(nc.psum_tensor("r_tot_ps", [P, 512], F32))

        const_in, aff_ready, chain, search = sem("const_in"), sem("aff_ready"), sem("chain"), sem("search")
        counted, total_mm, sums_in, sums_mm = sem("counted"), sem("total_mm"), sem("sums_in"), sem("sums_mm")
        routed, sent, v_step = sem("routed"), sem("sent"), sem("v_step")
        STEPS, LINKS = 30, 5
        ctx.callback(clear, nc, sems)
        block = ctx.enter_context(nc.Block())

        def wide(a, n=NT):
            return a[:, 0:E].rearrange("p (o e) -> p o e", o=1).to_broadcast([P, n, E])

        @block.sync
        def _(sp):
            sp.dma_start(tri[:], low_tri).then_inc(const_in, 16)
            sp.dma_start(base[:], slot_base.to_broadcast([P, EP])).then_inc(const_in, 16)

        @block.scalar
        def _(act):
            act.activation(aff[:], logits[:], ACT.Sigmoid).then_inc(aff_ready, 1)

        @block.vector
        def _(v):
            count = [0]

            def link(ins):
                count[0] += 1
                ins.then_inc(chain, 1)
                v.wait_ge(chain, count[0])

            def used(a):
                return a[:, :, 0:E]

            for a in (rank, score, kept, tied, over, beats[0], beats[1]):
                v.memset(a[:], 0.0)
            v.memset(cnt[:], 0.0)
            v.memset(ones[:], 1.0)
            v.memset(thr[:].bitcast(F32), 0.0)
            link(v.memset(bit[:], 1 << (STEPS - 1)))
            v.wait_ge(const_in, 32)
            v.wait_ge(aff_ready, 1)
            for e in range(E):
                one = aff[:, :, e:e + 1]
                b = beats[e % 2]
                if e:
                    v.tensor_tensor(b[:, :, 0:e], one.to_broadcast([P, NT, e]), aff[:, :, 0:e], ALU.is_gt)
                    last = v.memset(b[:, :, e:e + 1], 0.0)
                if e < E - 1:
                    last = v.tensor_tensor(b[:, :, e + 1:E], one.to_broadcast([P, NT, E - 1 - e]), aff[:, :, e + 1:E],
                                           ALU.is_ge)
                link(last)
                link(v.tensor_tensor(used(rank), used(rank), used(b), ALU.add))
            link(v.tensor_scalar(used(chosen), used(rank), TOP_K - 0.5, None, ALU.is_lt))
            link(v.tensor_tensor(used(score), used(aff), used(chosen), ALU.mult))
            link(v.tensor_copy(cand[:], bit[:]))

            v.sem_inc(search, 1)
            with v.Fori(0, STEPS) as i:
                val = Values(v, i)

                def step(ins, k):
                    ins.then_inc(search, 1)
                    v.wait_ge(search, val(LINKS, k + 1))

                step(v.tensor_tensor(used(over), used(score), wide(cand[:].bitcast(F32)), ALU.is_ge), 1)
                v.tensor_reduce(cnt[:, 0:E], used(over).rearrange("p t e -> p e t"), AX.X, ALU.add).then_inc(counted, 1)
                v.wait_ge(total_mm, val(1, 1))
                step(v.scalar_tensor_tensor(add[:], count_ps[:, 0:EP], CAP - 0.5, bit[:], ALU.is_gt, ALU.mult), 2)
                v.tensor_tensor(thr[:], thr[:], add[:], ALU.bitwise_or).then_inc(search, 1)
                step(v.tensor_scalar(bit[:], bit[:], 1, None, ALU.logical_shift_right), 4)
                step(v.tensor_tensor(cand[:], thr[:], bit[:], ALU.bitwise_or), 5)

            least = thr[:].bitcast(F32)
            v.tensor_tensor(used(over), used(score), wide(least), ALU.is_gt)
            link(v.tensor_tensor(used(tied), used(score), wide(least), ALU.is_equal))
            v.tensor_reduce(cnt[:, 0:E], used(over).rearrange("p t e -> p e t"), AX.X, ALU.add)
            link(v.tensor_tensor(used(tied), used(tied), used(chosen), ALU.mult))
            v.sem_inc(sums_in, 1)

            def places(k, of):
                v.wait_ge(sums_mm, k)
                v.tensor_copy(place[:], pre_ps[:, 0:NT * EP].rearrange("p (t e) -> p t e", e=EP))
                v.tensor_copy(tot[:], tot_ps[:, 0:NT * EP].rearrange("p (t e) -> p t e", e=EP))
                link(v.tensor_copy(scan[0][:], tot_ps[:, 0:NT * EP].rearrange("p (t e) -> p t e", e=EP)))
                d, n = 1, 0
                while d < NT:
                    v.tensor_copy(scan[1 - n][:, 0:d, :], scan[n][:, 0:d, :])
                    link(v.tensor_tensor(scan[1 - n][:, d:, :], scan[n][:, d:, :], scan[n][:, 0:NT - d, :], ALU.add))
                    d, n = 2 * d, 1 - n
                link(v.tensor_tensor(place[:], place[:], scan[n][:], ALU.add))
                link(v.tensor_tensor(place[:], place[:], tot[:], ALU.subtract))

            places(1, tied)
            link(v.tensor_scalar(need[:, 0:E], count_ps[:, 0:E], -1.0, float(CAP), ALU.mult, ALU.add))
            link(v.tensor_tensor(used(tmp), used(place), wide(need[:]), ALU.is_lt))
            link(v.tensor_tensor(used(tmp), used(tmp), used(tied), ALU.mult))
            link(v.tensor_tensor(used(kept), used(over), used(tmp), ALU.add))
            v.sem_inc(sums_in, 1)
            places(2, kept)
            link(v.tensor_tensor(used(place), used(place), wide(base[:]), ALU.add))
            v.tensor_copy(cum[:, :, 0:1], kept[:, :, 0:1])
            link(v.memset(cum[:, :, E:EP], 0.0))
            for e in range(1, E):
                link(v.tensor_tensor(cum[:, :, e:e + 1], cum[:, :, e - 1:e], kept[:, :, e:e + 1], ALU.add))
            for s in range(2):
                link(v.tensor_scalar(used(pick), used(cum), float(s + 1), None, ALU.is_equal))
                link(v.tensor_tensor(used(pick), used(pick), used(kept), ALU.mult))
                link(v.tensor_reduce(has[:, s, :], used(pick), AX.X, ALU.add))
                link(v.tensor_tensor(used(tmp), used(pick), used(place), ALU.mult))
                link(v.tensor_reduce(dest[:, s, :], used(tmp), AX.X, ALU.add))
                link(v.tensor_tensor(used(tmp), used(pick), used(aff), ALU.mult))
                link(v.tensor_reduce(weight[:, s, :], used(tmp), AX.X, ALU.add))
            for at, away in ((at_s, 4 * ROWS), (at_g, ROWS)):
                link(v.tensor_scalar(at[:], has[:], -float(away), float(away), ALU.mult, ALU.add))
                link(v.tensor_tensor(at[:], at[:], dest[:], ALU.add))
            link(v.tensor_copy(gather_at[:], at_g[:]))
            link(v.tensor_copy(scatter_at[:], at_s[:]))
            v.sem_inc(routed, 1)

        @block.tensor
        def _(pe):
            with pe.Fori(0, STEPS) as i:
                val = Values(pe, i)
                pe.wait_ge(counted, val(1, 1))
                pe.matmul(count_ps[:, 0:EP], ones[:], cnt[:], start=True, stop=True).then_inc(total_mm, 1)
            flat = "p t e -> p (t e)"
            pe.wait_ge(sums_in, 1)
            pe.matmul(count_ps[:, 0:EP], ones[:], cnt[:], start=True, stop=True)
            for k, flags in enumerate((tied, kept)):
                pe.wait_ge(sums_in, k + 1)
                pe.matmul(pre_ps[:, 0:NT * EP], tri[:], flags[:].rearrange(flat), start=True, stop=True)
                pe.matmul(tot_ps[:, 0:NT * EP], ones[:], flags[:].rearrange(flat), start=True,
                          stop=True).then_inc(sums_mm, 1)

        @block.gpsimd
        def _(g):
            g.wait_ge(routed, 1)
            for t in range(NT):
                for s in range(2):
                    g.indirect_dma_start(out=xg, out_offset=bass.IndirectOffsetOnAxis(scatter_at[:, s, t:t + 1], 0),
                                         in_=xn3[:, t, :], in_offset=None, bounds_check=ROWS - 1,
                                         oob_is_err=False).then_inc(sent, 16)
            g.wait_ge(sent, 16 * 2 * NT)


def routed_experts(nc, w1, w2, ident_in, xg, yg):
    HALF = SLOTS // 2
    UNITS = 2 * FC
    with ExitStack() as ctx:
        sems = []

        def sb(name, shape, dt=F32):
            return ctx.enter_context(nc.sbuf_tensor("e_" + name, shape, dt))

        def pb(name, shape):
            return ctx.enter_context(nc.psum_tensor("e_ps_" + name, shape, F32))

        def sem(name):
            sems.append(ctx.enter_context(nc.semaphore("e_" + name)))
            return sems[-1]

        def parts(name, shape):
            return sb(name + "_hi", shape, F32R), sb(name + "_lo", shape, F32R)

        r1, r2, w1p, w2p = sb("r1", [P, DC, 2 * F]), sb("r2", [P, FC, D]), parts("w1", [P, DC, 2 * F]), parts(
            "w2", [P, FC, D])
        ident, xin = sb("ident", [P, P]), sb("xin", [P, CT, D])
        xt = parts("xt", [P, DC, SLOTS])
        sil = [sb(f"sil{n}", [P, HALF]) for n in range(2)]
        gate = [sb(f"gate{n}", [P, HALF]) for n in range(2)]
        gt = parts("gt", [P, FC, SLOTS])
        ysb = sb("ysb", [P, CT, D])
        up_ps, gate_ps, x_ps, y_ps = ([pb(f"{name}{n}", [P, 512]) for n in range(2)] for name in ("up", "gt", "x", "y"))

        const_in, w1_in, w2_in, x_in, stored = sem("const_in"), sem("w1_in"), sem("w2_in"), sem("x_in"), sem("stored")
        w1_hi, w1_lo, w2_hi, w2_lo = sem("w1_hi"), sem("w1_lo"), sem("w2_hi"), sem("w2_lo")
        xt_mm, xt_hi, xt_lo = sem("xt_mm"), sem("xt_hi"), sem("xt_lo")
        gate_mm, up_mm, silu, gated, gt_hi, gt_lo = (sem("gate_mm"), sem("up_mm"), sem("silu"), sem("gated"),
                                                     sem("gt_hi"), sem("gt_lo"))
        y_mm, y_out, y_sent, sp_step = sem("y_mm"), sem("y_out"), sem("y_sent"), sem("sp_step")
        ctx.callback(clear, nc, sems)
        block = ctx.enter_context(nc.Block())

        def load(sp, e, which):
            if which == 1:
                sp.dma_start(r1[:], w1[e].rearrange("o (c p) n -> p (o c) n", p=P)).then_inc(w1_in, 16)
            elif which == 2:
                sp.dma_start(r2[:], w2[e].rearrange("o (c p) n -> p (o c) n", p=P)).then_inc(w2_in, 16)
            else:
                sp.dma_start(xin[:], xg[e].rearrange("o (t p) d -> p (o t) d", p=P)).then_inc(x_in, 16)

        @block.sync
        def _(sp):
            sp.dma_start(ident[:], ident_in).then_inc(const_in, 16)
            for which in (0, 1, 2):
                load(sp, slice(0, 1), which)
            sp.sem_inc(y_sent, 1)
            with sp.Fori(0, E) as i:
                val = Values(sp, i)
                now = Batch(val, 0)
                nxt = sp.snap((i + 1) % E)
                x_free, w1_free, w2_free, y_done, y_stored = (now.done(CT, CT), now.done(1, 1), now.done(1, 1),
                                                              now.done(CT, CT + SEED), now.done(16, 16))
                hold(sp, xt_mm, x_free, sp_step)
                load(sp, bass.ds(nxt, 1), 0)
                hold(sp, w1_lo, w1_free, sp_step)
                load(sp, bass.ds(nxt, 1), 1)
                hold(sp, w2_lo, w2_free, sp_step)
                load(sp, bass.ds(nxt, 1), 2)
                hold(sp, y_out, y_done, sp_step)
                sp.dma_start(yg[bass.ds(i, 1)].rearrange("o (t p) d -> p (o t) d", p=P), ysb[:]).then_inc(stored, 16)
                hold(sp, stored, y_stored, y_sent)

        def split1_hi(act, batch, free):
            act.wait_ge(w1_in, batch.done(16, 16))
            if free is not None:
                act.wait_ge(up_mm, free)
            act.activation(w1p[0][:], r1[:], ACT.Copy).then_inc(w1_hi, 1)

        @block.scalar
        def _(act):
            def norm_t(batch):
                for t in range(CT):
                    act.wait_ge(xt_mm, batch.done(CT, t + 1))
                    act.activation(xt[0][:, :, t * P:(t + 1) * P],
                                   x_ps[t % 2][:].rearrange("p (c t) -> p c t", c=DC), ACT.Copy).then_inc(xt_hi, 1)

            def split2(batch, free):
                act.wait_ge(w2_in, batch.done(16, 16))
                if free is not None:
                    act.wait_ge(y_mm, free)
                act.activation(w2p[0][:], r2[:], ACT.Copy).then_inc(w2_hi, 1)

            first = Batch(Values(act), 0)
            split1_hi(act, first, None)
            split2(first, None)
            norm_t(first)
            with act.Fori(0, E) as i:
                val = Values(act, i)
                now, nxt = Batch(val, 0), Batch(val, 1)
                for u in range(UNITS):
                    half, n = u // FC, u % FC
                    act.wait_ge(gate_mm, now.done(UNITS, u + 1))
                    act.activation(sil[u % 2][:], gate_ps[u % 2][:, 0:HALF], ACT.Silu).then_inc(silu, 1)
                    act.wait_ge(gated, now.done(UNITS, u + 1 + SEED))
                    act.activation(gt[0][:, n, half * HALF:(half + 1) * HALF], gate[u % 2][:],
                                   ACT.Copy).then_inc(gt_hi, 1)
                split1_hi(act, nxt, now.done(UNITS, UNITS))
                norm_t(nxt)
                split2(nxt, now.done(CT, CT))

        @block.vector
        def _(v):
            v.sem_inc(y_out, SEED)
            v.sem_inc(gated, SEED)

            def norm_t(batch):
                for t in range(CT):
                    v.wait_ge(xt_hi, batch.done(CT, t + 1))
                    rows = slice(t * P, (t + 1) * P)
                    v.tensor_tensor(xt[1][:, :, rows], x_ps[t % 2][:].rearrange("p (c t) -> p c t", c=DC),
                                    xt[0][:, :, rows].bitcast(F32), ALU.subtract).then_inc(xt_lo, 1)

            norm_t(Batch(Values(v), 0))
            with v.Fori(0, E) as i:
                val = Values(v, i)
                now, nxt = Batch(val, 0), Batch(val, 1)
                for u in range(UNITS):
                    half, n = u // FC, u % FC
                    cols = slice(half * HALF, (half + 1) * HALF)
                    v.wait_ge(silu, now.done(UNITS, u + 1))
                    v.wait_ge(up_mm, now.done(UNITS, u + 1))
                    v.tensor_tensor(gate[u % 2][:], up_ps[u % 2][:, 0:HALF], sil[u % 2][:], ALU.mult).then_inc(gated, 1)
                    v.wait_ge(gt_hi, now.done(UNITS, u + 1))
                    v.tensor_tensor(gt[1][:, n, cols], gate[u % 2][:], gt[0][:, n, cols].bitcast(F32),
                                    ALU.subtract).then_inc(gt_lo, 1)
                norm_t(nxt)
                for t in range(CT):
                    v.wait_ge(y_mm, now.done(CT, t + 1))
                    if t == 0:
                        v.wait_ge(y_sent, now.done(1, 1))
                    v.tensor_copy(ysb[:, t, :], y_ps[t % 2][:]).then_inc(y_out, 1)

        @block.gpsimd
        def _(g):
            def split(batch):
                g.wait_ge(w1_hi, batch.done(1, 1))
                g.tensor_tensor(w1p[1][:], r1[:], w1p[0][:].bitcast(F32), ALU.subtract).then_inc(w1_lo, 1)
                g.wait_ge(w2_hi, batch.done(1, 1))
                g.tensor_tensor(w2p[1][:], r2[:], w2p[0][:].bitcast(F32), ALU.subtract).then_inc(w2_lo, 1)

            split(Batch(Values(g), 0))
            with g.Fori(0, E) as i:
                split(Batch(Values(g, i), 1))

        @block.tensor
        def _(pe):
            pe.wait_ge(const_in, 16)

            def norm_t(batch, t_from=0):
                pe.wait_ge(x_in, batch.done(16, 16))
                for t in range(CT):
                    if t >= 2:
                        pe.wait_ge(xt_lo, batch.done(CT, t - 1))
                    for c in range(DC):
                        last = pe.transpose(x_ps[t % 2][:, c * P:(c + 1) * P], xin[:, t, c * P:(c + 1) * P], ident[:])
                    last.then_inc(xt_mm, 1)

            norm_t(Batch(Values(pe), 0))
            with pe.Fori(0, E) as i:
                val = Values(pe, i)
                now, nxt = Batch(val, 0), Batch(val, 1)
                pe.wait_ge(w1_lo, now.done(1, 1))
                pe.wait_ge(xt_lo, now.done(CT, CT))
                for u in range(UNITS):
                    half, n = u // FC, u % FC
                    pe.wait_ge(gated, now.done(UNITS, u - 1 + SEED))
                    for bank, f, done in ((gate_ps[u % 2], FC + n, gate_mm), (up_ps[u % 2], n, up_mm)):
                        for c in range(DC):
                            last = product(pe, bank[:, 0:HALF], [w[:, c, f * P:(f + 1) * P] for w in w1p],
                                           [w[:, c, half * HALF:(half + 1) * HALF] for w in xt], c == 0, c == DC - 1)
                        last.then_inc(done, 1)
                norm_t(nxt)
                pe.wait_ge(w2_lo, now.done(1, 1))
                pe.wait_ge(gt_lo, now.done(UNITS, UNITS))
                for t in range(CT):
                    pe.wait_ge(y_out, now.done(CT, t - 1 + SEED))
                    for n in range(FC):
                        last = product(pe, y_ps[t % 2][:], [w[:, n, t * P:(t + 1) * P] for w in gt],
                                       [w[:, n, :] for w in w2p], n == 0, n == FC - 1)
                    last.then_inc(y_mm, 1)


def combine(nc, acc_dram, weight, gather_at, yg, out):
    G = 4
    with ExitStack() as ctx:
        sems = []

        def sb(name, shape, dt=F32):
            return ctx.enter_context(nc.sbuf_tensor("o_" + name, shape, dt))

        def sem(name):
            sems.append(ctx.enter_context(nc.semaphore("o_" + name)))
            return sems[-1]

        acc = [sb(f"acc{n}", [P, D]) for n in range(G)]
        rows = [[sb(f"rows{s}_{n}", [P, D]) for s in range(2)] for n in range(G)]
        at = sb("at", [P, 2, G], U32)
        w = sb("w", [P, 2, G])
        at_copied, w_copied, g_step, v_step, sp_step, a_step = (sem("at_copied"), sem("w_copied"), sem("g_step"),
                                                                sem("v_step"), sem("sp_step"), sem("a_step"))
        acc_in, got, first_added, added, stored = ([sem(f"{k}{n}") for n in range(G)] for k in (
            "acc_in", "got", "first_added", "added", "stored"))
        ctx.callback(clear, nc, sems)
        block = ctx.enter_context(nc.Block())
        acc_t, out_t = (a.rearrange("b (t p) d -> (b t) p d", p=P) for a in (acc_dram, out))

        @block.gpsimd
        def _(g):
            with g.Fori(0, NT // G) as i:
                val = Values(g, i)
                col = g.snap(i * G)
                free, copied = val(1, 1), val(1, 1)
                hold(g, added[G - 1], free, g_step)
                g.tensor_copy(at[:], gather_at[:, :, bass.ds(col, G)]).then_inc(at_copied, 1)
                hold(g, at_copied, copied, g_step)
                for n in range(G):
                    for s in range(2):
                        g.indirect_dma_start(out=rows[n][s][:], out_offset=None, in_=yg,
                                             in_offset=bass.IndirectOffsetOnAxis(at[:, s, n:n + 1], 0)
                                             ).then_inc(got[n], 16)

        @block.sync
        def _(sp):
            with sp.Fori(0, NT // G) as i:
                val = Values(sp, i)
                free = val(16, 16)
                for n in range(G):
                    tile = sp.snap(i * G + n)
                    hold(sp, stored[n], free, sp_step)
                    sp.dma_start(acc[n][:], acc_t[bass.ds(tile, 1)].rearrange("o p d -> (o p) d")).then_inc(
                        acc_in[n], 16)

        @block.vector
        def _(v):
            v.sem_inc(added[G - 1], 1)
            with v.Fori(0, NT // G) as i:
                val = Values(v, i)
                col = v.snap(i * G)
                hold(v, added[G - 1], val(1, 1), v_step)
                v.tensor_copy(w[:], weight[:, :, bass.ds(col, G)]).then_inc(w_copied, 1)
                v.wait_ge(w_copied, val(1, 1))
                for n in range(G):
                    v.wait_ge(acc_in[n], val(16, 16))
                    v.wait_ge(got[n], val(32, 32))
                    v.scalar_tensor_tensor(acc[n][:], rows[n][0][:], w[:, 0, n:n + 1], acc[n][:], ALU.mult,
                                           ALU.add).then_inc(first_added[n], 1)
                for n in range(G):
                    v.wait_ge(first_added[n], val(1, 1))
                    v.scalar_tensor_tensor(acc[n][:], rows[n][1][:], w[:, 1, n:n + 1], acc[n][:], ALU.mult,
                                           ALU.add).then_inc(added[n], 1)

        @block.scalar
        def _(act):
            for n in range(G):
                act.sem_inc(stored[n], 16)
            with act.Fori(0, NT // G) as i:
                val = Values(act, i)
                for n in range(G):
                    tile = act.snap(i * G + n)
                    act.wait_ge(added[n], val(1, 2 if n == G - 1 else 1))
                    act.dma_start(out_t[bass.ds(tile, 1)].rearrange("o p d -> (o p) d"), acc[n][:]).then_inc(
                        stored[n], 16)
            for n in range(G):
                act.wait_ge(stored[n], 16 * (NT // G + 1))


def mixture(nc, x2, gate_w, bias, shared_w1, shared_w2, w1, w2, low_tri, slot_base, ident, acc, xg, yg, out):
    with ExitStack() as ctx:
        def sb(name, shape, dt=F32):
            return ctx.enter_context(nc.sbuf_tensor("m_" + name, shape, dt))

        weight, gather_at = sb("weight", [P, 2, NT]), sb("gather_at", [P, 2, NT], U32)
        with ExitStack() as until_sent:
            xn3 = until_sent.enter_context(nc.sbuf_tensor("m_xn3", [P, NT, D], F32))
            logits = until_sent.enter_context(nc.sbuf_tensor("m_logits", [P, NT, EP], F32))
            shared_expert(nc, x2, gate_w, bias, shared_w1, shared_w2, ident, xn3, logits, acc, xg, yg)
            route(nc, logits, low_tri, slot_base, xn3, weight, gather_at, xg)
        routed_experts(nc, w1, w2, ident, xg.rearrange("(e s) d -> e s d", s=SLOTS),
                       yg[0:ROWS, :].rearrange("(e s) d -> e s d", s=SLOTS))
        combine(nc, acc, weight, gather_at, yg, out)


def decoder_layer(nc, a, out):
    def scratch(name, shape):
        return nc.dram_tensor(name, shape, F32, kind="Internal").ap()

    x1, x2, acc = (scratch(name, (B, S, D)) for name in ("x1", "x2", "acc"))
    self_attention(nc, a["x"], a["w_lat"], a["b_lat"], a["w_d"], a["b_d"], a["w_proj"], a["b_proj"], a["causal"],
                   a["ident"], x1)
    cross_attention(nc, x1, a["ctx_t"], a["seg"], a["w_kvc"], a["w_dq"], a["uq_t"], a["w_qr"], a["uk_t"], a["kr_uv"],
                    a["uv_t"], a["w_o"], a["trig"], a["rot_cs"], a["key_ids"], a["ident"], x2)
    mixture(nc, x2, a["gate_w"], a["bias"], a["shared_w1"], a["shared_w2"], a["w1"], a["w2"], a["low_tri"],
            a["slot_base"], a["ident"], acc, scratch("xg", (ROWS, D)), scratch("yg", (ROWS + P, D)), out)


def kernel(**inputs):
    import numpy as np
    import concourse.bacc as bacc
    from concourse import mybir as _mybir
    from concourse.bass_utils import run_bass_kernel_spmd

    nc = bacc.Bacc("TRN2", target_bir_lowering=False, num_devices=1)
    arrays, args = {}, {}

    def give(name, a):
        a = np.ascontiguousarray(a)
        arrays[f"in_{name}"] = a
        args[name] = nc.dram_tensor(f"in_{name}", a.shape, _mybir.dt.from_np(a.dtype), kind="ExternalInput").ap()

    def padded(a, shape):
        wide = np.zeros(shape, np.float32)
        wide[:, 0:a.shape[-1]] = a
        return wide

    attn = {k: np.asarray(inputs["L0_attn_" + k]) for k in ("W_lat", "b_lat", "W_d", "b_d", "W_proj", "b_proj")}
    cross = {k: np.asarray(inputs["L0_xattn_" + k]) for k in ("W_kvc", "W_dq", "W_uq", "W_qr", "W_uk", "W_kr", "W_uv",
                                                              "W_o")}
    ffn = {k: np.asarray(inputs["L0_ffn_" + k]) for k in ("gate_w", "expert_bias", "shared_w1", "shared_w2",
                                                          "routed_w1", "routed_w2")}
    give("x", inputs["x"])
    for k in ("W_lat", "b_lat", "W_d", "W_proj", "b_proj"):
        give(k.lower(), attn[k])
    give("b_d", attn["b_d"].reshape(H, L).T)
    t = np.arange(P)
    triangle = np.where(t[None, :] <= t[:, None], 0.0, MASKED).astype(np.float32)
    give("causal", np.concatenate([triangle, np.zeros((P, P), np.float32), triangle], 1))
    give("ident", np.eye(P, dtype=np.float32))
    give("ctx_t", np.asarray(inputs["ctx_2048"]).transpose(0, 2, 1))
    give("seg", np.asarray(inputs["itok_BxS_0_1023"]).reshape(NT, P).T)
    for k in ("W_kvc", "W_dq", "W_qr", "W_o"):
        give(k.lower(), cross[k])
    for k in ("uq", "uk", "uv"):
        give(k + "_t", cross["W_" + k].T)
    half = R // 2
    k1, k2 = cross["W_kr"][:, 0:half], cross["W_kr"][:, half:R]
    give("kr_uv", np.stack([np.concatenate([k1, k2, k2, k1], 1), np.concatenate([k2, k1, k1, k2], 1)], 1))
    freq = np.float32(1.0) / np.float32(10000.0) ** (np.arange(half, dtype=np.float32) / np.float32(half))
    angle = np.arange(S, dtype=np.float32)[None, :] * freq[:, None]
    cos, sin = np.cos(angle), np.sin(angle)
    give("trig", np.concatenate([cos, cos, sin, sin], 0))
    give("rot_cs", np.stack([np.concatenate([cos, cos, cos, -cos], 0), np.concatenate([-sin, sin, sin, sin], 0)]))
    give("key_ids", np.broadcast_to(np.arange(S, dtype=np.float32)[None, :], (P, S)))
    give("gate_w", padded(ffn["gate_w"], (D, EP)))
    give("bias", padded(ffn["expert_bias"], (1, EP)))
    give("shared_w1", ffn["shared_w1"][0])
    give("shared_w2", ffn["shared_w2"][0])
    give("w1", ffn["routed_w1"])
    give("w2", ffn["routed_w2"])
    give("low_tri", np.triu(np.ones((P, P), np.float32), 1))
    give("slot_base", (np.arange(EP, dtype=np.float32) * SLOTS)[None, :])

    out = nc.dram_tensor("out_0", (B, S, D), _mybir.dt.float32, kind="ExternalOutput").ap()
    decoder_layer(nc, args, out)
    r = run_bass_kernel_spmd(nc, [arrays], core_ids=[0])
    return r.results[0]["out_0"]
```

```python
import math
from contextlib import ExitStack

import concourse.bass as bass
from concourse import mybir

F32 = mybir.dt.float32
F32R = mybir.dt.float32r
BF16 = mybir.dt.bfloat16
I32 = mybir.dt.int32
U32 = mybir.dt.uint32
ALU = mybir.AluOpType
ACT = mybir.ActivationFunctionType
AX = mybir.AxisListType

P = 128
B, S, D = 16, 256, 512
H = 16
L = 128
ST = S // P
DC = D // P
QC, QCC = 192, 2
R = 64
EPS = 1e-5
MASKED = -float(2 ** 100)
LOOKBACK = 8
NT = B * ST
E, EP = 7, 8
F = 256
FC = F // P
TOP_K = 2
CAP = B * S // E
CT = -(-CAP // P)
SLOTS = CT * P
ROWS = E * SLOTS
LN_LINKS = 14
NORM_AT = 5
SEED = 2


class Values:

    def __init__(self, eng, i=None):
        self.eng, self.i, self.known = eng, i, {}

    def __call__(self, per, k):
        if self.i is None or per == 0:
            return k
        if (per, k) not in self.known:
            self.known[per, k] = self.eng.snap(self.i * per + k)
        return self.known[per, k]


class Unit:

    def __init__(self, values):
        self.values = values

    def done(self, h):
        return self.values(H, h + 1 + SEED)


class Batch:

    def __init__(self, values, shift):
        self.values, self.shift = values, shift

    def done(self, per=1, k=0):
        return self.values(per, per * self.shift + k)


def clear(nc, sems):
    for s in sems:
        nc.gpsimd.sem_clear(s)
    nc.all_engine_barrier()


def hold(eng, sem, value, step):
    eng.wait_ge(sem, value)
    eng.sem_inc(step, 1)


def product(pe, out, lhs, rhs, first, last):
    pe.matmul(out, lhs[0], rhs[0], start=first, stop=False)
    pe.matmul(out, lhs[0], rhs[1], start=False, stop=False)
    return pe.matmul(out, lhs[1], rhs[0], start=False, stop=last)


class LayerNorm:

    PIECES = ST + 4 + ST

    def __init__(self, v, xt, stats, small, chain, at, step, out=None):
        self.v, self.xt, self.stats, self.chain, self.at, self.step = v, xt, stats, chain, at, step
        self.out = xt if out is None else out
        self.ve, self.half, self.y, self.w = (small[:, n, :] for n in range(4))
        self.links = 0

    def link(self, ins):
        self.links += 1
        ins.then_inc(self.chain, 1)
        self.v.wait_ge(self.chain, self.at(self.links))

    def moments(self, t):
        last = self.v.bn_stats(self.stats[:, t, 0:6], self.xt[:, t, :])
        if t == ST - 1:
            last.then_inc(self.chain, 1)
            self.links += 1

    def variance(self):
        v, y = self.v, self.y.bitcast(I32)
        hold(v, self.chain, self.at(1), self.step)
        for t in range(ST):
            last = v.bn_aggr(self.stats[:, t, 6:8], self.stats[:, t, 0:6])
        self.link(last)
        self.link(v.tensor_scalar(self.ve, self.stats[:, :, 7], EPS, None, ALU.add))
        v.tensor_scalar(self.half, self.ve, -0.5, None, ALU.mult)
        self.link(v.tensor_scalar(y, self.ve.bitcast(I32), 1, None, ALU.logical_shift_right))
        self.link(v.tensor_scalar(y, y, -1.0, float(0x5F3759DF), ALU.mult, ALU.add))

    def newton(self, n):
        v, y, w = self.v, self.y, self.w
        self.link(v.tensor_tensor(w, y, self.half, ALU.mult))
        self.link(v.tensor_tensor(w, w, y, ALU.mult))
        self.link(v.scalar_tensor_tensor(y, w, 1.5, y, ALU.add, ALU.mult))
        assert n < 2 or self.links == LN_LINKS

    def apply(self, t):
        return self.v.tensor_scalar(self.out[:, t, :], self.xt[:, t, :], self.stats[:, t, 6:7], self.y[:, t:t + 1],
                                    ALU.subtract, ALU.mult)

    def piece(self, n):
        if n < ST:
            return self.moments(n)
        if n == ST:
            return self.variance()
        if n < ST + 4:
            return self.newton(n - ST - 1)
        return self.apply(n - ST - 4)

    def whole(self):
        for n in range(self.PIECES):
            last = self.piece(n)
        return last


def self_attention(nc, x, w_lat, b_lat, w_d, b_d, w_proj, b_proj, causal, ident_in, x1):
    scale = 1.0 / math.sqrt(L)
    PK = 3 * P
    with ExitStack() as ctx:
        sems = []

        def sb(name, shape, dt=F32):
            return ctx.enter_context(nc.sbuf_tensor("a_" + name, shape, dt))

        def pb(name, shape):
            return ctx.enter_context(nc.psum_tensor("a_" + name, shape, F32))

        def sem(name):
            sems.append(ctx.enter_context(nc.semaphore("a_" + name)))
            return sems[-1]

        def parts(name, shape):
            return sb(name + "_hi", shape, F32R), sb(name + "_lo", shape, F32R)

        wd = parts("wd", [P, DC, H * L])
        wp = parts("wp", [P, H, D])
        wl = parts("wl", [P, DC, L])
        raw = [sb(f"raw{n}", [P, 2048]) for n in range(2)]
        raw_l = raw[0][:, 0:DC * L].rearrange("p (c n) -> p c n", c=DC)
        bd = sb("bd", [P, H])
        bl = sb("bl", [P, 1])
        bp = sb("bp", [P, D])
        mask = sb("mask", [P, PK])
        ident = sb("ident", [P, P])
        xin = sb("xin", [P, ST, D])
        stats = sb("stats", [P, ST, 8])
        small = sb("small", [P, 4, ST])
        xt = parts("xt", [P, DC, S])
        kt = parts("kt", [P, S])
        kn = parts("kn", [P, ST, L])
        q = [parts(f"q{n}", [P, S]) for n in range(2)]
        pr = [sb(f"pr{n}", [P, PK]) for n in range(2)]
        top = [sb(f"top{n}", [P, ST]) for n in range(2)]
        rsum = [sb(f"rsum{n}", [P, ST]) for n in range(2)]
        rinv = [sb(f"rinv{n}", [P, ST]) for n in range(2)]
        pt = parts("pt", [P, PK])
        y = parts("y", [P, S])
        res = sb("res", [P, ST, D])

        s_ps, t_ps, y_ps = (pb(n, [P, 512]) for n in ("s_ps", "t_ps", "y_ps"))
        o_ps = [pb(f"o_ps{n}", [P, D]) for n in range(ST)]
        x_ps = [pb(f"x_ps{n}", [P, 512]) for n in range(2)]
        q_ps = [pb("q_ps0", [P, 512]), x_ps[1]]

        raw_in = [sem(f"raw_in{n}") for n in range(2)]
        raw_split, w_hi = sem("raw_split"), sem("w_hi")
        const_in = sem("const_in")
        x_in, res_in, stored = sem("x_in"), sem("res_in"), sem("stored")
        ln_chain, xn_ready = sem("ln_chain"), sem("xn_ready")
        xt_mm, xt_hi, xt_lo = sem("xt_mm"), sem("xt_hi"), sem("xt_lo")
        k_mm, k_hi, k_lo = sem("k_mm"), sem("k_hi"), sem("k_lo")
        kn_mm, kn_ready = sem("kn_mm"), sem("kn_ready")
        res_biased, out_ready = sem("res_biased"), sem("out_ready")
        sp_step, v_step = sem("sp_step"), sem("v_step")
        q_mm, q_hi, q_lo = sem("q_mm"), sem("q_hi"), sem("q_lo")
        s_mm, s_masked, p_exp, p_inv, p_norm = sem("s_mm"), sem("s_masked"), sem("p_exp"), sem("p_inv"), sem("p_norm")
        t_mm, pt_hi, pt_lo = sem("t_mm"), sem("pt_hi"), sem("pt_lo")
        y_mm, y_hi, y_lo, o_mm = sem("y_mm"), sem("y_hi"), sem("y_lo"), sem("o_mm")

        def piece(src, dst, width):
            return src, dst[0], dst[1], width

        pieces = [piece(w_lat.rearrange("(c p) n -> p c n", p=P),
                        [w[:, :, :].rearrange("p c n -> p (c n)") for w in wl], DC * L)]
        for c in range(DC):
            pieces.append(piece(w_d[c * P:(c + 1) * P, :], [w[:, c, :] for w in wd], H * L))
        for g in range(0, H, 4):
            pieces.append(piece(w_proj[g * P:(g + 4) * P, :].rearrange("(h p) n -> p h n", p=P),
                                [w[:, g:g + 4, :].rearrange("p h n -> p (h n)") for w in wp], 4 * D))

        ctx.callback(clear, nc, sems)
        block = ctx.enter_context(nc.Block())

        @block.sync
        def _(sp):
            sp.dma_start(xin[:], x[0].rearrange("(t p) c -> p t c", p=P)).then_inc(x_in, 16)
            sp.dma_start(ident[:], ident_in).then_inc(const_in, 16)
            sp.dma_start(mask[:], causal).then_inc(const_in, 16)
            sp.dma_start(bd[:], b_d).then_inc(const_in, 16)
            sp.dma_start(bl[:], b_lat.rearrange("(p o) -> p o", o=1)).then_inc(const_in, 16)
            sp.dma_start(bp[:], b_proj.rearrange("(o n) -> o n", o=1).to_broadcast([P, D])).then_inc(const_in, 16)
            for n, (src, _, _, width) in enumerate(pieces):
                if n >= 2:
                    sp.wait_ge(raw_split, n - 1)
                dst = raw[n % 2][:, 0:width]
                if n == 0:
                    dst = raw_l
                elif n > DC:
                    dst = dst.rearrange("p (h n) -> p h n", n=D)
                sp.dma_start(dst, src).then_inc(raw_in[n % 2], 16)
            with sp.Fori(0, B) as i:
                val = Values(sp, i)
                now = Batch(val, 0)
                nxt = sp.snap((i + 1) % B)
                xt_read, out_done, out_stored = now.done(2, 2), now.done(1, 1 + SEED), now.done(16, 16)
                hold(sp, xt_mm, xt_read, sp_step)
                sp.dma_start(xin[:], x[bass.ds(nxt, 1)].rearrange("o (t p) c -> p (o t) c", p=P)).then_inc(x_in, 16)
                sp.dma_start(res[:], x[bass.ds(i, 1)].rearrange("o (t p) c -> p (o t) c", p=P)).then_inc(res_in, 16)
                hold(sp, out_ready, out_done, sp_step)
                sp.dma_start(x1[bass.ds(i, 1)].rearrange("o (t p) c -> p (o t) c", p=P), res[:]).then_inc(stored, 16)
                hold(sp, stored, out_stored, sp_step)

        @block.scalar
        def _(act):
            for n, (_, hi, _, width) in enumerate(pieces):
                act.wait_ge(raw_in[n % 2], 16 * (n // 2 + 1))
                act.activation(hi, raw[n % 2][:, 0:width], ACT.Copy).then_inc(w_hi, 1)
            act.wait_ge(const_in, 80)
            for s in (q_hi, p_exp, pt_hi, y_hi):
                act.sem_inc(s, SEED)

            def keys(batch):
                for n in range(2):
                    act.wait_ge(xt_mm, batch.done(2, n + 1))
                    act.activation(xt[0][:, 2 * n:2 * n + 2, :].rearrange("p c t -> p (c t)"), x_ps[n][:],
                                   ACT.Copy).then_inc(xt_hi, 1)

            def latent(batch):
                act.wait_ge(k_mm, batch.done(1, 1))
                act.activation(kt[0][:], x_ps[0][:, 0:S], ACT.Identity, bias=bl[:]).then_inc(k_hi, 1)

            def latent_rows(batch):
                act.wait_ge(kn_mm, batch.done(1, 1))
                for n in range(2):
                    last = act.activation(kn[n][:].rearrange("p t l -> p (t l)"), x_ps[0][:, n * S:(n + 1) * S], ACT.Copy)
                last.then_inc(kn_ready, 1)

            def query(unit, h, head):
                act.wait_ge(q_mm, unit.done(h))
                act.activation(q[h % 2][0][:], q_ps[h % 2][:, 0:S], ACT.Identity, bias=bd[:, head:head + 1]).then_inc(q_hi, 1)

            def exps(unit, h):
                act.wait_ge(s_masked, unit.done(h))
                n = h % 2
                act.activation(pr[n][:, 0:P], pr[n][:, 0:P], ACT.Exp, bias=top[n][:, 0:1], scale=-1.0,
                               accum_out=rsum[n][:, 0:1])
                act.activation(pr[n][:, P:PK], pr[n][:, P:PK], ACT.Exp, bias=top[n][:, 1:2], scale=-1.0,
                               accum_out=rsum[n][:, 1:2]).then_inc(p_exp, 1)

            def probs_t(unit, h):
                act.wait_ge(t_mm, unit.done(h))
                act.activation(pt[0][:], t_ps[:, 0:PK], ACT.Copy).then_inc(pt_hi, 1)

            def mixed(unit, h):
                act.wait_ge(y_mm, unit.done(h))
                act.activation(y[0][:], y_ps[:, 0:S], ACT.Copy).then_inc(y_hi, 1)

            first, unit = Batch(Values(act), 0), Unit(Values(act))
            keys(first)
            latent(first)
            query(unit, 0, 0)
            query(unit, 1, 1)
            exps(unit, 0)
            latent_rows(first)
            with act.Fori(0, B) as i:
                val = Values(act, i)
                unit, nxt = Unit(val), Batch(val, 1)
                probs_t(unit, 0)
                exps(unit, 1)
                query(unit, 2, 2)
                mixed(unit, 0)
                for h in range(1, H - 2):
                    query(unit, h + 2, h + 2)
                    probs_t(unit, h)
                    exps(unit, h + 1)
                    mixed(unit, h)
                keys(nxt)
                probs_t(unit, H - 2)
                exps(unit, H - 1)
                mixed(unit, H - 2)
                latent(nxt)
                probs_t(unit, H - 1)
                query(unit, H, 0)
                mixed(unit, H - 1)
                exps(unit, H)
                query(unit, H + 1, 1)
                latent_rows(nxt)

        @block.vector
        def _(v):
            for n, (_, hi, lo, width) in enumerate(pieces):
                v.wait_ge(w_hi, n + 1)
                v.tensor_tensor(lo, raw[n % 2][:, 0:width], hi.bitcast(F32), ALU.subtract).then_inc(raw_split, 1)
            v.wait_ge(const_in, 80)
            for s in (q_lo, s_masked, p_inv, p_norm, pt_lo, y_lo, out_ready, ln_chain):
                v.sem_inc(s, SEED)

            def norm(batch):
                v.wait_ge(x_in, batch.done(16, 16))
                return LayerNorm(v, xin, stats, small, ln_chain, lambda k: batch.done(LN_LINKS, k + SEED), v_step)

            def keys(batch, n):
                v.wait_ge(xt_hi, batch.done(2, n + 1))
                half = slice(2 * n, 2 * n + 2)
                v.tensor_tensor(xt[1][:, half, :].rearrange("p c t -> p (c t)"), x_ps[n][:],
                                xt[0][:, half, :].rearrange("p c t -> p (c t)").bitcast(F32),
                                ALU.subtract).then_inc(xt_lo, 1)

            def latent(batch):
                v.wait_ge(k_hi, batch.done(1, 1))
                v.scalar_tensor_tensor(kt[1][:], x_ps[0][:, 0:S], bl[:], kt[0][:].bitcast(F32), ALU.add,
                                       ALU.subtract).then_inc(k_lo, 1)

            def query(unit, h, head):
                v.wait_ge(q_hi, unit.done(h))
                v.scalar_tensor_tensor(q[h % 2][1][:], q_ps[h % 2][:, 0:S], bd[:, head:head + 1],
                                       q[h % 2][0][:].bitcast(F32), ALU.add, ALU.subtract).then_inc(q_lo, 1)

            def masked(unit, h):
                n = h % 2
                hold(v, s_mm, unit.done(h), v_step)
                v.tensor_tensor_reduce(out=pr[n][:, 0:P], in0=s_ps[:, 0:P], in1=mask[:, 0:P], scale=-scale, scalar=3e38,
                                       op0=ALU.add, op1=ALU.min, accum_out=top[n][:, 0:1])
                v.tensor_tensor_reduce(out=pr[n][:, P:PK], in0=s_ps[:, P:PK], in1=mask[:, P:PK], scale=-scale,
                                       scalar=3e38, op0=ALU.add, op1=ALU.min,
                                       accum_out=top[n][:, 1:2]).then_inc(s_masked, 1)

            def normalize(unit, h):
                n = h % 2
                v.wait_ge(p_exp, unit.done(h))
                v.reciprocal(rinv[n][:], rsum[n][:]).then_inc(p_inv, 1)
                v.wait_ge(p_inv, unit.done(h))
                v.tensor_scalar(pr[n][:, 0:P], pr[n][:, 0:P], rinv[n][:, 0:1], None, ALU.mult)
                v.tensor_scalar(pr[n][:, P:PK], pr[n][:, P:PK], rinv[n][:, 1:2], None, ALU.mult).then_inc(p_norm, 1)

            def probs_t(unit, h):
                v.wait_ge(pt_hi, unit.done(h))
                v.tensor_tensor(pt[1][:], t_ps[:, 0:PK], pt[0][:].bitcast(F32), ALU.subtract).then_inc(pt_lo, 1)

            def mixed(unit, h):
                v.wait_ge(y_hi, unit.done(h))
                v.tensor_tensor(y[1][:], y_ps[:, 0:S], y[0][:].bitcast(F32), ALU.subtract).then_inc(y_lo, 1)

            first, unit = Batch(Values(v), 0), Unit(Values(v))
            norm(first).whole().then_inc(xn_ready, 1)
            keys(first, 0)
            keys(first, 1)
            latent(first)
            query(unit, 0, 0)
            query(unit, 1, 1)
            masked(unit, 0)
            normalize(unit, 0)
            with v.Fori(0, B) as i:
                val = Values(v, i)
                unit, now, nxt = Unit(val), Batch(val, 0), Batch(val, 1)
                masked(unit, 1)
                probs_t(unit, 0)
                query(unit, 2, 2)
                normalize(unit, 1)
                mixed(unit, 0)
                for h in range(1, H - 2):
                    query(unit, h + 2, h + 2)
                    probs_t(unit, h)
                    masked(unit, h + 1)
                    if h == NORM_AT:
                        next_norm = norm(nxt)
                    if 0 <= h - NORM_AT < LayerNorm.PIECES:
                        last = next_norm.piece(h - NORM_AT)
                    normalize(unit, h + 1)
                    mixed(unit, h)
                last.then_inc(xn_ready, 1)
                keys(nxt, 0)
                probs_t(unit, H - 2)
                masked(unit, H - 1)
                keys(nxt, 1)
                normalize(unit, H - 1)
                mixed(unit, H - 2)
                latent(nxt)
                probs_t(unit, H - 1)
                query(unit, H, 0)
                mixed(unit, H - 1)
                masked(unit, H)
                query(unit, H + 1, 1)
                normalize(unit, H)
                v.wait_ge(res_biased, now.done(1, 1))
                v.wait_ge(o_mm, unit.done(H - 1))
                for t in range(ST):
                    last = v.tensor_tensor(res[:, t, :], o_ps[t][:], res[:, t, :], ALU.add)
                last.then_inc(out_ready, 1)

        @block.gpsimd
        def _(g):
            g.wait_ge(const_in, 80)
            with g.Fori(0, B) as i:
                now = Batch(Values(g, i), 0)
                g.wait_ge(res_in, now.done(16, 16))
                for t in range(ST):
                    last = g.tensor_tensor(res[:, t, :], res[:, t, :], bp[:], ALU.add)
                last.then_inc(res_biased, 1)

        @block.tensor
        def _(pe):
            pe.wait_ge(raw_split, len(pieces))
            pe.wait_ge(const_in, 80)
            for s in (q_mm, s_mm, t_mm, y_mm, o_mm):
                pe.sem_inc(s, SEED)

            def transposed_norm(batch):
                pe.wait_ge(xn_ready, batch.done(1, 1))
                for c in range(DC):
                    for t in range(ST):
                        at = (c % 2) * S + t * P
                        last = pe.transpose(x_ps[c // 2][:, at:at + P], xin[:, t, c * P:(c + 1) * P], ident[:])
                    if c % 2:
                        last.then_inc(xt_mm, 1)

            def latent(batch):
                pe.wait_ge(xt_lo, batch.done(2, 2))
                for c in range(DC):
                    last = product(pe, x_ps[0][:, 0:S], [w[:, c, :] for w in wl], [w[:, c, :] for w in xt],
                                   c == 0, c == DC - 1)
                last.then_inc(k_mm, 1)

            def latent_rows(batch):
                for n in range(2):
                    for t in range(ST):
                        at = n * S + t * P
                        last = pe.transpose(x_ps[0][:, at:at + P], kt[n][:, t * P:(t + 1) * P].bitcast(F32), ident[:])
                last.then_inc(kn_mm, 1)

            def query(unit, h, head):
                pe.wait_ge(q_lo, unit.done(h - 2))
                for c in range(DC):
                    last = product(pe, q_ps[h % 2][:, 0:S], [w[:, c, head * L:(head + 1) * L] for w in wd],
                                   [w[:, c, :] for w in xt], c == 0, c == DC - 1)
                last.then_inc(q_mm, 1)

            def scores(unit, h):
                n = h % 2
                pe.wait_ge(s_masked, unit.done(h - 1))
                pe.wait_ge(q_lo, unit.done(h))
                product(pe, s_ps[:, 0:P], [w[:, 0:P] for w in q[n]], [w[:, 0:P] for w in kt], True, True)
                product(pe, s_ps[:, P:PK], [w[:, P:S] for w in q[n]], [w[:, :] for w in kt], True,
                        True).then_inc(s_mm, 1)

            def probs_t(unit, h):
                n = h % 2
                pe.wait_ge(pt_lo, unit.done(h - 1))
                pe.wait_ge(p_norm, unit.done(h))
                for c in range(3):
                    last = pe.transpose(t_ps[:, c * P:(c + 1) * P], pr[n][:, c * P:(c + 1) * P], ident[:])
                last.then_inc(t_mm, 1)

            def mixed(unit, h):
                pe.wait_ge(y_lo, unit.done(h - 1))
                pe.wait_ge(pt_lo, unit.done(h))
                product(pe, y_ps[:, 0:S], [w[:, 0, :] for w in kn], [w[:, 0:S] for w in pt], True, False)
                product(pe, y_ps[:, P:S], [w[:, 1, :] for w in kn], [w[:, S:PK] for w in pt], False,
                        True).then_inc(y_mm, 1)

            def projected(unit, h):
                pe.wait_ge(y_lo, unit.done(h))
                for t in range(ST):
                    last = product(pe, o_ps[t][:], [w[:, t * P:(t + 1) * P] for w in y], [w[:, h, :] for w in wp],
                                   h == 0, h == H - 1)
                last.then_inc(o_mm, 1)

            first, unit = Batch(Values(pe), 0), Unit(Values(pe))
            transposed_norm(first)
            latent(first)
            query(unit, 0, 0)
            query(unit, 1, 1)
            pe.wait_ge(k_lo, 1)
            scores(unit, 0)
            latent_rows(first)
            with pe.Fori(0, B) as i:
                val = Values(pe, i)
                unit, now, nxt = Unit(val), Batch(val, 0), Batch(val, 1)
                scores(unit, 1)
                probs_t(unit, 0)
                query(unit, 2, 2)
                pe.wait_ge(kn_ready, now.done(1, 1))
                mixed(unit, 0)
                for h in range(1, H - 2):
                    query(unit, h + 2, h + 2)
                    probs_t(unit, h)
                    scores(unit, h + 1)
                    if h == 1:
                        pe.wait_ge(out_ready, now.done(1, SEED))
                    projected(unit, h - 1)
                    mixed(unit, h)
                pe.wait_ge(q_lo, unit.done(H - 1))
                transposed_norm(nxt)
                probs_t(unit, H - 2)
                scores(unit, H - 1)
                projected(unit, H - 3)
                mixed(unit, H - 2)
                latent(nxt)
                probs_t(unit, H - 1)
                query(unit, H, 0)
                projected(unit, H - 2)
                mixed(unit, H - 1)
                pe.wait_ge(k_lo, nxt.done(1, 1))
                scores(unit, H)
                query(unit, H + 1, 1)
                projected(unit, H - 1)
                latent_rows(nxt)


def cross_attention(nc, x1, ctx_t, seg_cols, w_kvc, w_dq, uq_t, w_qr, uk_t, kr_uv, uv_t, w_o, trig, rot_cs, key_ids,
                    ident_in, x2):
    scale = 1.0 / math.sqrt(L + R)
    with ExitStack() as outer:
        def osb(name, shape, dt=F32):
            return outer.enter_context(nc.sbuf_tensor("b_" + name, shape, dt))

        def oparts(name, shape):
            return osb(name + "_hi", shape, F32R), osb(name + "_lo", shape, F32R)

        QT = QC - P

        def stacked(name):
            return osb(name + "_hi", [P, QCC, H * L], F32R), osb(name + "_lo", [P, H * L], F32R)

        wa = stacked("wa")
        wr = stacked("wr")
        wvo = oparts("wvo", [P, H, D])
        wdq = oparts("wdq", [P, DC, QCC * P])
        wkv = oparts("wkv", [P, DC, L])
        wkr = oparts("wkr", [P, 2, 2 * R])

        with ExitStack() as ctx:
            sems = []

            def sb(name, shape, dt=F32):
                return ctx.enter_context(nc.sbuf_tensor("bw_" + name, shape, dt))

            def sem(name):
                sems.append(ctx.enter_context(nc.semaphore("bw_" + name)))
                return sems[-1]

            r_uq, r_uk, r_uv = sb("uq", [P, H, QCC * P]), sb("uk", [P, H, L]), sb("uv", [P, H, L])
            r_o = [sb(f"o{n}", [P, 4, D]) for n in range(2)]
            r_dq, r_kv, r_kr = sb("dq", [P, DC, QC]), sb("kv", [P, DC, L]), sb("kr", [P, 2, 2 * R])
            r_qr = sb("qr", [P, QCC, H * R])
            fold_ps = [ctx.enter_context(nc.psum_tensor(f"bw_ps{n}", [P, 512], F32)) for n in range(4)]
            plain_in, up_in = sem("plain_in"), sem("up_in")
            o_in = [sem(f"o_in{n}") for n in range(2)]
            plain_hi, fold_mm, fold_hi, fold_lo = (
                sem("plain_hi"), sem("fold_mm"), sem("fold_hi"), sem("fold_lo"))

            ctx.callback(clear, nc, sems)
            block = ctx.enter_context(nc.Block())

            def chunks(w, cols):
                low = w[0][QT:P, 1, cols]
                return [(slice(0, P), w[0][:, 0, cols], w[0][:, 0, cols], w[1][:, cols]),
                        (slice(QT, P), w[0][:, 1, cols], low, low)]

            plain = [(raw[:], slice(0, P), w[0][:], w[0][:], w[1][:]) for raw, w in ((r_kv, wkv), (r_kr, wkr))]
            for src, dst in ((slice(0, QC), slice(0, QC)), (slice(P, QC), slice(QC, QCC * P))):
                hi, lo = wdq[0][:, :, dst], wdq[1][:, :, dst]
                plain.append((r_dq[:, :, src], slice(0, P), hi, hi, lo))

            def doubled(a, copy):
                return a.rearrange("p (h two r) -> p h two r", two=2, r=R)[:, :, copy, :]

            for c, (rows, hi, hi_lo, lo) in enumerate(chunks(wr, slice(0, H * L))):
                for copy in range(2):
                    plain.append((r_qr[:, c, :].rearrange("p (h r) -> p h r", r=R), rows,
                                  *[doubled(a, copy) for a in (hi, hi_lo, lo)]))
            folded = []
            for g in range(H // 4):
                for part in chunks(wa, slice(g * 4 * L, (g + 1) * 4 * L)):
                    folded.append((fold_ps[len(folded) % 4][:], *part))
            for h in range(H):
                folded.append((fold_ps[len(folded) % 4][:], slice(0, P), wvo[0][:, h, :], wvo[0][:, h, :],
                               wvo[1][:, h, :]))

            @block.sync
            def _(sp):
                sp.dma_start(r_uq[:, :, 0:QC], uq_t.rearrange("(h p) n -> p h n", p=P)).then_inc(up_in, 16)
                sp.dma_start(r_uq[:, :, QC:], uq_t[:, P:QC].rearrange("(h p) n -> p h n", p=P)).then_inc(up_in, 16)
                sp.dma_start(r_uk[:], uk_t.rearrange("(h p) n -> p h n", p=P)).then_inc(up_in, 16)
                sp.dma_start(r_kv[:], w_kvc.rearrange("(c p) n -> p c n", p=P)).then_inc(plain_in, 16)
                sp.dma_start(r_kr[:], kr_uv).then_inc(plain_in, 16)
                sp.dma_start(r_dq[:], w_dq.rearrange("(c p) n -> p c n", p=P)).then_inc(plain_in, 16)
                sp.dma_start(r_qr[:, 0, :], w_qr[0:P, :]).then_inc(plain_in, 16)
                sp.dma_start(r_qr[0:QT, 1, :], w_qr[P:QC, :]).then_inc(plain_in, 16)
                sp.dma_start(r_qr[QT:P, 1, :], w_qr[P:QC, :]).then_inc(plain_in, 16)
                sp.dma_start(r_uv[:], uv_t.rearrange("(h p) n -> p h n", p=P)).then_inc(up_in, 16)
                for g in range(H // 4):
                    if g >= 2:
                        sp.wait_ge(fold_mm, 8 + 4 * (g - 1))
                    sp.dma_start(r_o[g % 2][:], w_o[g * 4 * L:(g + 1) * 4 * L, :].rearrange(
                        "(h p) n -> p h n", p=P)).then_inc(o_in[g % 2], 16)

            @block.scalar
            def _(act):
                act.wait_ge(plain_in, 96)
                for raw, _, hi, _, _ in plain:
                    act.activation(hi, raw, ACT.Copy).then_inc(plain_hi, 1)
                for n, (bank, _, hi, _, _) in enumerate(folded):
                    act.wait_ge(fold_mm, n + 1)
                    act.activation(hi, bank, ACT.Copy).then_inc(fold_hi, 1)

            @block.vector
            def _(v):
                v.wait_ge(plain_in, 96)
                for n, (raw, rows, _, hi, lo) in enumerate(plain):
                    v.wait_ge(plain_hi, n + 1)
                    v.tensor_tensor(lo, raw[rows], hi.bitcast(F32), ALU.subtract)
                for n, (bank, rows, _, hi, lo) in enumerate(folded):
                    v.wait_ge(fold_hi, n + 1)
                    v.tensor_tensor(lo, bank[rows], hi.bitcast(F32), ALU.subtract).then_inc(fold_lo, 1)

            @block.tensor
            def _(pe):
                pe.wait_ge(up_in, 64)
                n = 0
                for g in range(H // 4):
                    for c in range(QCC):
                        if n >= 4:
                            pe.wait_ge(fold_lo, n - 3)
                        for k in range(4):
                            last = pe.matmul(fold_ps[n % 4][:, k * L:(k + 1) * L],
                                             r_uq[:, 4 * g + k, c * P:(c + 1) * P], r_uk[:, 4 * g + k, :],
                                             start=True, stop=True)
                        last.then_inc(fold_mm, 1)
                        n += 1
                for h in range(H):
                    pe.wait_ge(fold_lo, n - 3)
                    if h % 4 == 0:
                        pe.wait_ge(o_in[(h // 4) % 2], 16 * (h // 8 + 1))
                    pe.matmul(fold_ps[n % 4][:], r_uv[:, h, :], r_o[(h // 4) % 2][:, h % 4, :], start=True,
                              stop=True).then_inc(fold_mm, 1)
                    n += 1

        with ExitStack() as ctx:
            sems = []

            def sb(name, shape, dt=F32):
                return ctx.enter_context(nc.sbuf_tensor("b_" + name, shape, dt))

            def pb(name, shape):
                return ctx.enter_context(nc.psum_tensor("b_" + name, shape, F32))

            def sem(name):
                sems.append(ctx.enter_context(nc.semaphore("b_" + name)))
                return sems[-1]

            def parts(name, shape):
                return sb(name + "_hi", shape, F32R), sb(name + "_lo", shape, F32R)

            ident, qtrig = sb("ident", [P, P]), sb("qtrig", [P, S])
            kcos, ksin, ids = sb("kcos", [P, S]), sb("ksin", [P, S]), sb("ids", [P, S])
            segi = sb("segi", [P, B * ST], I32)
            segf, segmid = sb("segf", [P, B * ST]), sb("segmid", [P, B * ST])
            seg_b = sb("seg_b", [P, ST])
            mask, mask_next = sb("mask", [P, ST, S], BF16), sb("mask_next", [P, ST, S], BF16)
            xin, res, ctr = sb("xin", [P, ST, D]), sb("res", [P, ST, D]), sb("ctr", [P, DC, S])
            stats, small = sb("stats", [P, ST, 8]), sb("small", [P, 4, ST])
            xt, ct, qc = parts("xt", [P, DC, S]), parts("ct", [P, DC, S]), parts("qc", [P, QCC, S])
            kt, kr, kn = parts("kt", [P, S]), parts("kr", [P, S]), parts("kn", [P, ST, L])
            q = [parts(f"q{n}", [P, S]) for n in range(2)]
            qr = [parts(f"qr{n}", [P, S]) for n in range(2)]
            tq = [sb(f"tq{n}", [P, S]) for n in range(2)]
            pr = [sb(f"pr{n}", [P, ST, S]) for n in range(2)]
            kr1, kr2 = pr[0][:, 0, :], pr[0][:, 1, :]
            top = [sb(f"top{n}", [P, ST]) for n in range(2)]
            rsum = [sb(f"rsum{n}", [P, ST]) for n in range(2)]
            rinv = [sb(f"rinv{n}", [P, ST]) for n in range(2)]
            pt, z = parts("pt", [P, ST, S]), parts("z", [P, S])

            qa_ps, qr_ps, s_ps, t_ps, z_ps, x_ps = (pb(n, [P, 512]) for n in ("qa_ps", "qr_ps", "s_ps", "t_ps", "z_ps",
                                                                              "x_ps"))
            o_ps = [pb(f"o_ps{n}", [P, D]) for n in range(ST)]

            MASK_AT, CONTEXT_AT = 1, H // 2

            const_in, seg_float, seg_ready = sem("const_in"), sem("seg_float"), sem("seg_ready")
            x_in, res_in, ctx_in, stored = sem("x_in"), sem("res_in"), sem("ctx_in"), sem("stored")
            ct_hi, ct_lo = sem("ct_hi"), sem("ct_lo")
            seg_copied, distance, squared, mask_made, mask_moved = (
                sem("seg_copied"), sem("distance"), sem("squared"), sem("mask_made"), sem("mask_moved"))
            ln_chain, xn_ready = sem("ln_chain"), sem("xn_ready")
            xt_mm, xt_hi, xt_lo = sem("xt_mm"), sem("xt_hi"), sem("xt_lo")
            qc_mm, qc_hi, qc_lo = sem("qc_mm"), sem("qc_hi"), sem("qc_lo")
            k_mm, k_hi, k_lo = sem("k_mm"), sem("k_hi"), sem("k_lo")
            kr_mm, kr_prod, kr_sum, kr_hi, kr_lo = (sem("kr_mm"), sem("kr_prod"), sem("kr_sum"), sem("kr_hi"),
                                                    sem("kr_lo"))
            kn_mm, kn_ready = sem("kn_mm"), sem("kn_ready")
            out_ready = sem("out_ready")
            sp_step, v_step, g_step = sem("sp_step"), sem("v_step"), sem("g_step")
            qa_mm, qa_hi, qa_lo = sem("qa_mm"), sem("qa_hi"), sem("qa_lo")
            qr_mm, qr_rot, qr_hi, qr_lo = sem("qr_mm"), sem("qr_rot"), sem("qr_hi"), sem("qr_lo")
            s_mm, s_masked, p_exp, p_inv, p_norm = (sem("s_mm"), sem("s_masked"), sem("p_exp"), sem("p_inv"),
                                                    sem("p_norm"))
            t_mm, pt_hi, pt_lo = sem("t_mm"), sem("pt_hi"), sem("pt_lo")
            z_mm, z_hi, z_lo, o_mm = sem("z_mm"), sem("z_hi"), sem("z_lo"), sem("o_mm")

            ctx.callback(clear, nc, sems)
            block = ctx.enter_context(nc.Block())

            def rows_of(array, b):
                return array[b].rearrange("o (t p) c -> p (o t) c", p=P)

            def context_of(b):
                return ctx_t[b].rearrange("o (c p) t -> p (o c) t", p=P)

            @block.sync
            def _(sp):
                sp.dma_start(xin[:], rows_of(x1, slice(0, 1))).then_inc(x_in, 16)
                sp.dma_start(ctr[:], context_of(slice(0, 1))).then_inc(ctx_in, 16)
                sp.dma_start(segi[:], seg_cols).then_inc(const_in, 16)
                for dst, src in ((ident, ident_in), (qtrig, trig), (kcos, rot_cs[0]), (ksin, rot_cs[1]), (ids, key_ids)):
                    sp.dma_start(dst[:], src).then_inc(const_in, 16)
                with sp.Fori(0, B) as i:
                    val = Values(sp, i)
                    now = Batch(val, 0)
                    nxt = sp.snap((i + 1) % B)
                    one, out_done, out_stored = now.done(1, 1), now.done(1, 1 + SEED), now.done(16, 16)
                    hold(sp, xt_mm, now.done(2, 2), sp_step)
                    sp.dma_start(xin[:], rows_of(x1, bass.ds(nxt, 1))).then_inc(x_in, 16)
                    hold(sp, ct_lo, one, sp_step)
                    sp.dma_start(ctr[:], context_of(bass.ds(nxt, 1))).then_inc(ctx_in, 16)
                    sp.dma_start(res[:], rows_of(x1, bass.ds(i, 1))).then_inc(res_in, 16)
                    hold(sp, out_ready, out_done, sp_step)
                    sp.dma_start(rows_of(x2, bass.ds(i, 1)), res[:]).then_inc(stored, 16)
                    hold(sp, stored, out_stored, sp_step)

            @block.scalar
            def _(act):
                act.wait_ge(const_in, 96)
                for s in (qa_hi, qr_hi, p_exp, pt_hi, z_hi):
                    act.sem_inc(s, SEED)

                def context(batch):
                    act.wait_ge(ctx_in, batch.done(16, 16))
                    act.activation(ct[0][:], ctr[:], ACT.Copy).then_inc(ct_hi, 1)

                def norm_t(batch, n):
                    act.wait_ge(xt_mm, batch.done(2, n + 1))
                    act.activation(xt[0][:, 2 * n:2 * n + 2, :].rearrange("p c t -> p (c t)"), x_ps[:],
                                   ACT.Copy).then_inc(xt_hi, 1)

                def latent(batch):
                    act.wait_ge(k_mm, batch.done(1, 1))
                    act.activation(kt[0][:], qa_ps[:, 0:S], ACT.Copy).then_inc(k_hi, 1)

                def query_latent(batch):
                    act.wait_ge(qc_mm, batch.done(1, 1))
                    act.activation(qc[0][:].rearrange("p c t -> p (c t)"), qr_ps[:], ACT.Copy).then_inc(qc_hi, 1)

                def rotated_keys(batch):
                    act.wait_ge(kr_sum, batch.done(1, 1))
                    act.activation(kr[0][:], kr1, ACT.Copy).then_inc(kr_hi, 1)

                def latent_rows(batch):
                    act.wait_ge(kn_mm, batch.done(1, 1))
                    for n in range(2):
                        last = act.activation(kn[n][:].rearrange("p t l -> p (t l)"), x_ps[:, n * S:(n + 1) * S],
                                              ACT.Copy)
                    last.then_inc(kn_ready, 1)

                def query(unit, h):
                    act.wait_ge(qr_rot, unit.done(h))
                    act.activation(qr[h % 2][0][:], tq[h % 2][:], ACT.Copy).then_inc(qr_hi, 1)
                    act.wait_ge(qa_mm, unit.done(h))
                    act.activation(q[h % 2][0][:], qa_ps[:, 0:S], ACT.Copy).then_inc(qa_hi, 1)

                def exps(unit, h):
                    act.wait_ge(s_masked, unit.done(h))
                    n = h % 2
                    for t in range(ST):
                        last = act.activation(pr[n][:, t, :], pr[n][:, t, :], ACT.Exp, bias=top[n][:, t:t + 1],
                                              scale=-1.0, accum_out=rsum[n][:, t:t + 1])
                    last.then_inc(p_exp, 1)

                def probs_t(unit, h):
                    act.wait_ge(t_mm, unit.done(h))
                    act.activation(pt[0][:].rearrange("p k t -> p (k t)"), t_ps[:], ACT.Copy).then_inc(pt_hi, 1)

                def mixed(unit, h):
                    act.wait_ge(z_mm, unit.done(h))
                    act.activation(z[0][:], z_ps[:, 0:S], ACT.Copy).then_inc(z_hi, 1)

                first, unit = Batch(Values(act), 0), Unit(Values(act))
                context(first)
                norm_t(first, 0)
                norm_t(first, 1)
                latent(first)
                query_latent(first)
                rotated_keys(first)
                query(unit, 0)
                query(unit, 1)
                exps(unit, 0)
                latent_rows(first)
                with act.Fori(0, B) as i:
                    val = Values(act, i)
                    unit, nxt = Unit(val), Batch(val, 1)
                    for h in range(H - 2):
                        probs_t(unit, h)
                        exps(unit, h + 1)
                        query(unit, h + 2)
                        mixed(unit, h)
                        if h == CONTEXT_AT:
                            context(nxt)
                    norm_t(nxt, 0)
                    act.wait_ge(s_mm, unit.done(H - 1))
                    latent(nxt)
                    probs_t(unit, H - 2)
                    norm_t(nxt, 1)
                    exps(unit, H - 1)
                    query_latent(nxt)
                    mixed(unit, H - 2)
                    probs_t(unit, H - 1)
                    query(unit, H)
                    rotated_keys(nxt)
                    mixed(unit, H - 1)
                    query(unit, H + 1)
                    exps(unit, H)
                    latent_rows(nxt)

            @block.vector
            def _(v):
                v.wait_ge(const_in, 96)
                for s in (qa_lo, qr_rot, s_masked, p_inv, p_norm, pt_lo, z_lo, out_ready, ln_chain):
                    v.sem_inc(s, SEED)
                v.tensor_copy(segf[:], segi[:]).then_inc(seg_float, 1)
                v.wait_ge(seg_float, 1)
                v.tensor_scalar(segmid[:], segf[:], -float(LOOKBACK // 2), None, ALU.add).then_inc(seg_ready, 1)

                def norm(batch):
                    v.wait_ge(x_in, batch.done(16, 16))
                    return LayerNorm(v, xin, stats, small, ln_chain, lambda k: batch.done(LN_LINKS, k + SEED), v_step)

                def norm_t(batch, n):
                    v.wait_ge(xt_hi, batch.done(2, n + 1))
                    half = slice(2 * n, 2 * n + 2)
                    v.tensor_tensor(xt[1][:, half, :].rearrange("p c t -> p (c t)"), x_ps[:],
                                    xt[0][:, half, :].rearrange("p c t -> p (c t)").bitcast(F32),
                                    ALU.subtract).then_inc(xt_lo, 1)

                def latent(batch):
                    v.wait_ge(k_hi, batch.done(1, 1))
                    v.tensor_tensor(kt[1][:], qa_ps[:, 0:S], kt[0][:].bitcast(F32), ALU.subtract).then_inc(k_lo, 1)

                def query_latent(batch):
                    v.wait_ge(qc_hi, batch.done(1, 1))
                    v.tensor_tensor(qc[1][:].rearrange("p c t -> p (c t)"), qr_ps[:],
                                    qc[0][:].rearrange("p c t -> p (c t)").bitcast(F32),
                                    ALU.subtract).then_inc(qc_lo, 1)

                def rotated_keys(batch):
                    v.wait_ge(kr_mm, batch.done(1, 1))
                    v.tensor_tensor(kr1, x_ps[:, 0:S], kcos[:], ALU.mult)
                    v.tensor_tensor(kr2, x_ps[:, S:], ksin[:], ALU.mult).then_inc(kr_prod, 1)
                    v.wait_ge(kr_prod, batch.done(1, 1))
                    v.tensor_tensor(kr1, kr1, kr2, ALU.add).then_inc(kr_sum, 1)

                def rotated_keys_lo(batch):
                    v.wait_ge(kr_hi, batch.done(1, 1))
                    v.tensor_tensor(kr[1][:], kr1, kr[0][:].bitcast(F32), ALU.subtract).then_inc(kr_lo, 1)

                def new_mask(batch):
                    v.wait_ge(mask_made, batch.done(1, 1))
                    v.tensor_copy(mask[:], mask_next[:]).then_inc(mask_moved, 1)

                def rotated(unit, h):
                    v.wait_ge(qr_mm, unit.done(h))
                    v.tensor_tensor(tq[h % 2][:], qr_ps[:, 0:S], qtrig[:], ALU.mult).then_inc(qr_rot, 1)

                def query(unit, h):
                    v.wait_ge(qa_hi, unit.done(h))
                    v.tensor_tensor(q[h % 2][1][:], qa_ps[:, 0:S], q[h % 2][0][:].bitcast(F32),
                                    ALU.subtract).then_inc(qa_lo, 1)

                def masked(unit, h):
                    n = h % 2
                    hold(v, s_mm, unit.done(h), v_step)
                    for t in range(ST):
                        last = v.tensor_tensor_reduce(out=pr[n][:, t, :], in0=s_ps[:, t * S:(t + 1) * S],
                                                      in1=mask[:, t, :], scale=-scale, scalar=3e38, op0=ALU.add,
                                                      op1=ALU.min, accum_out=top[n][:, t:t + 1])
                    last.then_inc(s_masked, 1)

                def normalize(unit, h):
                    n = h % 2
                    v.wait_ge(p_exp, unit.done(h))
                    v.reciprocal(rinv[n][:], rsum[n][:]).then_inc(p_inv, 1)
                    v.wait_ge(p_inv, unit.done(h))
                    for t in range(ST):
                        last = v.tensor_scalar(pr[n][:, t, :], pr[n][:, t, :], rinv[n][:, t:t + 1], None, ALU.mult)
                    last.then_inc(p_norm, 1)

                def probs_t(unit, h):
                    v.wait_ge(pt_hi, unit.done(h))
                    v.tensor_tensor(pt[1][:].rearrange("p k t -> p (k t)"), t_ps[:],
                                    pt[0][:].rearrange("p k t -> p (k t)").bitcast(F32),
                                    ALU.subtract).then_inc(pt_lo, 1)

                def mixed(unit, h):
                    v.wait_ge(z_hi, unit.done(h))
                    v.tensor_tensor(z[1][:], z_ps[:, 0:S], z[0][:].bitcast(F32), ALU.subtract).then_inc(z_lo, 1)

                first, unit = Batch(Values(v), 0), Unit(Values(v))
                norm(first).whole().then_inc(xn_ready, 1)
                norm_t(first, 0)
                norm_t(first, 1)
                latent(first)
                query_latent(first)
                rotated_keys(first)
                rotated_keys_lo(first)
                rotated(unit, 0)
                query(unit, 0)
                rotated(unit, 1)
                query(unit, 1)
                new_mask(first)
                v.wait_ge(mask_moved, 1)
                masked(unit, 0)
                normalize(unit, 0)
                with v.Fori(0, B) as i:
                    val = Values(v, i)
                    unit, now, nxt = Unit(val), Batch(val, 0), Batch(val, 1)
                    for h in range(H - 2):
                        masked(unit, h + 1)
                        rotated(unit, h + 2)
                        probs_t(unit, h)
                        query(unit, h + 2)
                        normalize(unit, h + 1)
                        if h == NORM_AT:
                            next_norm = norm(nxt)
                        if 0 <= h - NORM_AT < LayerNorm.PIECES:
                            last = next_norm.piece(h - NORM_AT)
                        mixed(unit, h)
                    last.then_inc(xn_ready, 1)
                    norm_t(nxt, 0)
                    masked(unit, H - 1)
                    latent(nxt)
                    probs_t(unit, H - 2)
                    norm_t(nxt, 1)
                    normalize(unit, H - 1)
                    query_latent(nxt)
                    mixed(unit, H - 2)
                    probs_t(unit, H - 1)
                    rotated(unit, H)
                    rotated_keys(nxt)
                    query(unit, H)
                    rotated_keys_lo(nxt)
                    new_mask(nxt)
                    mixed(unit, H - 1)
                    v.wait_ge(mask_moved, nxt.done(1, 1))
                    masked(unit, H)
                    rotated(unit, H + 1)
                    query(unit, H + 1)
                    normalize(unit, H)
                    v.wait_ge(res_in, now.done(16, 16))
                    v.wait_ge(o_mm, unit.done(H - 1))
                    for t in range(ST):
                        last = v.tensor_tensor(res[:, t, :], o_ps[t][:], res[:, t, :], ALU.add)
                    last.then_inc(out_ready, 1)

            @block.gpsimd
            def _(g):
                g.wait_ge(const_in, 96)
                g.sem_inc(qr_lo, SEED)
                g.wait_ge(seg_ready, 1)

                def context(batch, c):
                    if c == 0:
                        g.wait_ge(ct_hi, batch.done(1, 1))
                    last = g.tensor_tensor(ct[1][:, c, :], ctr[:, c, :], ct[0][:, c, :].bitcast(F32), ALU.subtract)
                    if c == DC - 1:
                        last.then_inc(ct_lo, 1)

                def make_mask(batch, n, col=None, moved=None):
                    stage, t = n // ST, n % ST
                    part = mask_next[:, t, :]
                    if n == 0:
                        g.tensor_copy(seg_b[:], segmid[:, col]).then_inc(seg_copied, 1)
                        if moved is not None:
                            hold(g, mask_moved, moved, g_step)
                        hold(g, seg_copied, batch.done(1, 1), g_step)
                    if stage == 0:
                        g.tensor_scalar(part, ids[:], seg_b[:, t:t + 1], None, ALU.subtract).then_inc(distance, 1)
                    elif stage == 1:
                        g.wait_ge(distance, batch.done(ST, t + 1))
                        g.tensor_tensor(part, part, part, ALU.mult).then_inc(squared, 1)
                    else:
                        hold(g, squared, batch.done(ST, t + 1), g_step)
                        last = g.tensor_scalar(part, part, float(LOOKBACK // 2) ** 2, MASKED, ALU.is_gt, ALU.mult)
                        if t == ST - 1:
                            last.then_inc(mask_made, 1)

                def query(unit, h):
                    g.wait_ge(qr_hi, unit.done(h))
                    g.tensor_tensor(qr[h % 2][1][:], tq[h % 2][:], qr[h % 2][0][:].bitcast(F32),
                                    ALU.subtract).then_inc(qr_lo, 1)

                first, unit = Batch(Values(g), 0), Unit(Values(g))
                for c in range(DC):
                    context(first, c)
                for n in range(3 * ST):
                    make_mask(first, n, slice(0, ST))
                query(unit, 0)
                query(unit, 1)
                with g.Fori(0, B) as i:
                    val = Values(g, i)
                    unit, now, nxt = Unit(val), Batch(val, 0), Batch(val, 1)
                    col = g.snap(((i + 1) % B) * ST)
                    for h in range(H):
                        query(unit, h + 2)
                        if 0 <= h - MASK_AT < 3 * ST:
                            make_mask(nxt, h - MASK_AT, bass.ds(col, ST), now.done(1, 1))
                        if 0 <= h - CONTEXT_AT < DC:
                            context(nxt, h - CONTEXT_AT)

            @block.tensor
            def _(pe):
                pe.wait_ge(const_in, 96)
                for s in (qa_mm, qr_mm, s_mm, t_mm, z_mm, o_mm):
                    pe.sem_inc(s, SEED)

                def norm_t(batch, n):
                    pe.wait_ge(xn_ready, batch.done(1, 1))
                    if n:
                        pe.wait_ge(xt_lo, batch.done(2, 1))
                    for c in range(2):
                        for t in range(ST):
                            at = c * S + t * P
                            last = pe.transpose(x_ps[:, at:at + P], xin[:, t, (2 * n + c) * P:(2 * n + c + 1) * P],
                                                ident[:])
                    last.then_inc(xt_mm, 1)

                def latent(batch, unit, h):
                    pe.wait_ge(ct_lo, batch.done(1, 1))
                    pe.wait_ge(qa_lo, unit.done(h - 1))
                    for c in range(DC):
                        last = product(pe, qa_ps[:, 0:S], [w[:, c, :] for w in wkv], [w[:, c, :] for w in ct],
                                       c == 0, c == DC - 1)
                    last.then_inc(k_mm, 1)

                def query_latent(batch, unit, h):
                    pe.wait_ge(qr_rot, unit.done(h - 1))
                    for n in range(QCC):
                        for c in range(DC):
                            if n == 0 and c % 2 == 0:
                                pe.wait_ge(xt_lo, batch.done(2, 1 + c // 2))
                            last = product(pe, qr_ps[:, n * S:(n + 1) * S], [w[:, c, n * P:(n + 1) * P] for w in wdq],
                                           [w[:, c, :] for w in xt], c == 0, c == DC - 1)
                    last.then_inc(qc_mm, 1)

                def rotated_keys(batch):
                    pe.wait_ge(k_lo, batch.done(1, 1))
                    pe.wait_ge(xt_lo, batch.done(2, 2))
                    for n in range(2):
                        last = product(pe, x_ps[:, n * S:(n + 1) * S], [w[:, n, :] for w in wkr], [w[:] for w in kt],
                                       True, True)
                    last.then_inc(kr_mm, 1)

                def latent_rows(batch):
                    pe.wait_ge(kr_sum, batch.done(1, 1))
                    for n in range(2):
                        for t in range(ST):
                            at = n * S + t * P
                            last = pe.transpose(x_ps[:, at:at + P], kt[n][:, t * P:(t + 1) * P].bitcast(F32), ident[:])
                    last.then_inc(kn_mm, 1)

                def query(unit, h, head):
                    for bank, free, w, done in ((qr_ps, qr_rot, wr, qr_mm), (qa_ps, qa_lo, wa, qa_mm)):
                        pe.wait_ge(free, unit.done(h - 1))
                        cols = slice(head * L, (head + 1) * L)
                        product(pe, bank[:, 0:S], (w[0][:, 0, cols], w[1][:, cols]), [a[:, 0, :] for a in qc], True,
                                False)
                        pe.matmul(bank[:, 0:S], w[0][:, 1, cols], qc[0][:, 1, :], start=False, stop=False)
                        pe.matmul(bank[:, 0:S], w[0][0:QT, 1, cols], qc[1][0:QT, 1, :], start=False,
                                  stop=True).then_inc(done, 1)

                def scores(unit, h):
                    n = h % 2
                    pe.wait_ge(s_masked, unit.done(h - 1))
                    pe.wait_ge(qa_lo, unit.done(h))
                    pe.wait_ge(qr_lo, unit.done(h))
                    for t in range(ST):
                        rows = slice(t * P, (t + 1) * P)
                        product(pe, s_ps[:, t * S:(t + 1) * S], [w[:, rows] for w in q[n]], [w[:] for w in kt], True,
                                False)
                        last = product(pe, s_ps[:, t * S:(t + 1) * S], [w[:, rows] for w in qr[n]], [w[:] for w in kr],
                                       False, True)
                    last.then_inc(s_mm, 1)

                def probs_t(unit, h):
                    n = h % 2
                    pe.wait_ge(pt_lo, unit.done(h - 1))
                    pe.wait_ge(p_norm, unit.done(h))
                    for k in range(ST):
                        for t in range(ST):
                            at = k * S + t * P
                            last = pe.transpose(t_ps[:, at:at + P], pr[n][:, t, k * P:(k + 1) * P], ident[:])
                    last.then_inc(t_mm, 1)

                def mixed(unit, h):
                    pe.wait_ge(z_lo, unit.done(h - 1))
                    pe.wait_ge(pt_lo, unit.done(h))
                    for k in range(ST):
                        last = product(pe, z_ps[:, 0:S], [w[:, k, :] for w in kn], [w[:, k, :] for w in pt], k == 0,
                                       k == ST - 1)
                    last.then_inc(z_mm, 1)

                def projected(unit, h):
                    pe.wait_ge(z_lo, unit.done(h))
                    for t in range(ST):
                        last = product(pe, o_ps[t][:], [w[:, t * P:(t + 1) * P] for w in z], [w[:, h, :] for w in wvo],
                                       h == 0, h == H - 1)
                    last.then_inc(o_mm, 1)

                first, unit = Batch(Values(pe), 0), Unit(Values(pe))
                norm_t(first, 0)
                norm_t(first, 1)
                latent(first, unit, 0)
                query_latent(first, unit, 0)
                rotated_keys(first)
                pe.wait_ge(qc_lo, 1)
                query(unit, 0, 0)
                query(unit, 1, 1)
                pe.wait_ge(kr_lo, 1)
                scores(unit, 0)
                latent_rows(first)
                with pe.Fori(0, B) as i:
                    val = Values(pe, i)
                    unit, now, nxt = Unit(val), Batch(val, 0), Batch(val, 1)
                    for h in range(H - 2):
                        scores(unit, h + 1)
                        probs_t(unit, h)
                        query(unit, h + 2, h + 2)
                        if h == 0:
                            pe.wait_ge(kn_ready, now.done(1, 1))
                        if h == 1:
                            pe.wait_ge(out_ready, now.done(1, SEED))
                        if h >= 1:
                            projected(unit, h - 1)
                        mixed(unit, h)
                    norm_t(nxt, 0)
                    latent(nxt, unit, H)
                    scores(unit, H - 1)
                    probs_t(unit, H - 2)
                    norm_t(nxt, 1)
                    projected(unit, H - 3)
                    query_latent(nxt, unit, H)
                    mixed(unit, H - 2)
                    probs_t(unit, H - 1)
                    rotated_keys(nxt)
                    pe.wait_ge(qc_lo, nxt.done(1, 1))
                    query(unit, H, 0)
                    projected(unit, H - 2)
                    mixed(unit, H - 1)
                    pe.wait_ge(kr_lo, nxt.done(1, 1))
                    scores(unit, H)
                    query(unit, H + 1, 1)
                    projected(unit, H - 1)
                    latent_rows(nxt)


def shared_expert(nc, x2, gate_w, bias, w1, w2, ident_in, xn3, logits, acc_dram, xg, yg):
    with ExitStack() as ctx:
        sems = []

        def sb(name, shape, dt=F32):
            return ctx.enter_context(nc.sbuf_tensor("s_" + name, shape, dt))

        def pb(name, shape):
            return ctx.enter_context(nc.psum_tensor("s_ps_" + name, shape, F32))

        def sem(name):
            sems.append(ctx.enter_context(nc.semaphore("s_" + name)))
            return sems[-1]

        def parts(name, shape):
            return sb(name + "_hi", shape, F32R), sb(name + "_lo", shape, F32R)

        r1, r2, rg = sb("r1", [P, DC, 2 * F]), sb("r2", [P, FC, D]), sb("rg", [P, DC, EP])
        w1p, w2p, wg = parts("w1", [P, DC, 2 * F]), parts("w2", [P, FC, D]), parts("wg", [P, DC, EP])
        ident, zeros, eb = sb("ident", [P, P]), sb("zeros", [P, CT * D]), sb("eb", [P, ST, EP])
        xin, xn, res = sb("xin", [P, ST, D]), sb("xn", [P, ST, D]), sb("res", [P, ST, D])
        stats, small = sb("stats", [P, ST, 8]), sb("small", [P, 4, ST])
        xt = parts("xt", [P, DC, S])
        sil = [sb(f"sil{n}", [P, S]) for n in range(FC)]
        gate = [sb(f"gate{n}", [P, S]) for n in range(FC)]
        gt = [parts(f"gt{n}", [P, S]) for n in range(FC)]
        up_ps = [pb(f"up{n}", [P, 512]) for n in range(FC)]
        gate_ps = [pb(f"gt{n}", [P, 512]) for n in range(FC)]
        x_ps = [pb(f"x{n}", [P, 512]) for n in range(2)]
        y_ps = [pb(f"y{n}", [P, D]) for n in range(ST)]

        w_in, w_hi, w_lo, const_in, zeroed, cleared = (sem("w_in"), sem("w_hi"), sem("w_lo"), sem("const_in"),
                                                       sem("zeroed"), sem("cleared"))
        x_in, res_in, stored = sem("x_in"), sem("res_in"), sem("stored")
        ln_chain, xn_ready, xn_kept = sem("ln_chain"), sem("xn_ready"), sem("xn_kept")
        xt_mm, xt_hi, xt_lo = sem("xt_mm"), sem("xt_hi"), sem("xt_lo")
        logit_mm, logit_out = sem("logit_mm"), sem("logit_out")
        gate_mm, up_mm = sem("gate_mm"), sem("up_mm")
        silu, gated, gt_hi, gt_lo = sem("silu"), sem("gated"), sem("gt_hi"), sem("gt_lo")
        y_mm, acc_ready = sem("y_mm"), sem("acc_ready")
        sp_step, v_step, g_step = sem("sp_step"), sem("v_step"), sem("g_step")

        weights = [(r1, w1p), (r2, w2p), (rg, wg)]
        ctx.callback(clear, nc, sems)
        block = ctx.enter_context(nc.Block())

        def rows_of(array, b):
            return array[b].rearrange("o (t p) c -> p (o t) c", p=P)

        @block.sync
        def _(sp):
            sp.dma_start(xin[:], rows_of(x2, slice(0, 1))).then_inc(x_in, 16)
            sp.dma_start(ident[:], ident_in).then_inc(const_in, 16)
            for t in range(ST):
                sp.dma_start(eb[:, t, :], bias.to_broadcast([P, EP])).then_inc(const_in, 16)
            sp.dma_start(r1[:], w1.rearrange("(c p) n -> p c n", p=P)).then_inc(w_in, 16)
            sp.dma_start(r2[:], w2.rearrange("(c p) n -> p c n", p=P)).then_inc(w_in, 16)
            sp.dma_start(rg[:], gate_w.rearrange("(c p) n -> p c n", p=P)).then_inc(w_in, 16)
            sp.wait_ge(xn_ready, 1)
            sp.dma_start(xin[:], rows_of(x2, slice(1, 2))).then_inc(x_in, 16)
            sp.wait_ge(zeroed, 1)
            for e in range(E):
                sp.dma_start(xg[e * SLOTS:(e + 1) * SLOTS, :].rearrange("(p t) d -> p (t d)", t=CT),
                             zeros[:]).then_inc(cleared, 16)
            sp.dma_start(yg[ROWS:ROWS + P, :], zeros[:, 0:D]).then_inc(cleared, 16)
            with sp.Fori(0, B) as i:
                val = Values(sp, i)
                now = Batch(val, 0)
                after = sp.snap((i + 2) % B)
                normed, out_done, out_stored = now.done(1, 2), now.done(1, 1 + SEED), now.done(16, 16)
                sp.dma_start(res[:], rows_of(x2, bass.ds(i, 1))).then_inc(res_in, 16)
                hold(sp, xn_ready, normed, sp_step)
                sp.dma_start(xin[:], rows_of(x2, bass.ds(after, 1))).then_inc(x_in, 16)
                hold(sp, acc_ready, out_done, sp_step)
                sp.dma_start(rows_of(acc_dram, bass.ds(i, 1)), res[:]).then_inc(stored, 16)
                hold(sp, stored, out_stored, sp_step)
            sp.wait_ge(cleared, 16 * (E + 1))

        @block.scalar
        def _(act):
            act.wait_ge(w_in, 48)
            for raw, w in weights:
                act.activation(w[0][:], raw[:], ACT.Copy).then_inc(w_hi, 1)

            def norm_t(batch):
                for n in range(2):
                    act.wait_ge(xt_mm, batch.done(1, 1))
                    act.activation(xt[0][:, 2 * n:2 * n + 2, :].rearrange("p c t -> p (c t)"), x_ps[n][:],
                                   ACT.Copy).then_inc(xt_hi, 1)

            norm_t(Batch(Values(act), 0))
            with act.Fori(0, B) as i:
                val = Values(act, i)
                now, nxt = Batch(val, 0), Batch(val, 1)
                for n in range(FC):
                    act.wait_ge(gate_mm, now.done(FC, n + 1))
                    act.activation(sil[n][:], gate_ps[n][:, 0:S], ACT.Silu).then_inc(silu, 1)
                    act.wait_ge(gated, now.done(FC, n + 1))
                    act.activation(gt[n][0][:], gate[n][:], ACT.Copy).then_inc(gt_hi, 1)
                norm_t(nxt)

        @block.vector
        def _(v):
            v.memset(zeros[:], 0.0).then_inc(zeroed, 1)
            for n, (raw, w) in enumerate(weights):
                v.wait_ge(w_hi, n + 1)
                v.tensor_tensor(w[1][:], raw[:], w[0][:].bitcast(F32), ALU.subtract).then_inc(w_lo, 1)
            v.wait_ge(const_in, 16 * (1 + ST))
            for s in (ln_chain, acc_ready):
                v.sem_inc(s, SEED)

            def norm(batch, kept):
                v.wait_ge(x_in, batch.done(16, 16))
                if kept:
                    v.wait_ge(xn_kept, batch.done(1, 0))
                    v.wait_ge(xt_mm, batch.done(1, 0))
                LayerNorm(v, xin, stats, small, ln_chain, lambda k: batch.done(LN_LINKS, k + SEED), v_step,
                          out=xn).whole().then_inc(xn_ready, 1)

            def norm_t(batch):
                for n in range(2):
                    v.wait_ge(xt_hi, batch.done(2, n + 1))
                    half = slice(2 * n, 2 * n + 2)
                    v.tensor_tensor(xt[1][:, half, :].rearrange("p c t -> p (c t)"), x_ps[n][:],
                                    xt[0][:, half, :].rearrange("p c t -> p (c t)").bitcast(F32),
                                    ALU.subtract).then_inc(xt_lo, 1)

            norm(Batch(Values(v), 0), False)
            norm_t(Batch(Values(v), 0))
            norm(Batch(Values(v), 1), True)
            with v.Fori(0, B) as i:
                val = Values(v, i)
                now, nxt, after = Batch(val, 0), Batch(val, 1), Batch(val, 2)
                col = v.snap(i * ST)
                v.wait_ge(logit_mm, now.done(1, 1))
                v.tensor_tensor(logits[:, bass.ds(col, ST), :], x_ps[0][:, 0:ST * EP].rearrange("p (t e) -> p t e", e=EP),
                                eb[:], ALU.add).then_inc(logit_out, 1)
                for n in range(FC):
                    v.wait_ge(silu, now.done(FC, n + 1))
                    v.wait_ge(up_mm, now.done(FC, n + 1))
                    v.tensor_tensor(gate[n][:], up_ps[n][:, 0:S], sil[n][:], ALU.mult).then_inc(gated, 1)
                    v.wait_ge(gt_hi, now.done(FC, n + 1))
                    v.tensor_tensor(gt[n][1][:], gate[n][:], gt[n][0][:].bitcast(F32), ALU.subtract).then_inc(gt_lo, 1)
                norm_t(nxt)
                norm(after, True)
                v.wait_ge(res_in, now.done(16, 16))
                v.wait_ge(y_mm, now.done(1, 1))
                for t in range(ST):
                    last = v.tensor_tensor(res[:, t, :], y_ps[t][:], res[:, t, :], ALU.add)
                last.then_inc(acc_ready, 1)

        @block.gpsimd
        def _(g):
            hold(g, xn_ready, 1, g_step)
            g.tensor_copy(xn3[:, 0:ST, :], xn[:]).then_inc(xn_kept, 1)
            hold(g, xn_ready, 2, g_step)
            g.tensor_copy(xn3[:, ST:2 * ST, :], xn[:]).then_inc(xn_kept, 1)
            with g.Fori(0, B) as i:
                val = Values(g, i)
                ready, col = val(1, 3), g.snap(((i + 2) % B) * ST)
                hold(g, xn_ready, ready, g_step)
                g.tensor_copy(xn3[:, bass.ds(col, ST), :], xn[:]).then_inc(xn_kept, 1)

        @block.tensor
        def _(pe):
            pe.wait_ge(w_lo, len(weights))
            pe.wait_ge(const_in, 16 * (1 + ST))

            def norm_t(batch):
                pe.wait_ge(xn_ready, batch.done(1, 1))
                for c in range(DC):
                    for t in range(ST):
                        at = (c % 2) * S + t * P
                        last = pe.transpose(x_ps[c // 2][:, at:at + P], xn[:, t, c * P:(c + 1) * P], ident[:])
                last.then_inc(xt_mm, 1)

            norm_t(Batch(Values(pe), 0))
            with pe.Fori(0, B) as i:
                val = Values(pe, i)
                now, nxt = Batch(val, 0), Batch(val, 1)
                pe.wait_ge(xt_lo, now.done(2, 2))
                for t in range(ST):
                    for c in range(DC):
                        last = product(pe, x_ps[0][:, t * EP:(t + 1) * EP], [w[:, c, t * P:(t + 1) * P] for w in xt],
                                       [w[:, c, :] for w in wg], c == 0, c == DC - 1)
                last.then_inc(logit_mm, 1)
                for n in range(FC):
                    for bank, f, done in ((gate_ps[n], FC + n, gate_mm), (up_ps[n], n, up_mm)):
                        for c in range(DC):
                            last = product(pe, bank[:, 0:S], [w[:, c, f * P:(f + 1) * P] for w in w1p],
                                           [w[:, c, :] for w in xt], c == 0, c == DC - 1)
                        last.then_inc(done, 1)
                pe.wait_ge(logit_out, now.done(1, 1))
                norm_t(nxt)
                pe.wait_ge(acc_ready, now.done(1, SEED))
                pe.wait_ge(gt_lo, now.done(FC, FC))
                for t in range(ST):
                    for n in range(FC):
                        last = product(pe, y_ps[t][:], [w[:, t * P:(t + 1) * P] for w in gt[n]],
                                       [w[:, n, :] for w in w2p], n == 0, n == FC - 1)
                last.then_inc(y_mm, 1)


def route(nc, logits, low_tri, slot_base, xn3, weight, gather_at, xg):
    with ExitStack() as ctx:
        sems = []

        def sb(name, shape, dt=F32):
            return ctx.enter_context(nc.sbuf_tensor("r_" + name, shape, dt))

        def sem(name):
            sems.append(ctx.enter_context(nc.semaphore("r_" + name)))
            return sems[-1]

        W = [P, NT, EP]
        aff, rank, beats, chosen, score = sb("aff", W), sb("rank", W), [sb(f"beats{n}", W) for n in range(2)], sb(
            "chosen", W), sb("score", W)
        over, tied, kept, place, tot = sb("over", W), sb("tied", W), sb("kept", W), sb("place", W), sb("tot", W)
        scan = [sb(f"scan{n}", W) for n in range(2)]
        cum, pick, tmp = sb("cum", W), sb("pick", W), sb("tmp", W)
        base = sb("base", [P, EP])
        cnt, need = sb("cnt", [P, EP]), sb("need", [P, EP])
        bit, thr, cand, add = (sb(n, [P, EP], I32) for n in ("bit", "thr", "cand", "add"))
        ones, tri = sb("ones", [P, P]), sb("tri", [P, P])
        dest, has = sb("dest", [P, 2, NT]), sb("has", [P, 2, NT])
        at_s, at_g = sb("at_s", [P, 2, NT]), sb("at_g", [P, 2, NT])
        scatter_at = sb("scatter_at", [P, 2, NT], U32)
        count_ps = ctx.enter_context(nc.psum_tensor("r_count_ps", [P, 512], F32))
        pre_ps = ctx.enter_context(nc.psum_tensor("r_pre_ps", [P, 512], F32))
        tot_ps = ctx.enter_context(nc.psum_tensor("r_tot_ps", [P, 512], F32))

        const_in, aff_ready, chain, search = sem("const_in"), sem("aff_ready"), sem("chain"), sem("search")
        counted, total_mm, sums_in, sums_mm = sem("counted"), sem("total_mm"), sem("sums_in"), sem("sums_mm")
        routed, sent, v_step = sem("routed"), sem("sent"), sem("v_step")
        STEPS, LINKS = 30, 5
        ctx.callback(clear, nc, sems)
        block = ctx.enter_context(nc.Block())

        def wide(a, n=NT):
            return a[:, 0:E].rearrange("p (o e) -> p o e", o=1).to_broadcast([P, n, E])

        @block.sync
        def _(sp):
            sp.dma_start(tri[:], low_tri).then_inc(const_in, 16)
            sp.dma_start(base[:], slot_base.to_broadcast([P, EP])).then_inc(const_in, 16)

        @block.scalar
        def _(act):
            act.activation(aff[:], logits[:], ACT.Sigmoid).then_inc(aff_ready, 1)

        @block.vector
        def _(v):
            count = [0]

            def link(ins):
                count[0] += 1
                ins.then_inc(chain, 1)
                v.wait_ge(chain, count[0])

            def used(a):
                return a[:, :, 0:E]

            for a in (rank, score, kept, tied, over, beats[0], beats[1]):
                v.memset(a[:], 0.0)
            v.memset(cnt[:], 0.0)
            v.memset(ones[:], 1.0)
            v.memset(thr[:].bitcast(F32), 0.0)
            link(v.memset(bit[:], 1 << (STEPS - 1)))
            v.wait_ge(const_in, 32)
            v.wait_ge(aff_ready, 1)
            for e in range(E):
                one = aff[:, :, e:e + 1]
                b = beats[e % 2]
                if e:
                    v.tensor_tensor(b[:, :, 0:e], one.to_broadcast([P, NT, e]), aff[:, :, 0:e], ALU.is_gt)
                    last = v.memset(b[:, :, e:e + 1], 0.0)
                if e < E - 1:
                    last = v.tensor_tensor(b[:, :, e + 1:E], one.to_broadcast([P, NT, E - 1 - e]), aff[:, :, e + 1:E],
                                           ALU.is_ge)
                link(last)
                link(v.tensor_tensor(used(rank), used(rank), used(b), ALU.add))
            link(v.tensor_scalar(used(chosen), used(rank), TOP_K - 0.5, None, ALU.is_lt))
            link(v.tensor_tensor(used(score), used(aff), used(chosen), ALU.mult))
            link(v.tensor_copy(cand[:], bit[:]))

            v.sem_inc(search, 1)
            with v.Fori(0, STEPS) as i:
                val = Values(v, i)

                def step(ins, k):
                    ins.then_inc(search, 1)
                    v.wait_ge(search, val(LINKS, k + 1))

                step(v.tensor_tensor(used(over), used(score), wide(cand[:].bitcast(F32)), ALU.is_ge), 1)
                v.tensor_reduce(cnt[:, 0:E], used(over).rearrange("p t e -> p e t"), AX.X, ALU.add).then_inc(counted, 1)
                v.wait_ge(total_mm, val(1, 1))
                step(v.scalar_tensor_tensor(add[:], count_ps[:, 0:EP], CAP - 0.5, bit[:], ALU.is_gt, ALU.mult), 2)
                v.tensor_tensor(thr[:], thr[:], add[:], ALU.bitwise_or).then_inc(search, 1)
                step(v.tensor_scalar(bit[:], bit[:], 1, None, ALU.logical_shift_right), 4)
                step(v.tensor_tensor(cand[:], thr[:], bit[:], ALU.bitwise_or), 5)

            least = thr[:].bitcast(F32)
            v.tensor_tensor(used(over), used(score), wide(least), ALU.is_gt)
            link(v.tensor_tensor(used(tied), used(score), wide(least), ALU.is_equal))
            v.tensor_reduce(cnt[:, 0:E], used(over).rearrange("p t e -> p e t"), AX.X, ALU.add)
            link(v.tensor_tensor(used(tied), used(tied), used(chosen), ALU.mult))
            v.sem_inc(sums_in, 1)

            def places(k, of):
                v.wait_ge(sums_mm, k)
                v.tensor_copy(place[:], pre_ps[:, 0:NT * EP].rearrange("p (t e) -> p t e", e=EP))
                v.tensor_copy(tot[:], tot_ps[:, 0:NT * EP].rearrange("p (t e) -> p t e", e=EP))
                link(v.tensor_copy(scan[0][:], tot_ps[:, 0:NT * EP].rearrange("p (t e) -> p t e", e=EP)))
                d, n = 1, 0
                while d < NT:
                    v.tensor_copy(scan[1 - n][:, 0:d, :], scan[n][:, 0:d, :])
                    link(v.tensor_tensor(scan[1 - n][:, d:, :], scan[n][:, d:, :], scan[n][:, 0:NT - d, :], ALU.add))
                    d, n = 2 * d, 1 - n
                link(v.tensor_tensor(place[:], place[:], scan[n][:], ALU.add))
                link(v.tensor_tensor(place[:], place[:], tot[:], ALU.subtract))

            places(1, tied)
            link(v.tensor_scalar(need[:, 0:E], count_ps[:, 0:E], -1.0, float(CAP), ALU.mult, ALU.add))
            link(v.tensor_tensor(used(tmp), used(place), wide(need[:]), ALU.is_lt))
            link(v.tensor_tensor(used(tmp), used(tmp), used(tied), ALU.mult))
            link(v.tensor_tensor(used(kept), used(over), used(tmp), ALU.add))
            v.sem_inc(sums_in, 1)
            places(2, kept)
            link(v.tensor_tensor(used(place), used(place), wide(base[:]), ALU.add))
            v.tensor_copy(cum[:, :, 0:1], kept[:, :, 0:1])
            link(v.memset(cum[:, :, E:EP], 0.0))
            for e in range(1, E):
                link(v.tensor_tensor(cum[:, :, e:e + 1], cum[:, :, e - 1:e], kept[:, :, e:e + 1], ALU.add))
            for s in range(2):
                link(v.tensor_scalar(used(pick), used(cum), float(s + 1), None, ALU.is_equal))
                link(v.tensor_tensor(used(pick), used(pick), used(kept), ALU.mult))
                link(v.tensor_reduce(has[:, s, :], used(pick), AX.X, ALU.add))
                link(v.tensor_tensor(used(tmp), used(pick), used(place), ALU.mult))
                link(v.tensor_reduce(dest[:, s, :], used(tmp), AX.X, ALU.add))
                link(v.tensor_tensor(used(tmp), used(pick), used(aff), ALU.mult))
                link(v.tensor_reduce(weight[:, s, :], used(tmp), AX.X, ALU.add))
            for at, away in ((at_s, 4 * ROWS), (at_g, ROWS)):
                link(v.tensor_scalar(at[:], has[:], -float(away), float(away), ALU.mult, ALU.add))
                link(v.tensor_tensor(at[:], at[:], dest[:], ALU.add))
            link(v.tensor_copy(gather_at[:], at_g[:]))
            link(v.tensor_copy(scatter_at[:], at_s[:]))
            v.sem_inc(routed, 1)

        @block.tensor
        def _(pe):
            with pe.Fori(0, STEPS) as i:
                val = Values(pe, i)
                pe.wait_ge(counted, val(1, 1))
                pe.matmul(count_ps[:, 0:EP], ones[:], cnt[:], start=True, stop=True).then_inc(total_mm, 1)
            flat = "p t e -> p (t e)"
            pe.wait_ge(sums_in, 1)
            pe.matmul(count_ps[:, 0:EP], ones[:], cnt[:], start=True, stop=True)
            for k, flags in enumerate((tied, kept)):
                pe.wait_ge(sums_in, k + 1)
                pe.matmul(pre_ps[:, 0:NT * EP], tri[:], flags[:].rearrange(flat), start=True, stop=True)
                pe.matmul(tot_ps[:, 0:NT * EP], ones[:], flags[:].rearrange(flat), start=True,
                          stop=True).then_inc(sums_mm, 1)

        @block.gpsimd
        def _(g):
            g.wait_ge(routed, 1)
            for t in range(NT):
                for s in range(2):
                    g.indirect_dma_start(out=xg, out_offset=bass.IndirectOffsetOnAxis(scatter_at[:, s, t:t + 1], 0),
                                         in_=xn3[:, t, :], in_offset=None, bounds_check=ROWS - 1,
                                         oob_is_err=False).then_inc(sent, 16)
            g.wait_ge(sent, 16 * 2 * NT)


def routed_experts(nc, w1, w2, ident_in, xg, yg):
    HALF = SLOTS // 2
    UNITS = 2 * FC
    with ExitStack() as ctx:
        sems = []

        def sb(name, shape, dt=F32):
            return ctx.enter_context(nc.sbuf_tensor("e_" + name, shape, dt))

        def pb(name, shape):
            return ctx.enter_context(nc.psum_tensor("e_ps_" + name, shape, F32))

        def sem(name):
            sems.append(ctx.enter_context(nc.semaphore("e_" + name)))
            return sems[-1]

        def parts(name, shape):
            return sb(name + "_hi", shape, F32R), sb(name + "_lo", shape, F32R)

        r1, r2, w1p, w2p = sb("r1", [P, DC, 2 * F]), sb("r2", [P, FC, D]), parts("w1", [P, DC, 2 * F]), parts(
            "w2", [P, FC, D])
        ident, xin = sb("ident", [P, P]), sb("xin", [P, CT, D])
        xt = parts("xt", [P, DC, SLOTS])
        sil = [sb(f"sil{n}", [P, HALF]) for n in range(2)]
        gate = [sb(f"gate{n}", [P, HALF]) for n in range(2)]
        gt = parts("gt", [P, FC, SLOTS])
        ysb = sb("ysb", [P, CT, D])
        up_ps, gate_ps, x_ps, y_ps = ([pb(f"{name}{n}", [P, 512]) for n in range(2)] for name in ("up", "gt", "x", "y"))

        const_in, w1_in, w2_in, x_in, stored = sem("const_in"), sem("w1_in"), sem("w2_in"), sem("x_in"), sem("stored")
        w1_hi, w1_lo, w2_hi, w2_lo = sem("w1_hi"), sem("w1_lo"), sem("w2_hi"), sem("w2_lo")
        xt_mm, xt_hi, xt_lo = sem("xt_mm"), sem("xt_hi"), sem("xt_lo")
        gate_mm, up_mm, silu, gated, gt_hi, gt_lo = (sem("gate_mm"), sem("up_mm"), sem("silu"), sem("gated"),
                                                     sem("gt_hi"), sem("gt_lo"))
        y_mm, y_out, y_sent, sp_step = sem("y_mm"), sem("y_out"), sem("y_sent"), sem("sp_step")
        ctx.callback(clear, nc, sems)
        block = ctx.enter_context(nc.Block())

        def load(sp, e, which):
            if which == 1:
                sp.dma_start(r1[:], w1[e].rearrange("o (c p) n -> p (o c) n", p=P)).then_inc(w1_in, 16)
            elif which == 2:
                sp.dma_start(r2[:], w2[e].rearrange("o (c p) n -> p (o c) n", p=P)).then_inc(w2_in, 16)
            else:
                sp.dma_start(xin[:], xg[e].rearrange("o (t p) d -> p (o t) d", p=P)).then_inc(x_in, 16)

        @block.sync
        def _(sp):
            sp.dma_start(ident[:], ident_in).then_inc(const_in, 16)
            for which in (0, 1, 2):
                load(sp, slice(0, 1), which)
            sp.sem_inc(y_sent, 1)
            with sp.Fori(0, E) as i:
                val = Values(sp, i)
                now = Batch(val, 0)
                nxt = sp.snap((i + 1) % E)
                x_free, w1_free, w2_free, y_done, y_stored = (now.done(CT, CT), now.done(1, 1), now.done(1, 1),
                                                              now.done(CT, CT + SEED), now.done(16, 16))
                hold(sp, xt_mm, x_free, sp_step)
                load(sp, bass.ds(nxt, 1), 0)
                hold(sp, w1_lo, w1_free, sp_step)
                load(sp, bass.ds(nxt, 1), 1)
                hold(sp, w2_lo, w2_free, sp_step)
                load(sp, bass.ds(nxt, 1), 2)
                hold(sp, y_out, y_done, sp_step)
                sp.dma_start(yg[bass.ds(i, 1)].rearrange("o (t p) d -> p (o t) d", p=P), ysb[:]).then_inc(stored, 16)
                hold(sp, stored, y_stored, y_sent)

        def split1_hi(act, batch, free):
            act.wait_ge(w1_in, batch.done(16, 16))
            if free is not None:
                act.wait_ge(up_mm, free)
            act.activation(w1p[0][:], r1[:], ACT.Copy).then_inc(w1_hi, 1)

        @block.scalar
        def _(act):
            def norm_t(batch):
                for t in range(CT):
                    act.wait_ge(xt_mm, batch.done(CT, t + 1))
                    act.activation(xt[0][:, :, t * P:(t + 1) * P],
                                   x_ps[t % 2][:].rearrange("p (c t) -> p c t", c=DC), ACT.Copy).then_inc(xt_hi, 1)

            def split2(batch, free):
                act.wait_ge(w2_in, batch.done(16, 16))
                if free is not None:
                    act.wait_ge(y_mm, free)
                act.activation(w2p[0][:], r2[:], ACT.Copy).then_inc(w2_hi, 1)

            first = Batch(Values(act), 0)
            split1_hi(act, first, None)
            split2(first, None)
            norm_t(first)
            with act.Fori(0, E) as i:
                val = Values(act, i)
                now, nxt = Batch(val, 0), Batch(val, 1)
                for u in range(UNITS):
                    half, n = u // FC, u % FC
                    act.wait_ge(gate_mm, now.done(UNITS, u + 1))
                    act.activation(sil[u % 2][:], gate_ps[u % 2][:, 0:HALF], ACT.Silu).then_inc(silu, 1)
                    act.wait_ge(gated, now.done(UNITS, u + 1 + SEED))
                    act.activation(gt[0][:, n, half * HALF:(half + 1) * HALF], gate[u % 2][:],
                                   ACT.Copy).then_inc(gt_hi, 1)
                split1_hi(act, nxt, now.done(UNITS, UNITS))
                norm_t(nxt)
                split2(nxt, now.done(CT, CT))

        @block.vector
        def _(v):
            v.sem_inc(y_out, SEED)
            v.sem_inc(gated, SEED)

            def norm_t(batch):
                for t in range(CT):
                    v.wait_ge(xt_hi, batch.done(CT, t + 1))
                    rows = slice(t * P, (t + 1) * P)
                    v.tensor_tensor(xt[1][:, :, rows], x_ps[t % 2][:].rearrange("p (c t) -> p c t", c=DC),
                                    xt[0][:, :, rows].bitcast(F32), ALU.subtract).then_inc(xt_lo, 1)

            norm_t(Batch(Values(v), 0))
            with v.Fori(0, E) as i:
                val = Values(v, i)
                now, nxt = Batch(val, 0), Batch(val, 1)
                for u in range(UNITS):
                    half, n = u // FC, u % FC
                    cols = slice(half * HALF, (half + 1) * HALF)
                    v.wait_ge(silu, now.done(UNITS, u + 1))
                    v.wait_ge(up_mm, now.done(UNITS, u + 1))
                    v.tensor_tensor(gate[u % 2][:], up_ps[u % 2][:, 0:HALF], sil[u % 2][:], ALU.mult).then_inc(gated, 1)
                    v.wait_ge(gt_hi, now.done(UNITS, u + 1))
                    v.tensor_tensor(gt[1][:, n, cols], gate[u % 2][:], gt[0][:, n, cols].bitcast(F32),
                                    ALU.subtract).then_inc(gt_lo, 1)
                norm_t(nxt)
                for t in range(CT):
                    v.wait_ge(y_mm, now.done(CT, t + 1))
                    if t == 0:
                        v.wait_ge(y_sent, now.done(1, 1))
                    v.tensor_copy(ysb[:, t, :], y_ps[t % 2][:]).then_inc(y_out, 1)

        @block.gpsimd
        def _(g):
            def split(batch):
                g.wait_ge(w1_hi, batch.done(1, 1))
                g.tensor_tensor(w1p[1][:], r1[:], w1p[0][:].bitcast(F32), ALU.subtract).then_inc(w1_lo, 1)
                g.wait_ge(w2_hi, batch.done(1, 1))
                g.tensor_tensor(w2p[1][:], r2[:], w2p[0][:].bitcast(F32), ALU.subtract).then_inc(w2_lo, 1)

            split(Batch(Values(g), 0))
            with g.Fori(0, E) as i:
                split(Batch(Values(g, i), 1))

        @block.tensor
        def _(pe):
            pe.wait_ge(const_in, 16)

            def norm_t(batch, t_from=0):
                pe.wait_ge(x_in, batch.done(16, 16))
                for t in range(CT):
                    if t >= 2:
                        pe.wait_ge(xt_lo, batch.done(CT, t - 1))
                    for c in range(DC):
                        last = pe.transpose(x_ps[t % 2][:, c * P:(c + 1) * P], xin[:, t, c * P:(c + 1) * P], ident[:])
                    last.then_inc(xt_mm, 1)

            norm_t(Batch(Values(pe), 0))
            with pe.Fori(0, E) as i:
                val = Values(pe, i)
                now, nxt = Batch(val, 0), Batch(val, 1)
                pe.wait_ge(w1_lo, now.done(1, 1))
                pe.wait_ge(xt_lo, now.done(CT, CT))
                for u in range(UNITS):
                    half, n = u // FC, u % FC
                    pe.wait_ge(gated, now.done(UNITS, u - 1 + SEED))
                    for bank, f, done in ((gate_ps[u % 2], FC + n, gate_mm), (up_ps[u % 2], n, up_mm)):
                        for c in range(DC):
                            last = product(pe, bank[:, 0:HALF], [w[:, c, f * P:(f + 1) * P] for w in w1p],
                                           [w[:, c, half * HALF:(half + 1) * HALF] for w in xt], c == 0, c == DC - 1)
                        last.then_inc(done, 1)
                norm_t(nxt)
                pe.wait_ge(w2_lo, now.done(1, 1))
                pe.wait_ge(gt_lo, now.done(UNITS, UNITS))
                for t in range(CT):
                    pe.wait_ge(y_out, now.done(CT, t - 1 + SEED))
                    for n in range(FC):
                        last = product(pe, y_ps[t % 2][:], [w[:, n, t * P:(t + 1) * P] for w in gt],
                                       [w[:, n, :] for w in w2p], n == 0, n == FC - 1)
                    last.then_inc(y_mm, 1)


def combine(nc, acc_dram, weight, gather_at, yg, out):
    G = 4
    with ExitStack() as ctx:
        sems = []

        def sb(name, shape, dt=F32):
            return ctx.enter_context(nc.sbuf_tensor("o_" + name, shape, dt))

        def sem(name):
            sems.append(ctx.enter_context(nc.semaphore("o_" + name)))
            return sems[-1]

        acc = [sb(f"acc{n}", [P, D]) for n in range(G)]
        rows = [[sb(f"rows{s}_{n}", [P, D]) for s in range(2)] for n in range(G)]
        at = sb("at", [P, 2, G], U32)
        w = sb("w", [P, 2, G])
        at_copied, w_copied, g_step, v_step, sp_step, a_step = (sem("at_copied"), sem("w_copied"), sem("g_step"),
                                                                sem("v_step"), sem("sp_step"), sem("a_step"))
        acc_in, got, first_added, added, stored = ([sem(f"{k}{n}") for n in range(G)] for k in (
            "acc_in", "got", "first_added", "added", "stored"))
        ctx.callback(clear, nc, sems)
        block = ctx.enter_context(nc.Block())
        acc_t, out_t = (a.rearrange("b (t p) d -> (b t) p d", p=P) for a in (acc_dram, out))

        @block.gpsimd
        def _(g):
            with g.Fori(0, NT // G) as i:
                val = Values(g, i)
                col = g.snap(i * G)
                free, copied = val(1, 1), val(1, 1)
                hold(g, added[G - 1], free, g_step)
                g.tensor_copy(at[:], gather_at[:, :, bass.ds(col, G)]).then_inc(at_copied, 1)
                hold(g, at_copied, copied, g_step)
                for n in range(G):
                    for s in range(2):
                        g.indirect_dma_start(out=rows[n][s][:], out_offset=None, in_=yg,
                                             in_offset=bass.IndirectOffsetOnAxis(at[:, s, n:n + 1], 0)
                                             ).then_inc(got[n], 16)

        @block.sync
        def _(sp):
            with sp.Fori(0, NT // G) as i:
                val = Values(sp, i)
                free = val(16, 16)
                for n in range(G):
                    tile = sp.snap(i * G + n)
                    hold(sp, stored[n], free, sp_step)
                    sp.dma_start(acc[n][:], acc_t[bass.ds(tile, 1)].rearrange("o p d -> (o p) d")).then_inc(
                        acc_in[n], 16)

        @block.vector
        def _(v):
            v.sem_inc(added[G - 1], 1)
            with v.Fori(0, NT // G) as i:
                val = Values(v, i)
                col = v.snap(i * G)
                hold(v, added[G - 1], val(1, 1), v_step)
                v.tensor_copy(w[:], weight[:, :, bass.ds(col, G)]).then_inc(w_copied, 1)
                v.wait_ge(w_copied, val(1, 1))
                for n in range(G):
                    v.wait_ge(acc_in[n], val(16, 16))
                    v.wait_ge(got[n], val(32, 32))
                    v.scalar_tensor_tensor(acc[n][:], rows[n][0][:], w[:, 0, n:n + 1], acc[n][:], ALU.mult,
                                           ALU.add).then_inc(first_added[n], 1)
                for n in range(G):
                    v.wait_ge(first_added[n], val(1, 1))
                    v.scalar_tensor_tensor(acc[n][:], rows[n][1][:], w[:, 1, n:n + 1], acc[n][:], ALU.mult,
                                           ALU.add).then_inc(added[n], 1)

        @block.scalar
        def _(act):
            for n in range(G):
                act.sem_inc(stored[n], 16)
            with act.Fori(0, NT // G) as i:
                val = Values(act, i)
                for n in range(G):
                    tile = act.snap(i * G + n)
                    act.wait_ge(added[n], val(1, 2 if n == G - 1 else 1))
                    act.dma_start(out_t[bass.ds(tile, 1)].rearrange("o p d -> (o p) d"), acc[n][:]).then_inc(
                        stored[n], 16)
            for n in range(G):
                act.wait_ge(stored[n], 16 * (NT // G + 1))


def mixture(nc, x2, gate_w, bias, shared_w1, shared_w2, w1, w2, low_tri, slot_base, ident, acc, xg, yg, out):
    with ExitStack() as ctx:
        def sb(name, shape, dt=F32):
            return ctx.enter_context(nc.sbuf_tensor("m_" + name, shape, dt))

        weight, gather_at = sb("weight", [P, 2, NT]), sb("gather_at", [P, 2, NT], U32)
        with ExitStack() as until_sent:
            xn3 = until_sent.enter_context(nc.sbuf_tensor("m_xn3", [P, NT, D], F32))
            logits = until_sent.enter_context(nc.sbuf_tensor("m_logits", [P, NT, EP], F32))
            shared_expert(nc, x2, gate_w, bias, shared_w1, shared_w2, ident, xn3, logits, acc, xg, yg)
            route(nc, logits, low_tri, slot_base, xn3, weight, gather_at, xg)
        routed_experts(nc, w1, w2, ident, xg.rearrange("(e s) d -> e s d", s=SLOTS),
                       yg[0:ROWS, :].rearrange("(e s) d -> e s d", s=SLOTS))
        combine(nc, acc, weight, gather_at, yg, out)


def decoder_layer(nc, a, out):
    def scratch(name, shape):
        return nc.dram_tensor(name, shape, F32, kind="Internal").ap()

    x1, x2, acc = (scratch(name, (B, S, D)) for name in ("x1", "x2", "acc"))
    self_attention(nc, a["x"], a["w_lat"], a["b_lat"], a["w_d"], a["b_d"], a["w_proj"], a["b_proj"], a["causal"],
                   a["ident"], x1)
    cross_attention(nc, x1, a["ctx_t"], a["seg"], a["w_kvc"], a["w_dq"], a["uq_t"], a["w_qr"], a["uk_t"], a["kr_uv"],
                    a["uv_t"], a["w_o"], a["trig"], a["rot_cs"], a["key_ids"], a["ident"], x2)
    mixture(nc, x2, a["gate_w"], a["bias"], a["shared_w1"], a["shared_w2"], a["w1"], a["w2"], a["low_tri"],
            a["slot_base"], a["ident"], acc, scratch("xg", (ROWS, D)), scratch("yg", (ROWS + P, D)), out)


def kernel(**inputs):
    import numpy as np
    import concourse.bacc as bacc
    from concourse import mybir as _mybir
    from concourse.bass_utils import run_bass_kernel_spmd

    nc = bacc.Bacc("TRN2", target_bir_lowering=False, num_devices=1)
    arrays, args = {}, {}

    def give(name, a):
        a = np.ascontiguousarray(a)
        arrays[f"in_{name}"] = a
        args[name] = nc.dram_tensor(f"in_{name}", a.shape, _mybir.dt.from_np(a.dtype), kind="ExternalInput").ap()

    def padded(a, shape):
        wide = np.zeros(shape, np.float32)
        wide[:, 0:a.shape[-1]] = a
        return wide

    attn = {k: np.asarray(inputs["L0_attn_" + k]) for k in ("W_lat", "b_lat", "W_d", "b_d", "W_proj", "b_proj")}
    cross = {k: np.asarray(inputs["L0_xattn_" + k]) for k in ("W_kvc", "W_dq", "W_uq", "W_qr", "W_uk", "W_kr", "W_uv",
                                                              "W_o")}
    ffn = {k: np.asarray(inputs["L0_ffn_" + k]) for k in ("gate_w", "expert_bias", "shared_w1", "shared_w2",
                                                          "routed_w1", "routed_w2")}
    give("x", inputs["x"])
    for k in ("W_lat", "b_lat", "W_d", "W_proj", "b_proj"):
        give(k.lower(), attn[k])
    give("b_d", attn["b_d"].reshape(H, L).T)
    t = np.arange(P)
    triangle = np.where(t[None, :] <= t[:, None], 0.0, MASKED).astype(np.float32)
    give("causal", np.concatenate([triangle, np.zeros((P, P), np.float32), triangle], 1))
    give("ident", np.eye(P, dtype=np.float32))
    give("ctx_t", np.asarray(inputs["ctx_2048"]).transpose(0, 2, 1))
    give("seg", np.asarray(inputs["itok_BxS_0_1023"]).reshape(NT, P).T)
    for k in ("W_kvc", "W_dq", "W_qr", "W_o"):
        give(k.lower(), cross[k])
    for k in ("uq", "uk", "uv"):
        give(k + "_t", cross["W_" + k].T)
    half = R // 2
    k1, k2 = cross["W_kr"][:, 0:half], cross["W_kr"][:, half:R]
    give("kr_uv", np.stack([np.concatenate([k1, k2, k2, k1], 1), np.concatenate([k2, k1, k1, k2], 1)], 1))
    freq = np.float32(1.0) / np.float32(10000.0) ** (np.arange(half, dtype=np.float32) / np.float32(half))
    angle = np.arange(S, dtype=np.float32)[None, :] * freq[:, None]
    cos, sin = np.cos(angle), np.sin(angle)
    give("trig", np.concatenate([cos, cos, sin, sin], 0))
    give("rot_cs", np.stack([np.concatenate([cos, cos, cos, -cos], 0), np.concatenate([-sin, sin, sin, sin], 0)]))
    give("key_ids", np.broadcast_to(np.arange(S, dtype=np.float32)[None, :], (P, S)))
    give("gate_w", padded(ffn["gate_w"], (D, EP)))
    give("bias", padded(ffn["expert_bias"], (1, EP)))
    give("shared_w1", ffn["shared_w1"][0])
    give("shared_w2", ffn["shared_w2"][0])
    give("w1", ffn["routed_w1"])
    give("w2", ffn["routed_w2"])
    give("low_tri", np.triu(np.ones((P, P), np.float32), 1))
    give("slot_base", (np.arange(EP, dtype=np.float32) * SLOTS)[None, :])

    out = nc.dram_tensor("out_0", (B, S, D), _mybir.dt.float32, kind="ExternalOutput").ap()
    decoder_layer(nc, args, out)
    r = run_bass_kernel_spmd(nc, [arrays], core_ids=[0])
    return r.results[0]["out_0"]
```

```python
import math
from contextlib import ExitStack

import concourse.bass as bass
from concourse import mybir

F32 = mybir.dt.float32
F32R = mybir.dt.float32r
BF16 = mybir.dt.bfloat16
I32 = mybir.dt.int32
U32 = mybir.dt.uint32
ALU = mybir.AluOpType
ACT = mybir.ActivationFunctionType
AX = mybir.AxisListType

P = 128
B, S, D = 16, 256, 512
H = 16
L = 128
ST = S // P
DC = D // P
QC, QCC = 192, 2
R = 64
EPS = 1e-5
MASKED = -float(2 ** 100)
LOOKBACK = 8
NT = B * ST
E, EP = 7, 8
F = 256
FC = F // P
TOP_K = 2
CAP = B * S // E
CT = -(-CAP // P)
SLOTS = CT * P
ROWS = E * SLOTS
DX = D + EP
NOWHERE = 4.0 * B * S
LN_LINKS = 14
NORM_AT = 5
SEED = 2


class Values:

    def __init__(self, eng, i=None):
        self.eng, self.i, self.known = eng, i, {}

    def __call__(self, per, k):
        if self.i is None or per == 0:
            return k
        if (per, k) not in self.known:
            self.known[per, k] = self.eng.snap(self.i * per + k)
        return self.known[per, k]


class Unit:

    def __init__(self, values):
        self.values = values

    def done(self, h):
        return self.values(H, h + 1 + SEED)


class Batch:

    def __init__(self, values, shift):
        self.values, self.shift = values, shift

    def done(self, per=1, k=0):
        return self.values(per, per * self.shift + k)


def clear(nc, sems):
    for s in sems:
        nc.gpsimd.sem_clear(s)
    nc.all_engine_barrier()


def hold(eng, sem, value, step):
    eng.wait_ge(sem, value)
    eng.sem_inc(step, 1)


def product(pe, out, lhs, rhs, first, last):
    pe.matmul(out, lhs[0], rhs[0], start=first, stop=False)
    pe.matmul(out, lhs[0], rhs[1], start=False, stop=False)
    return pe.matmul(out, lhs[1], rhs[0], start=False, stop=last)


class LayerNorm:

    PIECES = ST + 4 + ST

    def __init__(self, v, xt, stats, small, chain, at, step, out=None, tiles=ST):
        self.tiles = tiles
        self.v, self.xt, self.stats, self.chain, self.at, self.step = v, xt, stats, chain, at, step
        self.out = xt if out is None else out
        self.ve, self.half, self.y, self.w = (small[:, n, :] for n in range(4))
        self.links = 0

    def link(self, ins):
        self.links += 1
        ins.then_inc(self.chain, 1)
        self.v.wait_ge(self.chain, self.at(self.links))

    def moments(self, t):
        last = self.v.bn_stats(self.stats[:, t, 0:6], self.xt[:, t, :])
        if t == self.tiles - 1:
            last.then_inc(self.chain, 1)
            self.links += 1

    def variance(self):
        v, y = self.v, self.y.bitcast(I32)
        hold(v, self.chain, self.at(1), self.step)
        for t in range(self.tiles):
            last = v.bn_aggr(self.stats[:, t, 6:8], self.stats[:, t, 0:6])
        self.link(last)
        self.link(v.tensor_scalar(self.ve, self.stats[:, :, 7], EPS, None, ALU.add))
        v.tensor_scalar(self.half, self.ve, -0.5, None, ALU.mult)
        self.link(v.tensor_scalar(y, self.ve.bitcast(I32), 1, None, ALU.logical_shift_right))
        self.link(v.tensor_scalar(y, y, -1.0, float(0x5F3759DF), ALU.mult, ALU.add))

    def newton(self, n):
        v, y, w = self.v, self.y, self.w
        self.link(v.tensor_tensor(w, y, self.half, ALU.mult))
        self.link(v.tensor_tensor(w, w, y, ALU.mult))
        self.link(v.scalar_tensor_tensor(y, w, 1.5, y, ALU.add, ALU.mult))
        assert n < 2 or self.links == LN_LINKS

    def apply(self, t):
        return self.v.tensor_scalar(self.out[:, t, :], self.xt[:, t, :], self.stats[:, t, 6:7], self.y[:, t:t + 1],
                                    ALU.subtract, ALU.mult)

    def piece(self, n):
        n -= self.tiles
        if n < 0:
            return self.moments(n + self.tiles)
        if n == 0:
            return self.variance()
        return self.newton(n - 1) if n < 4 else self.apply(n - 4)

    def whole(self):
        for n in range(2 * self.tiles + 4):
            last = self.piece(n)
        return last


def self_attention(nc, x, w_lat, b_lat, w_d, b_d, w_proj, b_proj, causal, ident_in, x1):
    scale = 1.0 / math.sqrt(L)
    PK = 3 * P
    with ExitStack() as ctx:
        sems = []

        def sb(name, shape, dt=F32):
            return ctx.enter_context(nc.sbuf_tensor("a_" + name, shape, dt))

        def pb(name, shape):
            return ctx.enter_context(nc.psum_tensor("a_" + name, shape, F32))

        def sem(name):
            sems.append(ctx.enter_context(nc.semaphore("a_" + name)))
            return sems[-1]

        def parts(name, shape):
            return sb(name + "_hi", shape, F32R), sb(name + "_lo", shape, F32R)

        wd = parts("wd", [P, DC, H * L])
        wp = parts("wp", [P, H, D])
        wl = parts("wl", [P, DC, L])
        NRAW = 4
        raw = [sb(f"raw{n}", [P, 2048]) for n in range(NRAW)]
        raw_l = raw[0][:, 0:DC * L].rearrange("p (c n) -> p c n", c=DC)
        bd = sb("bd", [P, H])
        bl = sb("bl", [P, 1])
        bp = sb("bp", [P, D])
        mask = sb("mask", [P, PK])
        ident = sb("ident", [P, P])
        xin = sb("xin", [P, ST, D])
        stats = sb("stats", [P, ST, 8])
        small = sb("small", [P, 4, ST])
        xt = parts("xt", [P, DC, S])
        kt = parts("kt", [P, S])
        kn = parts("kn", [P, ST, L])
        q = [parts(f"q{n}", [P, S]) for n in range(2)]
        pr = [sb(f"pr{n}", [P, PK]) for n in range(2)]
        top = [sb(f"top{n}", [P, ST]) for n in range(2)]
        rsum = [sb(f"rsum{n}", [P, ST]) for n in range(2)]
        rinv = [sb(f"rinv{n}", [P, ST]) for n in range(2)]
        pt = parts("pt", [P, PK])
        y = parts("y", [P, S])
        res = sb("res", [P, ST, D])

        s_ps, t_ps, y_ps = (pb(n, [P, 512]) for n in ("s_ps", "t_ps", "y_ps"))
        o_ps = [pb(f"o_ps{n}", [P, D]) for n in range(ST)]
        x_ps = [pb(f"x_ps{n}", [P, 512]) for n in range(2)]
        q_ps = [pb("q_ps0", [P, 512]), x_ps[1]]

        raw_in = [sem(f"raw_in{n}") for n in range(NRAW)]
        raw_split, raw_split_g, w_hi = sem("raw_split"), sem("raw_split_g"), sem("w_hi")
        const_in = sem("const_in")
        x_in, res_in, stored = sem("x_in"), sem("res_in"), sem("stored")
        ln_chain, xn_ready = sem("ln_chain"), sem("xn_ready")
        xt_mm, xt_hi, xt_lo = sem("xt_mm"), sem("xt_hi"), sem("xt_lo")
        k_mm, k_hi, k_lo = sem("k_mm"), sem("k_hi"), sem("k_lo")
        kn_mm, kn_ready = sem("kn_mm"), sem("kn_ready")
        res_biased, out_ready = sem("res_biased"), sem("out_ready")
        sp_step, v_step = sem("sp_step"), sem("v_step")
        q_mm, q_hi, q_lo = sem("q_mm"), sem("q_hi"), sem("q_lo")
        s_mm, s_masked, p_exp, p_inv, p_norm = sem("s_mm"), sem("s_masked"), sem("p_exp"), sem("p_inv"), sem("p_norm")
        t_mm, pt_hi, pt_lo = sem("t_mm"), sem("pt_hi"), sem("pt_lo")
        y_mm, y_hi, y_lo, o_mm = sem("y_mm"), sem("y_hi"), sem("y_lo"), sem("o_mm")

        def piece(src, dst, width):
            return src, dst[0], dst[1], width

        pieces = [piece(w_lat.rearrange("(c p) n -> p c n", p=P),
                        [w[:, :, :].rearrange("p c n -> p (c n)") for w in wl], DC * L)]
        for c in range(DC):
            pieces.append(piece(w_d[c * P:(c + 1) * P, :], [w[:, c, :] for w in wd], H * L))
        for g in range(0, H, 4):
            pieces.append(piece(w_proj[g * P:(g + 4) * P, :].rearrange("(h p) n -> p h n", p=P),
                                [w[:, g:g + 4, :].rearrange("p h n -> p (h n)") for w in wp], 4 * D))

        by_gpsimd = (3, DC + 2)
        lo_done = []
        for n in range(len(pieces)):
            mine = raw_split_g if n in by_gpsimd else raw_split
            lo_done.append((mine, 1 + sum(s is mine for s, _ in lo_done)))

        def split_lo(eng, n):
            _, hi, lo, width = pieces[n]
            eng.wait_ge(w_hi, n + 1)
            eng.tensor_tensor(lo, raw[n % NRAW][:, 0:width], hi.bitcast(F32), ALU.subtract).then_inc(lo_done[n][0], 1)

        ctx.callback(clear, nc, sems)
        block = ctx.enter_context(nc.Block())

        @block.sync
        def _(sp):
            sp.dma_start(xin[:], x[0].rearrange("(t p) c -> p t c", p=P)).then_inc(x_in, 16)
            sp.dma_start(ident[:], ident_in).then_inc(const_in, 16)
            sp.dma_start(mask[:], causal).then_inc(const_in, 16)
            sp.dma_start(bd[:], b_d).then_inc(const_in, 16)
            sp.dma_start(bl[:], b_lat.rearrange("(p o) -> p o", o=1)).then_inc(const_in, 16)
            sp.dma_start(bp[:], b_proj.rearrange("(o n) -> o n", o=1).to_broadcast([P, D])).then_inc(const_in, 16)
            for n, (src, _, _, width) in enumerate(pieces):
                if n >= NRAW:
                    sp.wait_ge(*lo_done[n - NRAW])
                dst = raw[n % NRAW][:, 0:width]
                if n == 0:
                    dst = raw_l
                elif n > DC:
                    dst = dst.rearrange("p (h n) -> p h n", n=D)
                sp.dma_start(dst, src).then_inc(raw_in[n % NRAW], 16)
            with sp.Fori(0, B) as i:
                val = Values(sp, i)
                now = Batch(val, 0)
                nxt = sp.snap((i + 1) % B)
                xt_read, out_done, out_stored = now.done(2, 2), now.done(1, 1 + SEED), now.done(16, 16)
                hold(sp, xt_mm, xt_read, sp_step)
                sp.dma_start(xin[:], x[bass.ds(nxt, 1)].rearrange("o (t p) c -> p (o t) c", p=P)).then_inc(x_in, 16)
                sp.dma_start(res[:], x[bass.ds(i, 1)].rearrange("o (t p) c -> p (o t) c", p=P)).then_inc(res_in, 16)
                hold(sp, out_ready, out_done, sp_step)
                sp.dma_start(x1[bass.ds(i, 1)].rearrange("o (t p) c -> p (o t) c", p=P), res[:]).then_inc(stored, 16)
                hold(sp, stored, out_stored, sp_step)

        @block.scalar
        def _(act):
            def split(first, last):
                for n in range(first, last):
                    _, hi, _, width = pieces[n]
                    act.wait_ge(raw_in[n % NRAW], 16 * (n // NRAW + 1))
                    act.activation(hi, raw[n % NRAW][:, 0:width], ACT.Copy).then_inc(w_hi, 1)

            act.wait_ge(const_in, 80)
            for s in (q_hi, p_exp, pt_hi, y_hi):
                act.sem_inc(s, SEED)

            def keys(batch):
                for n in range(2):
                    act.wait_ge(xt_mm, batch.done(2, n + 1))
                    act.activation(xt[0][:, 2 * n:2 * n + 2, :].rearrange("p c t -> p (c t)"), x_ps[n][:],
                                   ACT.Copy).then_inc(xt_hi, 1)

            def latent(batch):
                act.wait_ge(k_mm, batch.done(1, 1))
                act.activation(kt[0][:], x_ps[0][:, 0:S], ACT.Identity, bias=bl[:]).then_inc(k_hi, 1)

            def latent_rows(batch):
                act.wait_ge(kn_mm, batch.done(1, 1))
                for n in range(2):
                    last = act.activation(kn[n][:].rearrange("p t l -> p (t l)"), x_ps[0][:, n * S:(n + 1) * S],
                                          ACT.Copy)
                last.then_inc(kn_ready, 1)

            def query(unit, h, head):
                act.wait_ge(q_mm, unit.done(h))
                act.activation(q[h % 2][0][:], q_ps[h % 2][:, 0:S], ACT.Identity,
                               bias=bd[:, head:head + 1]).then_inc(q_hi, 1)

            def exps(unit, h):
                act.wait_ge(s_masked, unit.done(h))
                n = h % 2
                act.activation(pr[n][:, 0:P], pr[n][:, 0:P], ACT.Exp, bias=top[n][:, 0:1], scale=-1.0,
                               accum_out=rsum[n][:, 0:1])
                act.activation(pr[n][:, P:PK], pr[n][:, P:PK], ACT.Exp, bias=top[n][:, 1:2], scale=-1.0,
                               accum_out=rsum[n][:, 1:2]).then_inc(p_exp, 1)

            def probs_t(unit, h):
                act.wait_ge(t_mm, unit.done(h))
                act.activation(pt[0][:], t_ps[:, 0:PK], ACT.Copy).then_inc(pt_hi, 1)

            def mixed(unit, h):
                act.wait_ge(y_mm, unit.done(h))
                act.activation(y[0][:], y_ps[:, 0:S], ACT.Copy).then_inc(y_hi, 1)

            first, unit = Batch(Values(act), 0), Unit(Values(act))
            split(0, 3)
            keys(first)
            split(3, 1 + DC)
            latent(first)
            query(unit, 0, 0)
            query(unit, 1, 1)
            split(1 + DC, 3 + DC)
            exps(unit, 0)
            latent_rows(first)
            split(3 + DC, len(pieces))
            with act.Fori(0, B) as i:
                val = Values(act, i)
                unit, nxt = Unit(val), Batch(val, 1)
                probs_t(unit, 0)
                exps(unit, 1)
                query(unit, 2, 2)
                mixed(unit, 0)
                for h in range(1, H - 2):
                    query(unit, h + 2, h + 2)
                    probs_t(unit, h)
                    exps(unit, h + 1)
                    mixed(unit, h)
                keys(nxt)
                probs_t(unit, H - 2)
                exps(unit, H - 1)
                mixed(unit, H - 2)
                latent(nxt)
                probs_t(unit, H - 1)
                query(unit, H, 0)
                mixed(unit, H - 1)
                exps(unit, H)
                query(unit, H + 1, 1)
                latent_rows(nxt)

        @block.vector
        def _(v):
            def split(first, last):
                for n in range(first, last):
                    if n not in by_gpsimd:
                        split_lo(v, n)

            v.wait_ge(const_in, 80)
            for s in (q_lo, s_masked, p_inv, p_norm, pt_lo, y_lo, out_ready, ln_chain):
                v.sem_inc(s, SEED)

            def norm(batch):
                v.wait_ge(x_in, batch.done(16, 16))
                return LayerNorm(v, xin, stats, small, ln_chain, lambda k: batch.done(LN_LINKS, k + SEED), v_step)

            def keys(batch, n):
                v.wait_ge(xt_hi, batch.done(2, n + 1))
                half = slice(2 * n, 2 * n + 2)
                v.tensor_tensor(xt[1][:, half, :].rearrange("p c t -> p (c t)"), x_ps[n][:],
                                xt[0][:, half, :].rearrange("p c t -> p (c t)").bitcast(F32),
                                ALU.subtract).then_inc(xt_lo, 1)

            def latent(batch):
                v.wait_ge(k_hi, batch.done(1, 1))
                v.scalar_tensor_tensor(kt[1][:], x_ps[0][:, 0:S], bl[:], kt[0][:].bitcast(F32), ALU.add,
                                       ALU.subtract).then_inc(k_lo, 1)

            def query(unit, h, head):
                v.wait_ge(q_hi, unit.done(h))
                v.scalar_tensor_tensor(q[h % 2][1][:], q_ps[h % 2][:, 0:S], bd[:, head:head + 1],
                                       q[h % 2][0][:].bitcast(F32), ALU.add, ALU.subtract).then_inc(q_lo, 1)

            def masked(unit, h):
                n = h % 2
                hold(v, s_mm, unit.done(h), v_step)
                v.tensor_tensor_reduce(out=pr[n][:, 0:P], in0=s_ps[:, 0:P], in1=mask[:, 0:P], scale=-scale, scalar=3e38,
                                       op0=ALU.add, op1=ALU.min, accum_out=top[n][:, 0:1])
                v.tensor_tensor_reduce(out=pr[n][:, P:PK], in0=s_ps[:, P:PK], in1=mask[:, P:PK], scale=-scale,
                                       scalar=3e38, op0=ALU.add, op1=ALU.min,
                                       accum_out=top[n][:, 1:2]).then_inc(s_masked, 1)

            def normalize(unit, h):
                n = h % 2
                v.wait_ge(p_exp, unit.done(h))
                v.reciprocal(rinv[n][:], rsum[n][:]).then_inc(p_inv, 1)
                v.wait_ge(p_inv, unit.done(h))
                v.tensor_scalar(pr[n][:, 0:P], pr[n][:, 0:P], rinv[n][:, 0:1], None, ALU.mult)
                v.tensor_scalar(pr[n][:, P:PK], pr[n][:, P:PK], rinv[n][:, 1:2], None, ALU.mult).then_inc(p_norm, 1)

            def probs_t(unit, h):
                v.wait_ge(pt_hi, unit.done(h))
                v.tensor_tensor(pt[1][:], t_ps[:, 0:PK], pt[0][:].bitcast(F32), ALU.subtract).then_inc(pt_lo, 1)

            def mixed(unit, h):
                v.wait_ge(y_hi, unit.done(h))
                v.tensor_tensor(y[1][:], y_ps[:, 0:S], y[0][:].bitcast(F32), ALU.subtract).then_inc(y_lo, 1)

            first, unit = Batch(Values(v), 0), Unit(Values(v))
            norm(first).whole().then_inc(xn_ready, 1)
            split(0, 3)
            keys(first, 0)
            keys(first, 1)
            split(3, 1 + DC)
            latent(first)
            query(unit, 0, 0)
            query(unit, 1, 1)
            masked(unit, 0)
            split(1 + DC, 3 + DC)
            normalize(unit, 0)
            split(3 + DC, len(pieces))
            with v.Fori(0, B) as i:
                val = Values(v, i)
                unit, now, nxt = Unit(val), Batch(val, 0), Batch(val, 1)
                masked(unit, 1)
                probs_t(unit, 0)
                query(unit, 2, 2)
                normalize(unit, 1)
                mixed(unit, 0)
                for h in range(1, H - 2):
                    query(unit, h + 2, h + 2)
                    probs_t(unit, h)
                    masked(unit, h + 1)
                    if h == NORM_AT:
                        next_norm = norm(nxt)
                    if 0 <= h - NORM_AT < LayerNorm.PIECES:
                        last = next_norm.piece(h - NORM_AT)
                    normalize(unit, h + 1)
                    mixed(unit, h)
                last.then_inc(xn_ready, 1)
                keys(nxt, 0)
                probs_t(unit, H - 2)
                masked(unit, H - 1)
                keys(nxt, 1)
                normalize(unit, H - 1)
                mixed(unit, H - 2)
                latent(nxt)
                probs_t(unit, H - 1)
                query(unit, H, 0)
                mixed(unit, H - 1)
                masked(unit, H)
                query(unit, H + 1, 1)
                normalize(unit, H)
                v.wait_ge(res_biased, now.done(1, 1))
                v.wait_ge(o_mm, unit.done(H - 1))
                for t in range(ST):
                    last = v.tensor_tensor(res[:, t, :], o_ps[t][:], res[:, t, :], ALU.add)
                last.then_inc(out_ready, 1)

        @block.gpsimd
        def _(g):
            for n in by_gpsimd:
                split_lo(g, n)
            g.wait_ge(const_in, 80)
            with g.Fori(0, B) as i:
                now = Batch(Values(g, i), 0)
                g.wait_ge(res_in, now.done(16, 16))
                for t in range(ST):
                    last = g.tensor_tensor(res[:, t, :], res[:, t, :], bp[:], ALU.add)
                last.then_inc(res_biased, 1)

        @block.tensor
        def _(pe):
            pe.wait_ge(const_in, 80)
            for s in (q_mm, s_mm, t_mm, y_mm, o_mm):
                pe.sem_inc(s, SEED)

            def transposed_norm(batch):
                pe.wait_ge(xn_ready, batch.done(1, 1))
                for c in range(DC):
                    for t in range(ST):
                        at = (c % 2) * S + t * P
                        last = pe.transpose(x_ps[c // 2][:, at:at + P], xin[:, t, c * P:(c + 1) * P], ident[:])
                    if c % 2:
                        last.then_inc(xt_mm, 1)

            def latent(batch):
                pe.wait_ge(xt_lo, batch.done(2, 2))
                for c in range(DC):
                    last = product(pe, x_ps[0][:, 0:S], [w[:, c, :] for w in wl], [w[:, c, :] for w in xt],
                                   c == 0, c == DC - 1)
                last.then_inc(k_mm, 1)

            def latent_rows(batch):
                for n in range(2):
                    for t in range(ST):
                        at = n * S + t * P
                        last = pe.transpose(x_ps[0][:, at:at + P], kt[n][:, t * P:(t + 1) * P].bitcast(F32), ident[:])
                last.then_inc(kn_mm, 1)

            def query(unit, h, head):
                pe.wait_ge(q_lo, unit.done(h - 2))
                for c in range(DC):
                    last = product(pe, q_ps[h % 2][:, 0:S], [w[:, c, head * L:(head + 1) * L] for w in wd],
                                   [w[:, c, :] for w in xt], c == 0, c == DC - 1)
                last.then_inc(q_mm, 1)

            def scores(unit, h):
                n = h % 2
                pe.wait_ge(s_masked, unit.done(h - 1))
                pe.wait_ge(q_lo, unit.done(h))
                product(pe, s_ps[:, 0:P], [w[:, 0:P] for w in q[n]], [w[:, 0:P] for w in kt], True, True)
                product(pe, s_ps[:, P:PK], [w[:, P:S] for w in q[n]], [w[:, :] for w in kt], True,
                        True).then_inc(s_mm, 1)

            def probs_t(unit, h):
                n = h % 2
                pe.wait_ge(pt_lo, unit.done(h - 1))
                pe.wait_ge(p_norm, unit.done(h))
                for c in range(3):
                    last = pe.transpose(t_ps[:, c * P:(c + 1) * P], pr[n][:, c * P:(c + 1) * P], ident[:])
                last.then_inc(t_mm, 1)

            def mixed(unit, h):
                pe.wait_ge(y_lo, unit.done(h - 1))
                pe.wait_ge(pt_lo, unit.done(h))
                product(pe, y_ps[:, 0:S], [w[:, 0, :] for w in kn], [w[:, 0:S] for w in pt], True, False)
                product(pe, y_ps[:, P:S], [w[:, 1, :] for w in kn], [w[:, S:PK] for w in pt], False,
                        True).then_inc(y_mm, 1)

            def projected(unit, h):
                pe.wait_ge(y_lo, unit.done(h))
                for t in range(ST):
                    last = product(pe, o_ps[t][:], [w[:, t * P:(t + 1) * P] for w in y], [w[:, h, :] for w in wp],
                                   h == 0, h == H - 1)
                last.then_inc(o_mm, 1)

            first, unit = Batch(Values(pe), 0), Unit(Values(pe))
            transposed_norm(first)
            pe.wait_ge(*lo_done[0])
            latent(first)
            pe.wait_ge(*lo_done[3])
            pe.wait_ge(*lo_done[DC])
            query(unit, 0, 0)
            query(unit, 1, 1)
            pe.wait_ge(k_lo, 1)
            scores(unit, 0)
            latent_rows(first)
            pe.wait_ge(*lo_done[DC + 2])
            pe.wait_ge(*lo_done[DC + 4])
            with pe.Fori(0, B) as i:
                val = Values(pe, i)
                unit, now, nxt = Unit(val), Batch(val, 0), Batch(val, 1)
                scores(unit, 1)
                probs_t(unit, 0)
                query(unit, 2, 2)
                pe.wait_ge(kn_ready, now.done(1, 1))
                mixed(unit, 0)
                for h in range(1, H - 2):
                    query(unit, h + 2, h + 2)
                    probs_t(unit, h)
                    scores(unit, h + 1)
                    if h == 1:
                        pe.wait_ge(out_ready, now.done(1, SEED))
                    projected(unit, h - 1)
                    mixed(unit, h)
                pe.wait_ge(q_lo, unit.done(H - 1))
                transposed_norm(nxt)
                probs_t(unit, H - 2)
                scores(unit, H - 1)
                projected(unit, H - 3)
                mixed(unit, H - 2)
                latent(nxt)
                probs_t(unit, H - 1)
                query(unit, H, 0)
                projected(unit, H - 2)
                mixed(unit, H - 1)
                pe.wait_ge(k_lo, nxt.done(1, 1))
                scores(unit, H)
                query(unit, H + 1, 1)
                projected(unit, H - 1)
                latent_rows(nxt)


def cross_attention(nc, x1, ctx_t, seg_cols, w_kvc, w_dq, uq_t, w_qr, uk_t, kr_uv, uv_t, w_o, trig, rot_cs, key_ids,
                    ident_in, x2):
    scale = 1.0 / math.sqrt(L + R)
    with ExitStack() as outer:
        def osb(name, shape, dt=F32):
            return outer.enter_context(nc.sbuf_tensor("b_" + name, shape, dt))

        def oparts(name, shape):
            return osb(name + "_hi", shape, F32R), osb(name + "_lo", shape, F32R)

        QT = QC - P

        def stacked(name):
            return osb(name + "_hi", [P, QCC, H * L], F32R), osb(name + "_lo", [P, H * L], F32R)

        wa = stacked("wa")
        wr = stacked("wr")
        wvo = oparts("wvo", [P, H, D])
        wdq = oparts("wdq", [P, DC, QCC * P])
        wkv = oparts("wkv", [P, DC, L])
        wkr = oparts("wkr", [P, 2, 2 * R])

        ident, qtrig = osb("ident", [P, P]), osb("qtrig", [P, S])
        kcos, ksin, ids = osb("kcos", [P, S]), osb("ksin", [P, S]), osb("ids", [P, S])
        segi = osb("segi", [P, B * ST], I32)
        xin, ctr = osb("xin", [P, ST, D]), osb("ctr", [P, DC, S])

        def rows_of(array, b):
            return array[b].rearrange("o (t p) c -> p (o t) c", p=P)

        def context_of(b):
            return ctx_t[b].rearrange("o (c p) t -> p (o c) t", p=P)

        with ExitStack() as ctx:
            sems = []

            def sb(name, shape, dt=F32):
                return ctx.enter_context(nc.sbuf_tensor("bw_" + name, shape, dt))

            def sem(name):
                sems.append(ctx.enter_context(nc.semaphore("bw_" + name)))
                return sems[-1]

            r_uq, r_uk, r_uv = sb("uq", [P, H, QCC * P]), sb("uk", [P, H, L]), sb("uv", [P, H, L])
            r_o = [sb(f"o{n}", [P, 4, D]) for n in range(2)]
            r_dq, r_kv, r_kr = sb("dq", [P, DC, QC]), sb("kv", [P, DC, L]), sb("kr", [P, 2, 2 * R])
            r_qr = sb("qr", [P, QCC, H * R])
            fold_ps = [ctx.enter_context(nc.psum_tensor(f"bw_ps{n}", [P, 512], F32)) for n in range(4)]
            plain_in, up_in, uv_in, start_in = sem("plain_in"), sem("up_in"), sem("uv_in"), sem("start_in")
            o_in = [sem(f"o_in{n}") for n in range(2)]
            plain_hi, fold_mm, fold_hi, fold_lo = (
                sem("plain_hi"), sem("fold_mm"), sem("fold_hi"), sem("fold_lo"))

            ctx.callback(clear, nc, sems)
            block = ctx.enter_context(nc.Block())

            def chunks(w, cols):
                low = w[0][QT:P, 1, cols]
                return [(slice(0, P), w[0][:, 0, cols], w[0][:, 0, cols], w[1][:, cols]),
                        (slice(QT, P), w[0][:, 1, cols], low, low)]

            plain = [(raw[:], slice(0, P), w[0][:], w[0][:], w[1][:]) for raw, w in ((r_kv, wkv), (r_kr, wkr))]
            for src, dst in ((slice(0, QC), slice(0, QC)), (slice(P, QC), slice(QC, QCC * P))):
                hi, lo = wdq[0][:, :, dst], wdq[1][:, :, dst]
                plain.append((r_dq[:, :, src], slice(0, P), hi, hi, lo))

            def doubled(a, copy):
                return a.rearrange("p (h two r) -> p h two r", two=2, r=R)[:, :, copy, :]

            for c, (rows, hi, hi_lo, lo) in enumerate(chunks(wr, slice(0, H * L))):
                for copy in range(2):
                    plain.append((r_qr[:, c, :].rearrange("p (h r) -> p h r", r=R), rows,
                                  *[doubled(a, copy) for a in (hi, hi_lo, lo)]))
            folded = []
            for g in range(H // 4):
                for part in chunks(wa, slice(g * 4 * L, (g + 1) * 4 * L)):
                    folded.append((fold_ps[len(folded) % 4][:], *part))
            for h in range(H):
                folded.append((fold_ps[len(folded) % 4][:], slice(0, P), wvo[0][:, h, :], wvo[0][:, h, :],
                               wvo[1][:, h, :]))

            @block.sync
            def _(sp):
                sp.dma_start(r_kv[:], w_kvc.rearrange("(c p) n -> p c n", p=P)).then_inc(plain_in, 16)
                sp.dma_start(r_kr[:], kr_uv).then_inc(plain_in, 16)
                sp.dma_start(r_dq[:], w_dq.rearrange("(c p) n -> p c n", p=P)).then_inc(plain_in, 16)
                sp.dma_start(r_qr[:, 0, :], w_qr[0:P, :]).then_inc(plain_in, 16)
                sp.dma_start(r_qr[0:QT, 1, :], w_qr[P:QC, :]).then_inc(plain_in, 16)
                sp.dma_start(r_qr[QT:P, 1, :], w_qr[P:QC, :]).then_inc(plain_in, 16)
                sp.dma_start(r_uq[:, :, 0:QC], uq_t.rearrange("(h p) n -> p h n", p=P)).then_inc(up_in, 16)
                sp.dma_start(r_uq[:, :, QC:], uq_t[:, P:QC].rearrange("(h p) n -> p h n", p=P)).then_inc(up_in, 16)
                sp.dma_start(r_uk[:], uk_t.rearrange("(h p) n -> p h n", p=P)).then_inc(up_in, 16)
                sp.dma_start(r_uv[:], uv_t.rearrange("(h p) n -> p h n", p=P)).then_inc(uv_in, 16)
                for g in range(H // 4):
                    if g >= 2:
                        sp.wait_ge(fold_mm, 8 + 4 * (g - 1))
                    sp.dma_start(r_o[g % 2][:], w_o[g * 4 * L:(g + 1) * 4 * L, :].rearrange(
                        "(h p) n -> p h n", p=P)).then_inc(o_in[g % 2], 16)
                    if g == 1:
                        sp.dma_start(xin[:], rows_of(x1, slice(0, 1))).then_inc(start_in, 16)
                        sp.dma_start(ctr[:], context_of(slice(0, 1))).then_inc(start_in, 16)
                        for dst, src in ((segi, seg_cols), (ident, ident_in), (qtrig, trig), (kcos, rot_cs[0]),
                                         (ksin, rot_cs[1]), (ids, key_ids)):
                            sp.dma_start(dst[:], src).then_inc(start_in, 16)
                sp.wait_ge(start_in, 16 * 8)

            @block.scalar
            def _(act):
                act.wait_ge(plain_in, 96)
                for raw, _, hi, _, _ in plain:
                    act.activation(hi, raw, ACT.Copy).then_inc(plain_hi, 1)
                for n, (bank, _, hi, _, _) in enumerate(folded):
                    act.wait_ge(fold_mm, n + 1)
                    act.activation(hi, bank, ACT.Copy).then_inc(fold_hi, 1)

            @block.vector
            def _(v):
                v.wait_ge(plain_in, 96)
                for n, (raw, rows, _, hi, lo) in enumerate(plain):
                    v.wait_ge(plain_hi, n + 1)
                    v.tensor_tensor(lo, raw[rows], hi.bitcast(F32), ALU.subtract)
                for n, (bank, rows, _, hi, lo) in enumerate(folded):
                    v.wait_ge(fold_hi, n + 1)
                    v.tensor_tensor(lo, bank[rows], hi.bitcast(F32), ALU.subtract).then_inc(fold_lo, 1)

            @block.tensor
            def _(pe):
                pe.wait_ge(up_in, 48)
                n = 0
                for g in range(H // 4):
                    for c in range(QCC):
                        if n >= 4:
                            pe.wait_ge(fold_lo, n - 3)
                        for k in range(4):
                            last = pe.matmul(fold_ps[n % 4][:, k * L:(k + 1) * L],
                                             r_uq[:, 4 * g + k, c * P:(c + 1) * P], r_uk[:, 4 * g + k, :],
                                             start=True, stop=True)
                        last.then_inc(fold_mm, 1)
                        n += 1
                pe.wait_ge(uv_in, 16)
                for h in range(H):
                    pe.wait_ge(fold_lo, n - 3)
                    if h % 4 == 0:
                        pe.wait_ge(o_in[(h // 4) % 2], 16 * (h // 8 + 1))
                    pe.matmul(fold_ps[n % 4][:], r_uv[:, h, :], r_o[(h // 4) % 2][:, h % 4, :], start=True,
                              stop=True).then_inc(fold_mm, 1)
                    n += 1

        with ExitStack() as ctx:
            sems = []

            def sb(name, shape, dt=F32):
                return ctx.enter_context(nc.sbuf_tensor("b_" + name, shape, dt))

            def pb(name, shape):
                return ctx.enter_context(nc.psum_tensor("b_" + name, shape, F32))

            def sem(name):
                sems.append(ctx.enter_context(nc.semaphore("b_" + name)))
                return sems[-1]

            def parts(name, shape):
                return sb(name + "_hi", shape, F32R), sb(name + "_lo", shape, F32R)

            segf, segmid = sb("segf", [P, B * ST]), sb("segmid", [P, B * ST])
            seg_b = sb("seg_b", [P, ST])
            mask, mask_next = sb("mask", [P, ST, S], BF16), sb("mask_next", [P, ST, S], BF16)
            res = sb("res", [P, ST, D])
            stats, small = sb("stats", [P, ST, 8]), sb("small", [P, 4, ST])
            xt, ct, qc = parts("xt", [P, DC, S]), parts("ct", [P, DC, S]), parts("qc", [P, QCC, S])
            kt, kr, kn = parts("kt", [P, S]), parts("kr", [P, S]), parts("kn", [P, ST, L])
            q = [parts(f"q{n}", [P, S]) for n in range(2)]
            qr = [parts(f"qr{n}", [P, S]) for n in range(2)]
            tq = [sb(f"tq{n}", [P, S]) for n in range(2)]
            pr = [sb(f"pr{n}", [P, ST, S]) for n in range(2)]
            kr1, kr2 = pr[0][:, 0, :], pr[0][:, 1, :]
            top = [sb(f"top{n}", [P, ST]) for n in range(2)]
            rsum = [sb(f"rsum{n}", [P, ST]) for n in range(2)]
            rinv = [sb(f"rinv{n}", [P, ST]) for n in range(2)]
            pt, z = parts("pt", [P, ST, S]), parts("z", [P, S])

            qa_ps, qr_ps, s_ps, t_ps, z_ps, x_ps = (pb(n, [P, 512]) for n in ("qa_ps", "qr_ps", "s_ps", "t_ps", "z_ps",
                                                                              "x_ps"))
            o_ps = [pb(f"o_ps{n}", [P, D]) for n in range(ST)]

            MASK_AT, CONTEXT_AT = 1, H // 2

            seg_float, seg_ready = sem("seg_float"), sem("seg_ready")
            x_in, res_in, ctx_in, stored = sem("x_in"), sem("res_in"), sem("ctx_in"), sem("stored")
            ct_hi, ct_lo = sem("ct_hi"), sem("ct_lo")
            seg_copied, distance, squared, mask_made, mask_moved = (
                sem("seg_copied"), sem("distance"), sem("squared"), sem("mask_made"), sem("mask_moved"))
            ln_chain, xn_ready = sem("ln_chain"), sem("xn_ready")
            xt_mm, xt_hi, xt_lo = sem("xt_mm"), sem("xt_hi"), sem("xt_lo")
            qc_mm, qc_hi, qc_lo = sem("qc_mm"), sem("qc_hi"), sem("qc_lo")
            k_mm, k_hi, k_lo = sem("k_mm"), sem("k_hi"), sem("k_lo")
            kr_mm, kr_prod, kr_sum, kr_hi, kr_lo = (sem("kr_mm"), sem("kr_prod"), sem("kr_sum"), sem("kr_hi"),
                                                    sem("kr_lo"))
            kn_mm, kn_ready = sem("kn_mm"), sem("kn_ready")
            out_ready = sem("out_ready")
            sp_step, v_step, g_step = sem("sp_step"), sem("v_step"), sem("g_step")
            qa_mm, qa_hi, qa_lo = sem("qa_mm"), sem("qa_hi"), sem("qa_lo")
            qr_mm, qr_rot, qr_hi, qr_lo = sem("qr_mm"), sem("qr_rot"), sem("qr_hi"), sem("qr_lo")
            s_mm, s_masked, p_exp, p_inv, p_norm = (sem("s_mm"), sem("s_masked"), sem("p_exp"), sem("p_inv"),
                                                    sem("p_norm"))
            t_mm, pt_hi, pt_lo = sem("t_mm"), sem("pt_hi"), sem("pt_lo")
            z_mm, z_hi, z_lo, o_mm = sem("z_mm"), sem("z_hi"), sem("z_lo"), sem("o_mm")

            ctx.callback(clear, nc, sems)
            block = ctx.enter_context(nc.Block())

            @block.sync
            def _(sp):
                for s in (x_in, ctx_in):
                    sp.sem_inc(s, 16)
                with sp.Fori(0, B) as i:
                    val = Values(sp, i)
                    now = Batch(val, 0)
                    nxt = sp.snap((i + 1) % B)
                    one, out_done, out_stored = now.done(1, 1), now.done(1, 1 + SEED), now.done(16, 16)
                    hold(sp, xt_mm, now.done(2, 2), sp_step)
                    sp.dma_start(xin[:], rows_of(x1, bass.ds(nxt, 1))).then_inc(x_in, 16)
                    hold(sp, ct_lo, one, sp_step)
                    sp.dma_start(ctr[:], context_of(bass.ds(nxt, 1))).then_inc(ctx_in, 16)
                    sp.dma_start(res[:], rows_of(x1, bass.ds(i, 1))).then_inc(res_in, 16)
                    hold(sp, out_ready, out_done, sp_step)
                    sp.dma_start(rows_of(x2, bass.ds(i, 1)), res[:]).then_inc(stored, 16)
                    hold(sp, stored, out_stored, sp_step)

            @block.scalar
            def _(act):
                for s in (qa_hi, qr_hi, p_exp, pt_hi, z_hi):
                    act.sem_inc(s, SEED)

                def context(batch):
                    act.wait_ge(ctx_in, batch.done(16, 16))
                    act.activation(ct[0][:], ctr[:], ACT.Copy).then_inc(ct_hi, 1)

                def norm_t(batch, n):
                    act.wait_ge(xt_mm, batch.done(2, n + 1))
                    act.activation(xt[0][:, 2 * n:2 * n + 2, :].rearrange("p c t -> p (c t)"), x_ps[:],
                                   ACT.Copy).then_inc(xt_hi, 1)

                def latent(batch):
                    act.wait_ge(k_mm, batch.done(1, 1))
                    act.activation(kt[0][:], qa_ps[:, 0:S], ACT.Copy).then_inc(k_hi, 1)

                def query_latent(batch):
                    act.wait_ge(qc_mm, batch.done(1, 1))
                    act.activation(qc[0][:].rearrange("p c t -> p (c t)"), qr_ps[:], ACT.Copy).then_inc(qc_hi, 1)

                def rotated_keys(batch):
                    act.wait_ge(kr_sum, batch.done(1, 1))
                    act.activation(kr[0][:], kr1, ACT.Copy).then_inc(kr_hi, 1)

                def latent_rows(batch):
                    act.wait_ge(kn_mm, batch.done(1, 1))
                    for n in range(2):
                        last = act.activation(kn[n][:].rearrange("p t l -> p (t l)"), x_ps[:, n * S:(n + 1) * S],
                                              ACT.Copy)
                    last.then_inc(kn_ready, 1)

                def query(unit, h):
                    act.wait_ge(qr_rot, unit.done(h))
                    act.activation(qr[h % 2][0][:], tq[h % 2][:], ACT.Copy).then_inc(qr_hi, 1)
                    act.wait_ge(qa_mm, unit.done(h))
                    act.activation(q[h % 2][0][:], qa_ps[:, 0:S], ACT.Copy).then_inc(qa_hi, 1)

                def exps(unit, h):
                    act.wait_ge(s_masked, unit.done(h))
                    n = h % 2
                    for t in range(ST):
                        last = act.activation(pr[n][:, t, :], pr[n][:, t, :], ACT.Exp, bias=top[n][:, t:t + 1],
                                              scale=-1.0, accum_out=rsum[n][:, t:t + 1])
                    last.then_inc(p_exp, 1)

                def probs_t(unit, h):
                    act.wait_ge(t_mm, unit.done(h))
                    act.activation(pt[0][:].rearrange("p k t -> p (k t)"), t_ps[:], ACT.Copy).then_inc(pt_hi, 1)

                def mixed(unit, h):
                    act.wait_ge(z_mm, unit.done(h))
                    act.activation(z[0][:], z_ps[:, 0:S], ACT.Copy).then_inc(z_hi, 1)

                first, unit = Batch(Values(act), 0), Unit(Values(act))
                context(first)
                norm_t(first, 0)
                norm_t(first, 1)
                latent(first)
                query_latent(first)
                rotated_keys(first)
                query(unit, 0)
                query(unit, 1)
                exps(unit, 0)
                latent_rows(first)
                with act.Fori(0, B) as i:
                    val = Values(act, i)
                    unit, nxt = Unit(val), Batch(val, 1)
                    for h in range(H - 2):
                        probs_t(unit, h)
                        exps(unit, h + 1)
                        query(unit, h + 2)
                        mixed(unit, h)
                        if h == CONTEXT_AT:
                            context(nxt)
                    norm_t(nxt, 0)
                    act.wait_ge(s_mm, unit.done(H - 1))
                    latent(nxt)
                    probs_t(unit, H - 2)
                    norm_t(nxt, 1)
                    exps(unit, H - 1)
                    query_latent(nxt)
                    mixed(unit, H - 2)
                    probs_t(unit, H - 1)
                    query(unit, H)
                    rotated_keys(nxt)
                    mixed(unit, H - 1)
                    query(unit, H + 1)
                    exps(unit, H)
                    latent_rows(nxt)

            @block.vector
            def _(v):
                for s in (qa_lo, qr_rot, s_masked, p_inv, p_norm, pt_lo, z_lo, out_ready, ln_chain):
                    v.sem_inc(s, SEED)
                v.tensor_copy(segf[:], segi[:]).then_inc(seg_float, 1)
                v.wait_ge(seg_float, 1)
                v.tensor_scalar(segmid[:], segf[:], -float(LOOKBACK // 2), None, ALU.add).then_inc(seg_ready, 1)

                def norm(batch):
                    v.wait_ge(x_in, batch.done(16, 16))
                    return LayerNorm(v, xin, stats, small, ln_chain, lambda k: batch.done(LN_LINKS, k + SEED), v_step)

                def norm_t(batch, n):
                    v.wait_ge(xt_hi, batch.done(2, n + 1))
                    half = slice(2 * n, 2 * n + 2)
                    v.tensor_tensor(xt[1][:, half, :].rearrange("p c t -> p (c t)"), x_ps[:],
                                    xt[0][:, half, :].rearrange("p c t -> p (c t)").bitcast(F32),
                                    ALU.subtract).then_inc(xt_lo, 1)

                def latent(batch):
                    v.wait_ge(k_hi, batch.done(1, 1))
                    v.tensor_tensor(kt[1][:], qa_ps[:, 0:S], kt[0][:].bitcast(F32), ALU.subtract).then_inc(k_lo, 1)

                def query_latent(batch):
                    v.wait_ge(qc_hi, batch.done(1, 1))
                    v.tensor_tensor(qc[1][:].rearrange("p c t -> p (c t)"), qr_ps[:],
                                    qc[0][:].rearrange("p c t -> p (c t)").bitcast(F32),
                                    ALU.subtract).then_inc(qc_lo, 1)

                def rotated_keys(batch):
                    v.wait_ge(kr_mm, batch.done(1, 1))
                    v.tensor_tensor(kr1, x_ps[:, 0:S], kcos[:], ALU.mult)
                    v.tensor_tensor(kr2, x_ps[:, S:], ksin[:], ALU.mult).then_inc(kr_prod, 1)
                    v.wait_ge(kr_prod, batch.done(1, 1))
                    v.tensor_tensor(kr1, kr1, kr2, ALU.add).then_inc(kr_sum, 1)

                def rotated_keys_lo(batch):
                    v.wait_ge(kr_hi, batch.done(1, 1))
                    v.tensor_tensor(kr[1][:], kr1, kr[0][:].bitcast(F32), ALU.subtract).then_inc(kr_lo, 1)

                def new_mask(batch):
                    v.wait_ge(mask_made, batch.done(1, 1))
                    v.tensor_copy(mask[:], mask_next[:]).then_inc(mask_moved, 1)

                def rotated(unit, h):
                    v.wait_ge(qr_mm, unit.done(h))
                    v.tensor_tensor(tq[h % 2][:], qr_ps[:, 0:S], qtrig[:], ALU.mult).then_inc(qr_rot, 1)

                def query(unit, h):
                    v.wait_ge(qa_hi, unit.done(h))
                    v.tensor_tensor(q[h % 2][1][:], qa_ps[:, 0:S], q[h % 2][0][:].bitcast(F32),
                                    ALU.subtract).then_inc(qa_lo, 1)

                def masked(unit, h):
                    n = h % 2
                    hold(v, s_mm, unit.done(h), v_step)
                    for t in range(ST):
                        last = v.tensor_tensor_reduce(out=pr[n][:, t, :], in0=s_ps[:, t * S:(t + 1) * S],
                                                      in1=mask[:, t, :], scale=-scale, scalar=3e38, op0=ALU.add,
                                                      op1=ALU.min, accum_out=top[n][:, t:t + 1])
                    last.then_inc(s_masked, 1)

                def normalize(unit, h):
                    n = h % 2
                    v.wait_ge(p_exp, unit.done(h))
                    v.reciprocal(rinv[n][:], rsum[n][:]).then_inc(p_inv, 1)
                    v.wait_ge(p_inv, unit.done(h))
                    for t in range(ST):
                        last = v.tensor_scalar(pr[n][:, t, :], pr[n][:, t, :], rinv[n][:, t:t + 1], None, ALU.mult)
                    last.then_inc(p_norm, 1)

                def probs_t(unit, h):
                    v.wait_ge(pt_hi, unit.done(h))
                    v.tensor_tensor(pt[1][:].rearrange("p k t -> p (k t)"), t_ps[:],
                                    pt[0][:].rearrange("p k t -> p (k t)").bitcast(F32),
                                    ALU.subtract).then_inc(pt_lo, 1)

                def mixed(unit, h):
                    v.wait_ge(z_hi, unit.done(h))
                    v.tensor_tensor(z[1][:], z_ps[:, 0:S], z[0][:].bitcast(F32), ALU.subtract).then_inc(z_lo, 1)

                first, unit = Batch(Values(v), 0), Unit(Values(v))
                norm(first).whole().then_inc(xn_ready, 1)
                norm_t(first, 0)
                norm_t(first, 1)
                latent(first)
                query_latent(first)
                rotated_keys(first)
                rotated_keys_lo(first)
                rotated(unit, 0)
                query(unit, 0)
                rotated(unit, 1)
                query(unit, 1)
                new_mask(first)
                v.wait_ge(mask_moved, 1)
                masked(unit, 0)
                normalize(unit, 0)
                with v.Fori(0, B) as i:
                    val = Values(v, i)
                    unit, now, nxt = Unit(val), Batch(val, 0), Batch(val, 1)
                    for h in range(H - 2):
                        masked(unit, h + 1)
                        rotated(unit, h + 2)
                        probs_t(unit, h)
                        query(unit, h + 2)
                        normalize(unit, h + 1)
                        if h == NORM_AT:
                            next_norm = norm(nxt)
                        if 0 <= h - NORM_AT < LayerNorm.PIECES:
                            last = next_norm.piece(h - NORM_AT)
                        mixed(unit, h)
                    last.then_inc(xn_ready, 1)
                    norm_t(nxt, 0)
                    masked(unit, H - 1)
                    latent(nxt)
                    probs_t(unit, H - 2)
                    norm_t(nxt, 1)
                    normalize(unit, H - 1)
                    query_latent(nxt)
                    mixed(unit, H - 2)
                    probs_t(unit, H - 1)
                    rotated(unit, H)
                    rotated_keys(nxt)
                    query(unit, H)
                    rotated_keys_lo(nxt)
                    new_mask(nxt)
                    mixed(unit, H - 1)
                    v.wait_ge(mask_moved, nxt.done(1, 1))
                    masked(unit, H)
                    rotated(unit, H + 1)
                    query(unit, H + 1)
                    normalize(unit, H)
                    v.wait_ge(res_in, now.done(16, 16))
                    v.wait_ge(o_mm, unit.done(H - 1))
                    for t in range(ST):
                        last = v.tensor_tensor(res[:, t, :], o_ps[t][:], res[:, t, :], ALU.add)
                    last.then_inc(out_ready, 1)

            @block.gpsimd
            def _(g):
                g.sem_inc(qr_lo, SEED)
                g.wait_ge(seg_ready, 1)

                def context(batch, c):
                    if c == 0:
                        g.wait_ge(ct_hi, batch.done(1, 1))
                    last = g.tensor_tensor(ct[1][:, c, :], ctr[:, c, :], ct[0][:, c, :].bitcast(F32), ALU.subtract)
                    if c == DC - 1:
                        last.then_inc(ct_lo, 1)

                def make_mask(batch, n, col=None, moved=None):
                    stage, t = n // ST, n % ST
                    part = mask_next[:, t, :]
                    if n == 0:
                        g.tensor_copy(seg_b[:], segmid[:, col]).then_inc(seg_copied, 1)
                        if moved is not None:
                            hold(g, mask_moved, moved, g_step)
                        hold(g, seg_copied, batch.done(1, 1), g_step)
                    if stage == 0:
                        g.tensor_scalar(part, ids[:], seg_b[:, t:t + 1], None, ALU.subtract).then_inc(distance, 1)
                    elif stage == 1:
                        g.wait_ge(distance, batch.done(ST, t + 1))
                        g.tensor_tensor(part, part, part, ALU.mult).then_inc(squared, 1)
                    else:
                        hold(g, squared, batch.done(ST, t + 1), g_step)
                        last = g.tensor_scalar(part, part, float(LOOKBACK // 2) ** 2, MASKED, ALU.is_gt, ALU.mult)
                        if t == ST - 1:
                            last.then_inc(mask_made, 1)

                def query(unit, h):
                    g.wait_ge(qr_hi, unit.done(h))
                    g.tensor_tensor(qr[h % 2][1][:], tq[h % 2][:], qr[h % 2][0][:].bitcast(F32),
                                    ALU.subtract).then_inc(qr_lo, 1)

                first, unit = Batch(Values(g), 0), Unit(Values(g))
                for c in range(DC):
                    context(first, c)
                for n in range(3 * ST):
                    make_mask(first, n, slice(0, ST))
                query(unit, 0)
                query(unit, 1)
                with g.Fori(0, B) as i:
                    val = Values(g, i)
                    unit, now, nxt = Unit(val), Batch(val, 0), Batch(val, 1)
                    col = g.snap(((i + 1) % B) * ST)
                    for h in range(H):
                        query(unit, h + 2)
                        if 0 <= h - MASK_AT < 3 * ST:
                            make_mask(nxt, h - MASK_AT, bass.ds(col, ST), now.done(1, 1))
                        if 0 <= h - CONTEXT_AT < DC:
                            context(nxt, h - CONTEXT_AT)

            @block.tensor
            def _(pe):
                for s in (qa_mm, qr_mm, s_mm, t_mm, z_mm, o_mm):
                    pe.sem_inc(s, SEED)

                def norm_t(batch, n):
                    pe.wait_ge(xn_ready, batch.done(1, 1))
                    if n:
                        pe.wait_ge(xt_lo, batch.done(2, 1))
                    for c in range(2):
                        for t in range(ST):
                            at = c * S + t * P
                            last = pe.transpose(x_ps[:, at:at + P], xin[:, t, (2 * n + c) * P:(2 * n + c + 1) * P],
                                                ident[:])
                    last.then_inc(xt_mm, 1)

                def latent(batch, unit, h):
                    pe.wait_ge(ct_lo, batch.done(1, 1))
                    pe.wait_ge(qa_lo, unit.done(h - 1))
                    for c in range(DC):
                        last = product(pe, qa_ps[:, 0:S], [w[:, c, :] for w in wkv], [w[:, c, :] for w in ct],
                                       c == 0, c == DC - 1)
                    last.then_inc(k_mm, 1)

                def query_latent(batch, unit, h):
                    pe.wait_ge(qr_rot, unit.done(h - 1))
                    for n in range(QCC):
                        for c in range(DC):
                            if n == 0 and c % 2 == 0:
                                pe.wait_ge(xt_lo, batch.done(2, 1 + c // 2))
                            last = product(pe, qr_ps[:, n * S:(n + 1) * S], [w[:, c, n * P:(n + 1) * P] for w in wdq],
                                           [w[:, c, :] for w in xt], c == 0, c == DC - 1)
                    last.then_inc(qc_mm, 1)

                def rotated_keys(batch):
                    pe.wait_ge(k_lo, batch.done(1, 1))
                    pe.wait_ge(xt_lo, batch.done(2, 2))
                    for n in range(2):
                        last = product(pe, x_ps[:, n * S:(n + 1) * S], [w[:, n, :] for w in wkr], [w[:] for w in kt],
                                       True, True)
                    last.then_inc(kr_mm, 1)

                def latent_rows(batch):
                    pe.wait_ge(kr_sum, batch.done(1, 1))
                    for n in range(2):
                        for t in range(ST):
                            at = n * S + t * P
                            last = pe.transpose(x_ps[:, at:at + P], kt[n][:, t * P:(t + 1) * P].bitcast(F32), ident[:])
                    last.then_inc(kn_mm, 1)

                def query(unit, h, head):
                    for bank, free, w, done in ((qr_ps, qr_rot, wr, qr_mm), (qa_ps, qa_lo, wa, qa_mm)):
                        pe.wait_ge(free, unit.done(h - 1))
                        cols = slice(head * L, (head + 1) * L)
                        product(pe, bank[:, 0:S], (w[0][:, 0, cols], w[1][:, cols]), [a[:, 0, :] for a in qc], True,
                                False)
                        pe.matmul(bank[:, 0:S], w[0][:, 1, cols], qc[0][:, 1, :], start=False, stop=False)
                        pe.matmul(bank[:, 0:S], w[0][0:QT, 1, cols], qc[1][0:QT, 1, :], start=False,
                                  stop=True).then_inc(done, 1)

                def scores(unit, h):
                    n = h % 2
                    pe.wait_ge(s_masked, unit.done(h - 1))
                    pe.wait_ge(qa_lo, unit.done(h))
                    pe.wait_ge(qr_lo, unit.done(h))
                    for t in range(ST):
                        rows = slice(t * P, (t + 1) * P)
                        product(pe, s_ps[:, t * S:(t + 1) * S], [w[:, rows] for w in q[n]], [w[:] for w in kt], True,
                                False)
                        last = product(pe, s_ps[:, t * S:(t + 1) * S], [w[:, rows] for w in qr[n]], [w[:] for w in kr],
                                       False, True)
                    last.then_inc(s_mm, 1)

                def probs_t(unit, h):
                    n = h % 2
                    pe.wait_ge(pt_lo, unit.done(h - 1))
                    pe.wait_ge(p_norm, unit.done(h))
                    for k in range(ST):
                        for t in range(ST):
                            at = k * S + t * P
                            last = pe.transpose(t_ps[:, at:at + P], pr[n][:, t, k * P:(k + 1) * P], ident[:])
                    last.then_inc(t_mm, 1)

                def mixed(unit, h):
                    pe.wait_ge(z_lo, unit.done(h - 1))
                    pe.wait_ge(pt_lo, unit.done(h))
                    for k in range(ST):
                        last = product(pe, z_ps[:, 0:S], [w[:, k, :] for w in kn], [w[:, k, :] for w in pt], k == 0,
                                       k == ST - 1)
                    last.then_inc(z_mm, 1)

                def projected(unit, h):
                    pe.wait_ge(z_lo, unit.done(h))
                    for t in range(ST):
                        last = product(pe, o_ps[t][:], [w[:, t * P:(t + 1) * P] for w in z], [w[:, h, :] for w in wvo],
                                       h == 0, h == H - 1)
                    last.then_inc(o_mm, 1)

                first, unit = Batch(Values(pe), 0), Unit(Values(pe))
                norm_t(first, 0)
                norm_t(first, 1)
                latent(first, unit, 0)
                query_latent(first, unit, 0)
                rotated_keys(first)
                pe.wait_ge(qc_lo, 1)
                query(unit, 0, 0)
                query(unit, 1, 1)
                pe.wait_ge(kr_lo, 1)
                scores(unit, 0)
                latent_rows(first)
                with pe.Fori(0, B) as i:
                    val = Values(pe, i)
                    unit, now, nxt = Unit(val), Batch(val, 0), Batch(val, 1)
                    for h in range(H - 2):
                        scores(unit, h + 1)
                        probs_t(unit, h)
                        query(unit, h + 2, h + 2)
                        if h == 0:
                            pe.wait_ge(kn_ready, now.done(1, 1))
                        if h == 1:
                            pe.wait_ge(out_ready, now.done(1, SEED))
                        if h >= 1:
                            projected(unit, h - 1)
                        mixed(unit, h)
                    norm_t(nxt, 0)
                    latent(nxt, unit, H)
                    scores(unit, H - 1)
                    probs_t(unit, H - 2)
                    norm_t(nxt, 1)
                    projected(unit, H - 3)
                    query_latent(nxt, unit, H)
                    mixed(unit, H - 2)
                    probs_t(unit, H - 1)
                    rotated_keys(nxt)
                    pe.wait_ge(qc_lo, nxt.done(1, 1))
                    query(unit, H, 0)
                    projected(unit, H - 2)
                    mixed(unit, H - 1)
                    pe.wait_ge(kr_lo, nxt.done(1, 1))
                    scores(unit, H)
                    query(unit, H + 1, 1)
                    projected(unit, H - 1)
                    latent_rows(nxt)


def shared_and_route(nc, x2, gate_w, bias, w1, w2, low_tri, slot_base, token_ids, ident_in, xg, out):
    G = 4
    STEPS, LINKS = 30, 5
    PER = 3
    SEARCHED = STEPS // PER
    PAIRS = NT // G // 2
    SPLIT_AT = 1
    with ExitStack() as ctx:
        sems = []

        def sb(name, shape, dt=F32):
            return ctx.enter_context(nc.sbuf_tensor("s_" + name, shape, dt))

        def pb(name, shape):
            return ctx.enter_context(nc.psum_tensor("s_ps_" + name, shape, F32))

        def sem(name):
            sems.append(ctx.enter_context(nc.semaphore("s_" + name)))
            return sems[-1]

        def parts(name, shape):
            return sb(name + "_hi", shape, F32R), sb(name + "_lo", shape, F32R)

        xn3, acc = sb("xn3", [P, NT, DX]), sb("acc", [P, NT, D])
        r1, r2 = xn3[:, NT - 8:NT - 4, 0:D], xn3[:, NT - 4:NT - 2, 0:D]
        w1p, w2p, wg = parts("w1", [P, DC, 2 * F]), parts("w2", [P, FC, D]), sb("wg", [P, DC, EP])
        ident, zeros, eb = sb("ident", [P, P]), sb("zeros", [P, DX]), sb("eb", [P, EP])
        xn = sb("xn", [P, G, D])
        xs = xn[:, 0:ST, :]
        stats, small = sb("stats", [P, G, 8]), sb("small", [P, 4, G])
        tile_t = [sb(f"tile_t{t}", [P, DC, P]) for t in range(G)]
        xt = parts("xt", [P, DC, S])
        sil = [sb(f"sil{n}", [P, S]) for n in range(FC)]
        gate = [sb(f"gate{n}", [P, S]) for n in range(FC)]
        gt = [parts(f"gt{n}", [P, S]) for n in range(FC)]
        W = [P, NT, EP]
        logits, aff, rank, beats, chosen, score = (sb("logits", W), sb("aff", W), sb("rank", W),
                                                   [sb(f"beats{n}", W) for n in range(2)], sb("chosen", W),
                                                   sb("score", W))
        over, tied, kept, place, tot = sb("over", W), sb("tied", W), sb("kept", W), sb("place", W), sb("tot", W)
        scan = [sb(f"scan{n}", W) for n in range(2)]
        cum, pick, tmp = sb("cum", W), sb("pick", W), sb("tmp", W)
        base, ids = sb("base", [P, EP]), sb("ids", [P, NT, 1])
        cnt, need = sb("cnt", [P, EP]), sb("need", [P, EP])
        bit, thr, cand, add = (sb(n, [P, EP], I32) for n in ("bit", "thr", "cand", "add"))
        ones, tri = sb("ones", [P, P]), sb("tri", [P, P])
        dest, has, at = (sb(n, [P, 2, NT]) for n in ("dest", "has", "at"))
        slot_at = sb("slot_at", [P, 2, NT], U32)

        up_ps = [pb(f"up{n}", [P, 512]) for n in range(FC)]
        gate_ps = [pb(f"gt{n}", [P, 512]) for n in range(FC)]
        x_ps, count_ps = pb("x", [P, 512]), pb("count", [P, 512])
        y_ps = [pb(f"y{n}", [P, D]) for n in range(ST)]
        tile_ps = [*gate_ps, *up_ps]
        pre_ps, tot_ps = x_ps[:, 0:NT * EP], x_ps[:, NT * EP:2 * NT * EP]

        w_in, w_hi, w_lo, gate_in, const_in, zeroed, cleared = (sem("w_in"), sem("w_hi"), sem("w_lo"), sem("gate_in"),
                                                                sem("const_in"), sem("zeroed"), sem("cleared"))
        x_in = [sem(f"x_in{n}") for n in range(2)]
        ln_chain, xn_ready, xn_kept = sem("ln_chain"), sem("xn_ready"), sem("xn_kept")
        tile_mm, tile_out, logit_mm, logits_out, aff_ready = (sem("tile_mm"), sem("tile_out"), sem("logit_mm"),
                                                              sem("logits_out"), sem("aff_ready"))
        xs_ready, xt_mm, xt_hi, xt_lo = sem("xs_ready"), sem("xt_mm"), sem("xt_hi"), sem("xt_lo")
        gate_mm, up_mm = sem("gate_mm"), sem("up_mm")
        silu, gated, gt_hi, gt_lo = sem("silu"), sem("gated"), sem("gt_hi"), sem("gt_lo")
        y_mm, acc_ready = sem("y_mm"), sem("acc_ready")
        chain, search = sem("chain"), sem("search")
        counted, total_mm, sums_in, sums_mm = sem("counted"), sem("total_mm"), sem("sums_in"), sem("sums_mm")
        sums_read, routed, sent = sem("sums_read"), sem("routed"), sem("sent")
        ids_in, aff_kept, stored = sem("ids_in"), sem("aff_kept"), sem("stored")
        sp_step, v_step = sem("sp_step"), sem("v_step")

        weights = [(r1, w1p), (r2, w2p)]
        x2_tiles = x2.rearrange("b (t p) c -> p (b t) c", p=P)
        ctx.callback(clear, nc, sems)
        block = ctx.enter_context(nc.Block())

        @block.sync
        def _(sp):
            sp.dma_start(acc[:, 0:G, :], x2_tiles[:, 0:G, :]).then_inc(x_in[0], 16)
            sp.dma_start(ident[:], ident_in).then_inc(gate_in, 16)
            sp.dma_start(wg[:], gate_w.rearrange("(c p) n -> p c n", p=P)).then_inc(gate_in, 16)
            sp.dma_start(acc[:, G:2 * G, :], x2_tiles[:, G:2 * G, :]).then_inc(x_in[1], 16)
            sp.dma_start(r1, w1.rearrange("(c p) n -> p c n", p=P)).then_inc(w_in, 16)
            sp.dma_start(r2, w2.rearrange("(c p) n -> p c n", p=P)).then_inc(w_in, 16)
            for dst, src in ((tri, low_tri), (base, slot_base.to_broadcast([P, EP])), (eb, bias.to_broadcast([P, EP]))):
                sp.dma_start(dst[:], src).then_inc(const_in, 16)
            sp.dma_start(ids[:, :, 0], token_ids).then_inc(ids_in, 16)
            with sp.Fori(0, PAIRS - 1) as i:
                val = Values(sp, i)
                arrived = val(16, 16)
                for n in range(2):
                    tiles = sp.snap((i * 2 + 2 + n) * G)
                    hold(sp, x_in[n], arrived, sp_step)
                    sp.dma_start(acc[:, bass.ds(tiles, G), :], x2_tiles[:, bass.ds(tiles, G), :]).then_inc(
                        x_in[n], 16)
            sp.wait_ge(zeroed, 1)
            for e in range(E):
                sp.dma_start(xg[e * SLOTS:(e + 1) * SLOTS, :].rearrange("(p t) d -> p t d", t=CT),
                             zeros[:].rearrange("p (o d) -> p o d", o=1).to_broadcast([P, CT, DX])).then_inc(
                                 cleared, 16)
            out_tiles = out.rearrange("b (t p) c -> p (b t) c", p=P)
            with sp.Fori(0, B) as i:
                tile = sp.snap(i * ST)
                hold(sp, acc_ready, Values(sp, i)(1, 1 + SEED), sp_step)
                sp.dma_start(out_tiles[:, bass.ds(tile, ST), :], acc[:, bass.ds(tile, ST), :]).then_inc(stored, 16)
            sp.wait_ge(cleared, 16 * E)
            sp.wait_ge(stored, 16 * B)

        @block.scalar
        def _(act):
            def gates(i):
                val = Values(act, i)
                for n in range(2):
                    tiles = act.snap((i * 2 + n) * G)
                    act.wait_ge(xn_ready, val(2, n + 1))
                    act.activation(xn3[:, bass.ds(tiles, G), 0:D], xn[:], ACT.Copy).then_inc(xn_kept, 1)
                    for t in range(G):
                        act.wait_ge(tile_mm, val(2 * G, n * G + t + 1 + SEED))
                        act.activation(tile_t[t][:].rearrange("p c t -> p (c t)"), tile_ps[t][:], ACT.Copy).then_inc(
                            tile_out, 1)
            act.sem_inc(xn_kept, SEED)
            with act.Fori(0, SPLIT_AT) as i:
                gates(i)
            act.wait_ge(w_in, 32)
            for raw, w in weights:
                act.activation(w[0][:], raw, ACT.Copy).then_inc(w_hi, 1)
            act.wait_ge(w_lo, len(weights))
            with act.Fori(SPLIT_AT, PAIRS) as i:
                gates(i)
            act.wait_ge(logits_out, 1)
            act.activation(aff[:], logits[:], ACT.Sigmoid).then_inc(aff_ready, 1)
            act.wait_ge(aff_ready, 1)
            act.wait_ge(ids_in, 16)
            act.activation(xn3[:, :, D:D + E], aff[:, :, 0:E], ACT.Copy)
            act.activation(xn3[:, :, D + E:DX], ids[:], ACT.Copy).then_inc(aff_kept, 1)

            def rows(i, shift, batch):
                if i is not None:
                    act.wait_ge(xt_mm, batch.done(2, 0))
                tile = slice(0, ST) if i is None else bass.ds(act.snap(((i + shift) % B) * ST), ST)
                act.activation(xs, xn3[:, tile, 0:D], ACT.Copy).then_inc(xs_ready, 1)

            def norm_t(batch, n):
                act.wait_ge(xt_mm, batch.done(2, n + 1))
                act.activation(xt[0][:, 2 * n:2 * n + 2, :].rearrange("p c t -> p (c t)"), x_ps[:],
                               ACT.Copy).then_inc(xt_hi, 1)

            def batch_of(i):
                val = Values(act, i)
                now, nxt = Batch(val, 0), Batch(val, 1)
                for n in range(FC):
                    act.wait_ge(gate_mm, now.done(FC, n + 1))
                    act.activation(sil[n][:], gate_ps[n][:, 0:S], ACT.Silu).then_inc(silu, 1)
                    if n == 0:
                        rows(i, 1, nxt)
                    if n == FC - 1:
                        act.wait_ge(up_mm, now.done(FC, FC))
                        norm_t(nxt, 0)
                    act.wait_ge(gated, now.done(FC, n + 1))
                    act.activation(gt[n][0][:], gate[n][:], ACT.Copy).then_inc(gt_hi, 1)
                norm_t(nxt, 1)

            act.wait_ge(xn_kept, NT // G + SEED)
            rows(None, 0, None)
            norm_t(Batch(Values(act), 0), 0)
            norm_t(Batch(Values(act), 0), 1)
            with act.Fori(0, SEARCHED) as i:
                batch_of(i)
            with act.Fori(SEARCHED, B) as i:
                batch_of(i)

        @block.vector
        def _(v):
            v.memset(zeros[:, 0:D + E], 0.0)
            v.memset(zeros[:, D + E:DX], NOWHERE).then_inc(zeroed, 1)
            for s in (ln_chain, acc_ready, search):
                v.sem_inc(s, SEED)

            def norm_of(i):
                val = Values(v, i)
                for n in range(2):
                    tiles = v.snap((i * 2 + n) * G)
                    hold(v, x_in[n], val(16, 16), v_step)
                    norm = LayerNorm(v, acc[:, bass.ds(tiles, G), :], stats, small, ln_chain,
                                     lambda k: val(2 * LN_LINKS, n * LN_LINKS + k + SEED), v_step, out=xn, tiles=G)
                    for k in range(G + 4):
                        norm.piece(k)
                    v.wait_ge(xn_kept, val(2, n + SEED))
                    v.wait_ge(tile_mm, val(2 * G, n * G + SEED))
                    for t in range(G):
                        last = norm.apply(t)
                    last.then_inc(xn_ready, 1)

            with v.Fori(0, SPLIT_AT) as i:
                norm_of(i)
            for n, (raw, w) in enumerate(weights):
                v.wait_ge(w_hi, n + 1)
                v.tensor_tensor(w[1][:], raw, w[0][:].bitcast(F32), ALU.subtract).then_inc(w_lo, 1)
            with v.Fori(SPLIT_AT, PAIRS) as i:
                norm_of(i)

            count = [0]

            def link(ins):
                count[0] += 1
                ins.then_inc(chain, 1)
                v.wait_ge(chain, count[0])

            def used(a):
                return a[:, :, 0:E]

            def wide(a, n=NT):
                return a[:, 0:E].rearrange("p (o e) -> p o e", o=1).to_broadcast([P, n, E])

            for a in (rank, score, kept, tied, over, beats[0], beats[1]):
                v.memset(a[:], 0.0)
            v.memset(cnt[:], 0.0)
            v.memset(ones[:], 1.0)
            v.memset(thr[:].bitcast(F32), 0.0)
            link(v.memset(bit[:], 1 << (STEPS - 1)))
            v.wait_ge(const_in, 48)
            v.wait_ge(logit_mm, NT // G)
            v.tensor_tensor(logits[:], count_ps[:, 0:NT * EP].rearrange("p (t e) -> p t e", e=EP),
                            eb[:].rearrange("p (o e) -> p o e", o=1).to_broadcast(W), ALU.add).then_inc(logits_out, 1)
            v.wait_ge(aff_ready, 1)
            for e in range(E):
                one = aff[:, :, e:e + 1]
                b = beats[e % 2]
                if e:
                    v.tensor_tensor(b[:, :, 0:e], one.to_broadcast([P, NT, e]), aff[:, :, 0:e], ALU.is_gt)
                    last = v.memset(b[:, :, e:e + 1], 0.0)
                if e < E - 1:
                    last = v.tensor_tensor(b[:, :, e + 1:E], one.to_broadcast([P, NT, E - 1 - e]), aff[:, :, e + 1:E],
                                           ALU.is_ge)
                link(last)
                link(v.tensor_tensor(used(rank), used(rank), used(b), ALU.add))
            link(v.tensor_scalar(used(chosen), used(rank), TOP_K - 0.5, None, ALU.is_lt))
            link(v.tensor_tensor(used(score), used(aff), used(chosen), ALU.mult))
            link(v.tensor_copy(cand[:], bit[:]))


            def norm_t(batch, n):
                v.wait_ge(xt_hi, batch.done(2, n + 1))
                half = slice(2 * n, 2 * n + 2)
                v.tensor_tensor(xt[1][:, half, :].rearrange("p c t -> p (c t)"), x_ps[:],
                                xt[0][:, half, :].rearrange("p c t -> p (c t)").bitcast(F32),
                                ALU.subtract).then_inc(xt_lo, 1)

            def hidden(now, n):
                v.wait_ge(silu, now.done(FC, n + 1))
                v.wait_ge(up_mm, now.done(FC, n + 1))
                v.tensor_tensor(gate[n][:], up_ps[n][:, 0:S], sil[n][:], ALU.mult).then_inc(gated, 1)

            def hidden_lo(now, n):
                v.wait_ge(gt_hi, now.done(FC, n + 1))
                v.tensor_tensor(gt[n][1][:], gate[n][:], gt[n][0][:].bitcast(F32), ALU.subtract).then_inc(gt_lo, 1)

            def try_bit(val, k):
                v.wait_ge(search, val(PER * LINKS, k * LINKS + SEED))
                v.tensor_tensor(used(over), used(score), wide(cand[:].bitcast(F32)), ALU.is_ge).then_inc(search, 1)
                v.wait_ge(search, val(PER * LINKS, k * LINKS + 1 + SEED))
                v.tensor_reduce(cnt[:, 0:E], used(over).rearrange("p t e -> p e t"), AX.X, ALU.add).then_inc(counted, 1)

            def take_bit(val, k):
                at_link = lambda n: val(PER * LINKS, k * LINKS + n + SEED)
                v.wait_ge(total_mm, val(PER, k + 1))
                v.scalar_tensor_tensor(add[:], count_ps[:, 0:EP], CAP - 0.5, bit[:], ALU.is_gt, ALU.mult).then_inc(
                    search, 1)
                v.wait_ge(search, at_link(2))
                v.tensor_tensor(thr[:], thr[:], add[:], ALU.bitwise_or).then_inc(search, 1)
                v.tensor_scalar(bit[:], bit[:], 1, None, ALU.logical_shift_right).then_inc(search, 1)
                v.wait_ge(search, at_link(4))
                v.tensor_tensor(cand[:], thr[:], bit[:], ALU.bitwise_or).then_inc(search, 1)

            def batch_of(i, searching):
                val = Values(v, i)
                now, nxt = Batch(val, 0), Batch(val, 1)
                tile = v.snap(i * ST)
                if searching:
                    try_bit(val, 0)
                hidden(now, 0)
                if searching:
                    take_bit(val, 0)
                hidden_lo(now, 0)
                if searching:
                    try_bit(val, 1)
                hidden(now, 1)
                norm_t(nxt, 0)
                hidden_lo(now, 1)
                if searching:
                    take_bit(val, 1)
                    try_bit(val, 2)
                norm_t(nxt, 1)
                v.wait_ge(y_mm, now.done(1, 1))
                for t in range(ST):
                    rows = acc[:, bass.ds(v.snap(tile + t), 1), :].rearrange("p o d -> p (o d)")
                    last = v.tensor_tensor(rows, y_ps[t][:], rows, ALU.add)
                last.then_inc(acc_ready, 1)
                if searching:
                    take_bit(val, 2)

            norm_t(Batch(Values(v), 0), 0)
            norm_t(Batch(Values(v), 0), 1)
            with v.Fori(0, SEARCHED) as i:
                batch_of(i, True)
            v.wait_ge(search, STEPS * LINKS + SEED)

            least = thr[:].bitcast(F32)
            v.tensor_tensor(used(over), used(score), wide(least), ALU.is_gt)
            link(v.tensor_tensor(used(tied), used(score), wide(least), ALU.is_equal))
            v.tensor_reduce(cnt[:, 0:E], used(over).rearrange("p t e -> p e t"), AX.X, ALU.add)
            link(v.tensor_tensor(used(tied), used(tied), used(chosen), ALU.mult))
            v.sem_inc(sums_in, 1)

            def places(k, of):
                v.wait_ge(sums_mm, k)
                v.tensor_copy(place[:], pre_ps.rearrange("p (t e) -> p t e", e=EP))
                v.tensor_copy(scan[0][:], tot_ps.rearrange("p (t e) -> p t e", e=EP))
                v.tensor_copy(tot[:], tot_ps.rearrange("p (t e) -> p t e", e=EP)).then_inc(sums_read, 1)
                v.wait_ge(sums_read, k)
                d, n = 1, 0
                while d < NT:
                    v.tensor_copy(scan[1 - n][:, 0:d, :], scan[n][:, 0:d, :])
                    link(v.tensor_tensor(scan[1 - n][:, d:, :], scan[n][:, d:, :], scan[n][:, 0:NT - d, :], ALU.add))
                    d, n = 2 * d, 1 - n
                link(v.tensor_tensor(place[:], place[:], scan[n][:], ALU.add))
                link(v.tensor_tensor(place[:], place[:], tot[:], ALU.subtract))

            places(1, tied)
            link(v.tensor_scalar(need[:, 0:E], count_ps[:, 0:E], -1.0, float(CAP), ALU.mult, ALU.add))
            link(v.tensor_tensor(used(tmp), used(place), wide(need[:]), ALU.is_lt))
            link(v.tensor_tensor(used(tmp), used(tmp), used(tied), ALU.mult))
            link(v.tensor_tensor(used(kept), used(over), used(tmp), ALU.add))
            v.sem_inc(sums_in, 1)
            places(2, kept)
            link(v.tensor_tensor(used(place), used(place), wide(base[:]), ALU.add))
            v.tensor_copy(cum[:, :, 0:1], kept[:, :, 0:1])
            link(v.memset(cum[:, :, E:EP], 0.0))
            for e in range(1, E):
                link(v.tensor_tensor(cum[:, :, e:e + 1], cum[:, :, e - 1:e], kept[:, :, e:e + 1], ALU.add))
            for s in range(2):
                link(v.tensor_scalar(used(pick), used(cum), float(s + 1), None, ALU.is_equal))
                link(v.tensor_tensor(used(pick), used(pick), used(kept), ALU.mult))
                link(v.tensor_reduce(has[:, s, :], used(pick), AX.X, ALU.add))
                link(v.tensor_tensor(used(tmp), used(pick), used(place), ALU.mult))
                link(v.tensor_reduce(dest[:, s, :], used(tmp), AX.X, ALU.add))
            link(v.tensor_scalar(at[:], has[:], -4.0 * ROWS, 4.0 * ROWS, ALU.mult, ALU.add))
            link(v.tensor_tensor(at[:], at[:], dest[:], ALU.add))
            link(v.tensor_copy(slot_at[:], at[:]))
            v.sem_inc(routed, 1)


            with v.Fori(SEARCHED, B) as i:
                batch_of(i, False)

        @block.gpsimd
        def _(g):
            g.wait_ge(cleared, 16 * E)
            g.wait_ge(aff_kept, 1)
            g.wait_ge(routed, 1)
            for t in range(NT):
                for s in range(2):
                    g.indirect_dma_start(out=xg, out_offset=bass.IndirectOffsetOnAxis(slot_at[:, s, t:t + 1], 0),
                                         in_=xn3[:, t, :], in_offset=None, bounds_check=ROWS - 1,
                                         oob_is_err=False).then_inc(sent, 16)
            g.wait_ge(sent, 16 * 2 * NT)

        @block.tensor
        def _(pe):
            pe.wait_ge(gate_in, 32)
            pe.sem_inc(tile_mm, SEED)
            with pe.Fori(0, PAIRS) as i:
                val = Values(pe, i)
                for n in range(2):
                    col = pe.snap((i * 2 + n) * G * EP)
                    pe.wait_ge(xn_ready, val(2, n + 1))
                    for t in range(G):
                        for c in range(DC):
                            last = pe.transpose(tile_ps[t][:, c * P:(c + 1) * P], xn[:, t, c * P:(c + 1) * P],
                                                ident[:])
                        last.then_inc(tile_mm, 1)
                    for t in range(G):
                        pe.wait_ge(tile_out, val(2 * G, n * G + t + 1))
                        for c in range(DC):
                            last = pe.matmul(count_ps[:, bass.ds(pe.snap(col + t * EP), EP)], tile_t[t][:, c, :],
                                             wg[:, c, :], start=c == 0, stop=c == DC - 1)
                    last.then_inc(logit_mm, 1)

            def norm_t(batch, n):
                if n == 0:
                    pe.wait_ge(xs_ready, batch.done(1, 1))
                else:
                    pe.wait_ge(xt_lo, batch.done(2, 1))
                for c in range(2):
                    for t in range(ST):
                        where = c * S + t * P
                        last = pe.transpose(x_ps[:, where:where + P], xs[:, t, (2 * n + c) * P:(2 * n + c + 1) * P],
                                            ident[:])
                last.then_inc(xt_mm, 1)

            def count_tokens(val, k):
                pe.wait_ge(counted, val(PER, k + 1))
                pe.matmul(count_ps[:, 0:EP], ones[:], cnt[:], start=True, stop=True).then_inc(total_mm, 1)

            def batch_of(i, searching):
                val = Values(pe, i)
                now, nxt = Batch(val, 0), Batch(val, 1)
                pe.wait_ge(xt_lo, now.done(2, 2))
                for n in range(FC):
                    for bank, f, done in ((gate_ps[n], FC + n, gate_mm), (up_ps[n], n, up_mm)):
                        for c in range(DC):
                            last = product(pe, bank[:, 0:S], [w[:, c, f * P:(f + 1) * P] for w in w1p],
                                           [w[:, c, :] for w in xt], c == 0, c == DC - 1)
                        last.then_inc(done, 1)
                    if searching:
                        count_tokens(val, n)
                    if n == 0:
                        norm_t(nxt, 0)
                pe.wait_ge(acc_ready, now.done(1, SEED))
                for n in range(FC):
                    pe.wait_ge(gt_lo, now.done(FC, n + 1))
                    for t in range(ST):
                        last = product(pe, y_ps[t][:], [w[:, t * P:(t + 1) * P] for w in gt[n]],
                                       [w[:, n, :] for w in w2p], n == 0, n == FC - 1)
                    if n == 0:
                        norm_t(nxt, 1)
                last.then_inc(y_mm, 1)
                if searching:
                    count_tokens(val, 2)

            pe.wait_ge(const_in, 48)
            first = Batch(Values(pe), 0)
            norm_t(first, 0)
            norm_t(first, 1)
            with pe.Fori(0, SEARCHED) as i:
                batch_of(i, True)
            flat = "p t e -> p (t e)"
            pe.wait_ge(sums_in, 1)
            pe.matmul(count_ps[:, 0:EP], ones[:], cnt[:], start=True, stop=True)
            for k, flags in enumerate((tied, kept)):
                pe.wait_ge(sums_in, k + 1)
                if k:
                    pe.wait_ge(sums_read, k)
                pe.matmul(pre_ps, tri[:], flags[:].rearrange(flat), start=True, stop=True)
                pe.matmul(tot_ps, ones[:], flags[:].rearrange(flat), start=True, stop=True).then_inc(sums_mm, 1)
            pe.wait_ge(sums_read, 2)
            with pe.Fori(SEARCHED, B) as i:
                batch_of(i, False)


def routed_experts(nc, w1, w2, ident_in, xg, out):
    HALF = SLOTS // 2
    UNITS = 2 * FC
    EARLY = P * ((HALF - 1) // P + 1)
    with ExitStack() as ctx:
        sems = []

        def sb(name, shape, dt=F32):
            return ctx.enter_context(nc.sbuf_tensor("e_" + name, shape, dt))

        def pb(name, shape):
            return ctx.enter_context(nc.psum_tensor("e_ps_" + name, shape, F32))

        def sem(name):
            sems.append(ctx.enter_context(nc.semaphore("e_" + name)))
            return sems[-1]

        def parts(name, shape):
            return sb(name + "_hi", shape, F32R), sb(name + "_lo", shape, F32R)

        r1, r2 = sb("r1", [P, DC, 2, FC, P]), sb("r2", [P, FC, D])
        w1p, w2p = [parts(f"w1_{n}", [P, DC, 2, P]) for n in range(FC)], parts("w2", [P, FC, D])
        ident, xin = sb("ident", [P, P]), sb("xin", [P, CT, DX])
        xt = parts("xt", [P, DC, SLOTS])
        sil = [sb(f"sil{n}", [P, HALF]) for n in range(2)]
        gate = [sb(f"gate{n}", [P, HALF]) for n in range(2)]
        gt = parts("gt", [P, FC, SLOTS])
        ysb = sb("ysb", [P, CT, D])
        meta_next, weight, token = sb("meta_next", [P, 2, CT]), sb("weight", [P, CT]), sb("token", [P, CT], U32)
        up_ps, gate_ps, x_ps, y_ps = ([pb(f"{name}{n}", [P, 512]) for n in range(2)] for name in ("up", "gt", "x", "y"))

        const_in, w1_in, w2_in, x_in, added = sem("const_in"), sem("w1_in"), sem("w2_in"), sem("x_in"), sem("added")
        w1_hi, w1_lo, w2_hi, w2_lo = sem("w1_hi"), sem("w1_lo"), sem("w2_hi"), sem("w2_lo")
        xt_mm, xt_hi, xt_lo = sem("xt_mm"), sem("xt_hi"), sem("xt_lo")
        gate_mm, up_mm, silu, gated, gt_hi, gt_lo = (sem("gate_mm"), sem("up_mm"), sem("silu"), sem("gated"),
                                                     sem("gt_hi"), sem("gt_lo"))
        y_mm, y_out, sp_step = sem("y_mm"), sem("y_out"), sem("sp_step")
        all_added = sem("all_added")
        meta_taken, meta_ready, v_step, g_step = sem("meta_taken"), sem("meta_ready"), sem("v_step"), sem("g_step")
        ctx.callback(clear, nc, sems)
        block = ctx.enter_context(nc.Block())

        def load(sp, e, which):
            if which == 1:
                sp.dma_start(r1[:].rearrange("p c u n f -> p c (u n f)"),
                             w1[e].rearrange("o (c p) n -> p (o c) n", p=P)).then_inc(w1_in, 16)
            elif which == 2:
                sp.dma_start(r2[:], w2[e].rearrange("o (c p) n -> p (o c) n", p=P)).then_inc(w2_in, 16)
            else:
                sp.dma_start(xin[:], xg[e].rearrange("o (t p) d -> p (o t) d", p=P)).then_inc(x_in, 16)

        @block.sync
        def _(sp):
            sp.dma_start(ident[:], ident_in).then_inc(const_in, 16)
            for which in (0, 1, 2):
                load(sp, slice(0, 1), which)
            with sp.Fori(0, E) as i:
                val = Values(sp, i)
                now = Batch(val, 0)
                nxt = sp.snap((i + 1) % E)
                x_free, w1_free, w2_free = now.done(CT, CT), now.done(FC, FC), now.done(1, 1)
                hold(sp, xt_mm, x_free, sp_step)
                hold(sp, meta_taken, now.done(1, 1), sp_step)
                load(sp, bass.ds(nxt, 1), 0)
                hold(sp, w1_lo, w1_free, sp_step)
                load(sp, bass.ds(nxt, 1), 1)
                hold(sp, w2_lo, w2_free, sp_step)
                load(sp, bass.ds(nxt, 1), 2)

        @block.scalar
        def _(act):
            act.sem_inc(y_out, SEED)

            def split1(batch, n, free):
                act.wait_ge(w1_in, batch.done(16, 16))
                if free is not None:
                    act.wait_ge(up_mm, free)
                act.activation(w1p[n][0][:], r1[:, :, :, n, :], ACT.Copy).then_inc(w1_hi, 1)

            def split2(batch, free):
                act.wait_ge(w2_in, batch.done(16, 16))
                if free is not None:
                    act.wait_ge(y_mm, free)
                act.activation(w2p[0][:], r2[:], ACT.Copy).then_inc(w2_hi, 1)

            def rows_t(batch, t):
                act.wait_ge(xt_mm, batch.done(CT, t + 1))
                act.activation(xt[0][:, :, t * P:(t + 1) * P], x_ps[t % 2][:].rearrange("p (c t) -> p c t", c=DC),
                               ACT.Copy).then_inc(xt_hi, 1)

            def gate_of(now, u):
                act.wait_ge(gate_mm, now.done(UNITS, u + 1))
                act.activation(sil[u % 2][:], gate_ps[u % 2][:, 0:HALF], ACT.Silu).then_inc(silu, 1)

            def hidden(now, u):
                n, half = u // 2, u % 2
                act.wait_ge(gated, now.done(UNITS, u + 1 + SEED))
                act.activation(gt[0][:, n, half * HALF:(half + 1) * HALF], gate[u % 2][:], ACT.Copy).then_inc(gt_hi, 1)

            def output(now, t):
                act.wait_ge(y_mm, now.done(CT, t + 1))
                if t == 0:
                    act.wait_ge(meta_ready, now.done(1, 1))
                act.activation(ysb[:, t, :], y_ps[t % 2][:], ACT.Copy, scale=weight[:, t:t + 1]).then_inc(y_out, 1)

            first = Batch(Values(act), 0)
            for t in range(2):
                rows_t(first, t)
            for n in range(FC):
                split1(first, n, None)
            for t in range(2, CT):
                rows_t(first, t)
            split2(first, None)
            with act.Fori(0, E) as i:
                val = Values(act, i)
                now, nxt = Batch(val, 0), Batch(val, 1)
                for u in range(UNITS - 1):
                    gate_of(now, u)
                    hidden(now, u)
                split1(nxt, 0, now.done(UNITS, 2))
                gate_of(now, UNITS - 1)
                act.wait_ge(up_mm, now.done(UNITS, UNITS))
                rows_t(nxt, 0)
                hidden(now, UNITS - 1)
                rows_t(nxt, 1)
                for t in range(2, CT):
                    output(now, t - 2)
                    rows_t(nxt, t)
                output(now, CT - 2)
                split1(nxt, 1, now.done(UNITS, UNITS))
                output(now, CT - 1)
                split2(nxt, now.done(CT, CT))
        @block.vector
        def _(v):
            v.sem_inc(gated, SEED)

            def rows_t(batch, t):
                v.wait_ge(xt_hi, batch.done(CT, t + 1))
                rows = slice(t * P, (t + 1) * P)
                v.tensor_tensor(xt[1][:, :, rows], x_ps[t % 2][:].rearrange("p (c t) -> p c t", c=DC),
                                xt[0][:, :, rows].bitcast(F32), ALU.subtract).then_inc(xt_lo, 1)

            def hidden(now, u):
                v.wait_ge(silu, now.done(UNITS, u + 1))
                v.wait_ge(up_mm, now.done(UNITS, u + 1))
                v.tensor_tensor(gate[u % 2][:], up_ps[u % 2][:, 0:HALF], sil[u % 2][:], ALU.mult).then_inc(gated, 1)

            def hidden_lo(now, u):
                n, half = u // 2, u % 2
                cols = slice(half * HALF, (half + 1) * HALF)
                v.wait_ge(gt_hi, now.done(UNITS, u + 1))
                v.tensor_tensor(gt[1][:, n, cols], gate[u % 2][:], gt[0][:, n, cols].bitcast(F32),
                                ALU.subtract).then_inc(gt_lo, 1)

            def take_meta(col):
                v.tensor_copy(meta_next[:, 0, :], xin[:, :, col].rearrange("p t o -> p (t o)"))
                v.tensor_copy(meta_next[:, 1, :], xin[:, :, D + E:DX].rearrange("p t o -> p (t o)")).then_inc(
                    meta_taken, 1)

            def place_meta(now):
                hold(v, meta_taken, now.done(1, 1), v_step)
                hold(v, all_added, now.done(1, SEED), v_step)
                v.tensor_copy(weight[:], meta_next[:, 0, :])
                v.tensor_copy(token[:], meta_next[:, 1, :]).then_inc(meta_ready, 1)

            v.sem_inc(all_added, SEED)
            v.wait_ge(x_in, 16)
            take_meta(slice(D, D + 1))
            for t in range(CT):
                rows_t(Batch(Values(v), 0), t)
            with v.Fori(0, E) as i:
                val = Values(v, i)
                now, nxt = Batch(val, 0), Batch(val, 1)
                for u in range(UNITS - 1):
                    hidden(now, u)
                    hidden_lo(now, u)
                    if u == 1:
                        place_meta(now)
                hidden(now, UNITS - 1)
                rows_t(nxt, 0)
                hidden_lo(now, UNITS - 1)
                for t in range(1, CT):
                    rows_t(nxt, t)
                hold(v, meta_ready, now.done(1, 1), v_step)
                take_meta(bass.ds(v.snap(i + (D + 1)), 1))

        @block.gpsimd
        def _(g):
            def split1(batch, n):
                g.wait_ge(w1_hi, batch.done(FC, n + 1))
                g.tensor_tensor(w1p[n][1][:], r1[:, :, :, n, :], w1p[n][0][:].bitcast(F32), ALU.subtract).then_inc(
                    w1_lo, 1)

            def split2(batch):
                g.wait_ge(w2_hi, batch.done(1, 1))
                g.tensor_tensor(w2p[1][:], r2[:], w2p[0][:].bitcast(F32), ALU.subtract).then_inc(w2_lo, 1)

            def add(now, t):
                done = now.done(CT, t + 1 + SEED)
                hold(g, y_out, done, g_step)
                g.indirect_dma_start(out=out, out_offset=bass.IndirectOffsetOnAxis(token[:, t:t + 1], 0),
                                     in_=ysb[:, t, :], in_offset=None, bounds_check=B * S - 1, oob_is_err=False,
                                     compute_op=ALU.add).then_inc(added, 16)

            first = Batch(Values(g), 0)
            for n in range(FC):
                split1(first, n)
            split2(first)
            with g.Fori(0, E) as i:
                val = Values(g, i)
                now, nxt = Batch(val, 0), Batch(val, 1)
                split1(nxt, 0)
                for t in range(CT - 1):
                    add(now, t)
                split1(nxt, 1)
                add(now, CT - 1)
                split2(nxt)
                done = now.done(16 * CT, 16 * CT)
                hold(g, added, done, all_added)

        @block.tensor
        def _(pe):
            pe.wait_ge(const_in, 16)

            def rows_t(batch, t):
                if t == 0:
                    pe.wait_ge(x_in, batch.done(16, 16))
                if t >= 2:
                    pe.wait_ge(xt_lo, batch.done(CT, t - 1))
                for c in range(DC):
                    last = pe.transpose(x_ps[t % 2][:, c * P:(c + 1) * P], xin[:, t, c * P:(c + 1) * P], ident[:])
                last.then_inc(xt_mm, 1)

            def unit(now, u):
                n, half = u // 2, u % 2
                if u % 2 == 0:
                    pe.wait_ge(w1_lo, now.done(FC, n + 1))
                pe.wait_ge(xt_lo, now.done(CT, CT if half else EARLY // P))
                pe.wait_ge(gated, now.done(UNITS, u - 1 + SEED))
                for bank, gate_part, done in ((gate_ps[u % 2], 1, gate_mm), (up_ps[u % 2], 0, up_mm)):
                    for c in range(DC):
                        last = product(pe, bank[:, 0:HALF], [w[:, c, gate_part, :] for w in w1p[n]],
                                       [w[:, c, half * HALF:(half + 1) * HALF] for w in xt], c == 0, c == DC - 1)
                    last.then_inc(done, 1)

            def output(now, t):
                if t == 0:
                    pe.wait_ge(w2_lo, now.done(1, 1))
                pe.wait_ge(gt_lo, now.done(UNITS, UNITS - 1 if (t + 1) * P <= HALF else UNITS))
                pe.wait_ge(y_out, now.done(CT, t - 1 + SEED))
                for n in range(FC):
                    last = product(pe, y_ps[t % 2][:], [w[:, n, t * P:(t + 1) * P] for w in gt],
                                   [w[:, n, :] for w in w2p], n == 0, n == FC - 1)
                last.then_inc(y_mm, 1)

            for t in range(CT):
                rows_t(Batch(Values(pe), 0), t)
            with pe.Fori(0, E) as i:
                val = Values(pe, i)
                now, nxt = Batch(val, 0), Batch(val, 1)
                for u in range(UNITS - 1):
                    unit(now, u)
                rows_t(nxt, 0)
                rows_t(nxt, 1)
                unit(now, UNITS - 1)
                for t in range(CT):
                    output(now, t)
                    if t + 2 < CT:
                        rows_t(nxt, t + 2)


def mixture(nc, x2, gate_w, bias, shared_w1, shared_w2, w1, w2, low_tri, slot_base, token_ids, ident, xg, out):
    shared_and_route(nc, x2, gate_w, bias, shared_w1, shared_w2, low_tri, slot_base, token_ids, ident, xg, out)
    routed_experts(nc, w1, w2, ident, xg.rearrange("(e s) d -> e s d", s=SLOTS),
                   out.rearrange("b s d -> (b s) d"))


def decoder_layer(nc, a, out):
    def scratch(name, shape):
        return nc.dram_tensor(name, shape, F32, kind="Internal").ap()

    x1, x2 = (scratch(name, (B, S, D)) for name in ("x1", "x2"))
    self_attention(nc, a["x"], a["w_lat"], a["b_lat"], a["w_d"], a["b_d"], a["w_proj"], a["b_proj"], a["causal"],
                   a["ident"], x1)
    cross_attention(nc, x1, a["ctx_t"], a["seg"], a["w_kvc"], a["w_dq"], a["uq_t"], a["w_qr"], a["uk_t"], a["kr_uv"],
                    a["uv_t"], a["w_o"], a["trig"], a["rot_cs"], a["key_ids"], a["ident"], x2)
    mixture(nc, x2, a["gate_w"], a["bias"], a["shared_w1"], a["shared_w2"], a["w1"], a["w2"], a["low_tri"],
            a["slot_base"], a["token_ids"], a["ident"], scratch("xg", (ROWS, DX)), out)


def kernel(**inputs):
    import numpy as np
    import concourse.bacc as bacc
    from concourse import mybir as _mybir
    from concourse.bass_utils import run_bass_kernel_spmd

    nc = bacc.Bacc("TRN2", target_bir_lowering=False, num_devices=1)
    arrays, args = {}, {}

    def give(name, a):
        a = np.ascontiguousarray(a)
        arrays[f"in_{name}"] = a
        args[name] = nc.dram_tensor(f"in_{name}", a.shape, _mybir.dt.from_np(a.dtype), kind="ExternalInput").ap()

    def padded(a, shape):
        wide = np.zeros(shape, np.float32)
        wide[:, 0:a.shape[-1]] = a
        return wide

    attn = {k: np.asarray(inputs["L0_attn_" + k]) for k in ("W_lat", "b_lat", "W_d", "b_d", "W_proj", "b_proj")}
    cross = {k: np.asarray(inputs["L0_xattn_" + k]) for k in ("W_kvc", "W_dq", "W_uq", "W_qr", "W_uk", "W_kr", "W_uv",
                                                              "W_o")}
    ffn = {k: np.asarray(inputs["L0_ffn_" + k]) for k in ("gate_w", "expert_bias", "shared_w1", "shared_w2",
                                                          "routed_w1", "routed_w2")}
    give("x", inputs["x"])
    for k in ("W_lat", "b_lat", "W_d", "W_proj", "b_proj"):
        give(k.lower(), attn[k])
    give("b_d", attn["b_d"].reshape(H, L).T)
    t = np.arange(P)
    triangle = np.where(t[None, :] <= t[:, None], 0.0, MASKED).astype(np.float32)
    give("causal", np.concatenate([triangle, np.zeros((P, P), np.float32), triangle], 1))
    give("ident", np.eye(P, dtype=np.float32))
    give("ctx_t", np.asarray(inputs["ctx_2048"]).transpose(0, 2, 1))
    give("seg", np.asarray(inputs["itok_BxS_0_1023"]).reshape(NT, P).T)
    for k in ("W_kvc", "W_dq", "W_qr", "W_o"):
        give(k.lower(), cross[k])
    for k in ("uq", "uk", "uv"):
        give(k + "_t", cross["W_" + k].T)
    half = R // 2
    k1, k2 = cross["W_kr"][:, 0:half], cross["W_kr"][:, half:R]
    give("kr_uv", np.stack([np.concatenate([k1, k2, k2, k1], 1), np.concatenate([k2, k1, k1, k2], 1)], 1))
    freq = np.float32(1.0) / np.float32(10000.0) ** (np.arange(half, dtype=np.float32) / np.float32(half))
    angle = np.arange(S, dtype=np.float32)[None, :] * freq[:, None]
    cos, sin = np.cos(angle), np.sin(angle)
    give("trig", np.concatenate([cos, cos, sin, sin], 0))
    give("rot_cs", np.stack([np.concatenate([cos, cos, cos, -cos], 0), np.concatenate([-sin, sin, sin, sin], 0)]))
    give("key_ids", np.broadcast_to(np.arange(S, dtype=np.float32)[None, :], (P, S)))
    give("gate_w", padded(ffn["gate_w"], (D, EP)))
    give("bias", padded(ffn["expert_bias"], (1, EP)))
    give("shared_w1", ffn["shared_w1"][0])
    give("shared_w2", ffn["shared_w2"][0])
    give("w1", ffn["routed_w1"])
    give("w2", ffn["routed_w2"])
    give("low_tri", np.triu(np.ones((P, P), np.float32), 1))
    give("slot_base", (np.arange(EP, dtype=np.float32) * SLOTS)[None, :])

    give("token_ids", np.arange(NT * P, dtype=np.float32).reshape(NT, P).T)

    out = nc.dram_tensor("out_0", (B, S, D), _mybir.dt.float32, kind="ExternalOutput").ap()
    decoder_layer(nc, args, out)
    r = run_bass_kernel_spmd(nc, [arrays], core_ids=[0])
    return r.results[0]["out_0"]
```
